# Optimizing a Trainium2 kernel written in Bass

```python
import numpy as np
import jax
import jax.numpy as jnp

def _softmax(x, axis=-1):
    return jax.nn.softmax(x, axis=axis)

def _gelu(x):
    return jax.nn.gelu(x, approximate=True)

def _silu(x):
    return jax.nn.silu(x)

def _sigmoid(x):
    return jax.nn.sigmoid(x)

def _layernorm(x, axis=-1, eps=1e-05):
    m = jnp.mean(x, axis=axis, keepdims=True)
    v = jnp.var(x, axis=axis, keepdims=True)
    return (x - m) / jnp.sqrt(v + eps)

def _scatter_add(tgt, idx, src, axis=0):
    return tgt.at[idx].add(src)

def _segment_sum(src, seg, n):
    return jax.ops.segment_sum(src, seg, n)
kernel_name = 'mk_adaln_d1_jaxref_r8_4675e3'

def setup_inputs(seed: int=0):
    np.random.seed(seed)
    _w = jnp.asarray

    def _L0_attn_setup():
        import jax, jax.numpy as jnp
        import numpy as np
        B, S, HID = (4, 128, 128)
        H = 8
        HD = HID // H
        NQ = 8
        RATIO = 0.5
        FF = 4 * HID
        EPS_COS = 1e-08
        LN_EPS = 1e-05

        def _layernorm(x, g, b):
            m = jnp.mean(x, axis=-1, keepdims=True)
            v = jnp.var(x, axis=-1, keepdims=True)
            return (x - m) * jax.lax.rsqrt(v + LN_EPS) * g + b
        key = jax.random.key(seed)
        ks = jax.random.split(key, 24)
        sc = 0.02
        inp = {'x': jax.random.normal(ks[0], (B, S, HID), jnp.float32), 'Wq': jax.random.normal(ks[1], (H, HID, HD)) * sc, 'bq': jnp.zeros((H, HD)), 'Wk': jax.random.normal(ks[2], (H, HID, HD)) * sc, 'bk': jnp.zeros((H, HD)), 'Wv': jax.random.normal(ks[3], (H, HID, HD)) * sc, 'bv': jnp.zeros((H, HD)), 'Wc2q': jax.random.normal(ks[4], (H, HD, NQ)) * sc, 'bc2q': jnp.zeros((H, NQ)), 'Wo': jax.random.normal(ks[5], (HID, HID)) * sc, 'bo': jnp.zeros((HID,)), 'g1': jnp.ones((HID,)), 'beta1': jnp.zeros((HID,)), 'g2': jnp.ones((HID,)), 'beta2': jnp.zeros((HID,)), 'W1': jax.random.normal(ks[6], (HID, FF)) * sc, 'b1': jnp.zeros((FF,)), 'Wm': jax.random.normal(ks[7], (FF, NQ)) * sc, 'bm': jnp.zeros((NQ,)), 'Wqo': jax.random.normal(ks[8], (NQ, FF)) * sc, 'bqo': jnp.zeros((FF,)), 'W2': jax.random.normal(ks[9], (FF, HID)) * sc, 'b2': jnp.zeros((HID,))}
        return inp
    _L0_attn_in = _L0_attn_setup()

    def _L0_ffn_setup():
        import jax, jax.numpy as jnp
        import numpy as np
        D_MODEL = 128
        EXPANSION = 4
        D_HIDDEN = D_MODEL * EXPANSION
        NUM_STAGES = int(np.log2(D_HIDDEN))

        def butterfly(y, weights, dim):
            lead = y.shape[:-1]
            for stage in range(weights.shape[0]):
                s = 2 ** stage
                nb = dim // (2 * s)
                yr = y.reshape(*lead, nb, 2, s)
                a = yr[..., 0, :]
                b = yr[..., 1, :]
                w = weights[stage].reshape(nb, s, 2, 2)
                na = w[..., 0, 0] * a + w[..., 0, 1] * b
                nb2 = w[..., 1, 0] * a + w[..., 1, 1] * b
                y = jnp.stack([na, nb2], axis=-2).reshape(*lead, dim)
            return y
        key = jax.random.key(seed)
        ks = jax.random.split(key, 6)
        B, S = (4, 256)
        x = jax.random.normal(ks[0], (B, S, D_MODEL), jnp.float32)
        W_exp = jax.random.normal(ks[1], (D_MODEL, D_HIDDEN), jnp.float32) * 0.02
        b_exp = jnp.zeros((D_HIDDEN,), jnp.float32)
        up_weights = jax.random.normal(ks[2], (NUM_STAGES, D_HIDDEN // 2, 2, 2), jnp.float32) * 0.02
        up_bias = jnp.zeros((D_HIDDEN,), jnp.float32)
        down_weights = jax.random.normal(ks[3], (NUM_STAGES, D_HIDDEN // 2, 2, 2), jnp.float32) * 0.02
        W_con = jax.random.normal(ks[4], (D_HIDDEN, D_MODEL), jnp.float32) * 0.02
        b_con = jnp.zeros((D_MODEL,), jnp.float32)
        down_bias = jnp.zeros((D_MODEL,), jnp.float32)
        return dict(x=x, W_exp=W_exp, b_exp=b_exp, up_weights=up_weights, up_bias=up_bias, down_weights=down_weights, W_con=W_con, b_con=b_con, down_bias=down_bias)
    _L0_ffn_in = _L0_ffn_setup()
    _L0_c = _w((lambda *s: np.random.randn(*s).astype(np.float32) * 0.05)(16, 128))
    _L0_wmod = _w((lambda *s: np.random.randn(*s).astype(np.float32) * 0.05)(128, 6 * 128) * 128 ** (-0.5))
    _d = {'L0_attn_x': _L0_attn_in['x'], 'L0_attn_Wq': _L0_attn_in['Wq'], 'L0_attn_bq': _L0_attn_in['bq'], 'L0_attn_Wk': _L0_attn_in['Wk'], 'L0_attn_bk': _L0_attn_in['bk'], 'L0_attn_Wv': _L0_attn_in['Wv'], 'L0_attn_bv': _L0_attn_in['bv'], 'L0_attn_Wc2q': _L0_attn_in['Wc2q'], 'L0_attn_bc2q': _L0_attn_in['bc2q'], 'L0_attn_Wo': _L0_attn_in['Wo'], 'L0_attn_bo': _L0_attn_in['bo'], 'L0_attn_g1': _L0_attn_in['g1'], 'L0_attn_beta1': _L0_attn_in['beta1'], 'L0_attn_g2': _L0_attn_in['g2'], 'L0_attn_beta2': _L0_attn_in['beta2'], 'L0_attn_W1': _L0_attn_in['W1'], 'L0_attn_b1': _L0_attn_in['b1'], 'L0_attn_Wm': _L0_attn_in['Wm'], 'L0_attn_bm': _L0_attn_in['bm'], 'L0_attn_Wqo': _L0_attn_in['Wqo'], 'L0_attn_bqo': _L0_attn_in['bqo'], 'L0_attn_W2': _L0_attn_in['W2'], 'L0_attn_b2': _L0_attn_in['b2'], 'L0_ffn_W_exp': _L0_ffn_in['W_exp'], 'L0_ffn_b_exp': _L0_ffn_in['b_exp'], 'L0_ffn_up_weights': _L0_ffn_in['up_weights'], 'L0_ffn_up_bias': _L0_ffn_in['up_bias'], 'L0_ffn_down_weights': _L0_ffn_in['down_weights'], 'L0_ffn_W_con': _L0_ffn_in['W_con'], 'L0_ffn_b_con': _L0_ffn_in['b_con'], 'L0_ffn_down_bias': _L0_ffn_in['down_bias'], 'L0_c': _L0_c, 'L0_wmod': _L0_wmod}
    _x0 = _d['L0_attn_x']
    _d['L0_attn_x'] = jax.random.normal(jax.random.fold_in(jax.random.key(seed), 1), (16, 256, 128), dtype=_x0.dtype)
    del _x0
    return _d

def reference(L0_attn_x, L0_attn_Wq, L0_attn_bq, L0_attn_Wk, L0_attn_bk, L0_attn_Wv, L0_attn_bv, L0_attn_Wc2q, L0_attn_bc2q, L0_attn_Wo, L0_attn_bo, L0_attn_g1, L0_attn_beta1, L0_attn_g2, L0_attn_beta2, L0_attn_W1, L0_attn_b1, L0_attn_Wm, L0_attn_bm, L0_attn_Wqo, L0_attn_bqo, L0_attn_W2, L0_attn_b2, L0_ffn_W_exp, L0_ffn_b_exp, L0_ffn_up_weights, L0_ffn_up_bias, L0_ffn_down_weights, L0_ffn_W_con, L0_ffn_b_con, L0_ffn_down_bias, L0_c, L0_wmod):

    def _L0_attn_ref(x, Wq, bq, Wk, bk, Wv, bv, Wc2q, bc2q, Wo, bo, g1, beta1, g2, beta2, W1, b1, Wm, bm, Wqo, bqo, W2, b2):
        import jax, jax.numpy as jnp
        import numpy as np
        B, S, HID = (4, 128, 128)
        H = 8
        HD = HID // H
        NQ = 8
        RATIO = 0.5
        FF = 4 * HID
        EPS_COS = 1e-08
        LN_EPS = 1e-05

        def _layernorm(x, g, b):
            m = jnp.mean(x, axis=-1, keepdims=True)
            v = jnp.var(x, axis=-1, keepdims=True)
            return (x - m) * jax.lax.rsqrt(v + LN_EPS) * g + b
        Q = jnp.einsum('bsh,nhd->bnsd', x, Wq) + bq[None, :, None, :]
        K = jnp.einsum('bsh,nhd->bnsd', x, Wk) + bk[None, :, None, :]
        V = jnp.einsum('bsh,nhd->bnsd', x, Wv) + bv[None, :, None, :]
        qq = jnp.einsum('bnsd,ndq->bnsq', Q, Wc2q) + bc2q[None, :, None, :]
        kq = jnp.einsum('bnsd,ndq->bnsq', K, Wc2q) + bc2q[None, :, None, :]
        qn = jnp.linalg.norm(qq, axis=-1)
        kn = jnp.linalg.norm(kq, axis=-1)
        dots = jnp.einsum('bnsq,bntq->bnst', qq, kq)
        fid = dots / jnp.maximum(qn[..., :, None] * kn[..., None, :], EPS_COS)
        qw = fid * (1.0 + 0.1 * jnp.sin(fid * jnp.pi))
        cw = jnp.einsum('bnsd,bntd->bnst', Q, K) / np.sqrt(HD).astype(np.float32)
        aw = RATIO * qw + (1.0 - RATIO) * cw
        probs = jax.nn.softmax(aw, axis=-1)
        heads = jnp.einsum('bnst,bntd->bnsd', probs, V)
        attn = heads.transpose(0, 2, 1, 3).reshape(x.shape[0], x.shape[1], HID)
        attn = attn @ Wo + bo
        x1 = _layernorm(x + attn, g1, beta1)
        h = x1 @ W1 + b1
        qm = h @ Wm + bm
        qe = jnp.tanh(qm) * jnp.cos(qm * (jnp.pi / 4))
        ha = qe @ Wqo + bqo
        ff = ha @ W2 + b2
        out = _layernorm(x1 + ff, g2, beta2)
        return out

    def _L0_ffn_ref(x, W_exp, b_exp, up_weights, up_bias, down_weights, W_con, b_con, down_bias):
        import jax, jax.numpy as jnp
        import numpy as np
        D_MODEL = 128
        EXPANSION = 4
        D_HIDDEN = D_MODEL * EXPANSION
        NUM_STAGES = int(np.log2(D_HIDDEN))

        def butterfly(y, weights, dim):
            lead = y.shape[:-1]
            for stage in range(weights.shape[0]):
                s = 2 ** stage
                nb = dim // (2 * s)
                yr = y.reshape(*lead, nb, 2, s)
                a = yr[..., 0, :]
                b = yr[..., 1, :]
                w = weights[stage].reshape(nb, s, 2, 2)
                na = w[..., 0, 0] * a + w[..., 0, 1] * b
                nb2 = w[..., 1, 0] * a + w[..., 1, 1] * b
                y = jnp.stack([na, nb2], axis=-2).reshape(*lead, dim)
            return y
        h = jnp.einsum('bsd,dh->bsh', x, W_exp) + b_exp
        h = butterfly(h, up_weights, D_HIDDEN)
        h = jax.nn.gelu(h + up_bias, approximate=False)
        h = butterfly(h, down_weights, D_HIDDEN)
        y = jnp.einsum('bsh,hd->bsd', h, W_con) + b_con
        return y + down_bias
    x = L0_attn_x
    mod = (_silu(L0_c) @ L0_wmod).reshape(L0_c.shape[0], 6, 1, -1)
    sa, ca, ga, sb, cb, gb = (mod[:, 0], mod[:, 1], mod[:, 2], mod[:, 3], mod[:, 4], mod[:, 5])
    ga = (2 * (ga >= 0) - 1) * jnp.maximum(jnp.abs(ga), 0.25)
    gb = (2 * (gb >= 0) - 1) * jnp.maximum(jnp.abs(gb), 0.25)
    h = _layernorm(x, axis=-1) * (1 + ca) + sa
    x = x + ga * _L0_attn_ref(h, L0_attn_Wq, L0_attn_bq, L0_attn_Wk, L0_attn_bk, L0_attn_Wv, L0_attn_bv, L0_attn_Wc2q, L0_attn_bc2q, L0_attn_Wo, L0_attn_bo, L0_attn_g1, L0_attn_beta1, L0_attn_g2, L0_attn_beta2, L0_attn_W1, L0_attn_b1, L0_attn_Wm, L0_attn_bm, L0_attn_Wqo, L0_attn_bqo, L0_attn_W2, L0_attn_b2)
    h = _layernorm(x, axis=-1) * (1 + cb) + sb
    x = x + gb * _L0_ffn_ref(h, L0_ffn_W_exp, L0_ffn_b_exp, L0_ffn_up_weights, L0_ffn_up_bias, L0_ffn_down_weights, L0_ffn_W_con, L0_ffn_b_con, L0_ffn_down_bias)
    return x

_drawn_inputs = setup_inputs


def setup_inputs(seed=0):
    import zlib

    import numpy as np

    out = dict(_drawn_inputs(seed))
    spreads = {'L0_attn_bq': (0.0, 0.8),
     'L0_attn_bk': (0.0, 0.8),
     'L0_attn_bv': (0.0, 0.8),
     'L0_attn_bc2q': (0.0, 0.8),
     'L0_attn_bo': (0.0, 0.336),
     'L0_attn_g1': (1.0, 0.2),
     'L0_attn_beta1': (0.0, 0.364),
     'L0_attn_g2': (1.0, 0.2),
     'L0_attn_beta2': (0.0, 0.312),
     'L0_attn_b1': (0.0, 0.8),
     'L0_attn_bm': (0.0, 0.8),
     'L0_attn_bqo': (0.0, 0.702),
     'L0_attn_b2': (0.0, 0.331),
     'L0_ffn_b_exp': (0.0, 0.1),
     'L0_ffn_up_bias': (0.0, 0.1),
     'L0_ffn_b_con': (0.0, 0.371),
     'L0_ffn_down_bias': (0.0, 0.308)}
    factors = {'L0_attn_Wq': 8.0,
     'L0_attn_Wk': 8.0,
     'L0_attn_Wv': 8.0,
     'L0_attn_Wc2q': 8.0,
     'L0_attn_Wo': 8.0,
     'L0_attn_W1': 8.0,
     'L0_attn_Wm': 8.0,
     'L0_attn_Wqo': 8.0,
     'L0_attn_W2': 5.51}
    for name, (base, spread) in spreads.items():
        noise = np.random.default_rng([zlib.crc32(name.encode()), seed]).standard_normal(out[name].shape)
        drawn = base * np.exp(spread * noise) if base else spread * noise
        out[name] = jnp.asarray(drawn.astype(out[name].dtype))
    for name, factor in factors.items():
        out[name] = (out[name] * factor).astype(out[name].dtype)
    return out
```

```python
from contextlib import ExitStack

import concourse.bass as bass
from concourse import mybir

F32 = mybir.dt.float32
F16 = mybir.dt.float16
ALU = mybir.AluOpType
ACT = mybir.ActivationFunctionType
AX = mybir.AxisListType

P = 128
B, S, D = 16, 256, 128
H, HD, NQ = 8, 16, 8
FF = 512
PB = 2
PAIRS = B // PB
TOK = PB * S
T = TOK // P
CH = FF // P
STAGES = 9
TILES = PB * H // 2
LN_EPS = 1e-5
PI = 3.141592653589793
SIN_SCALE = PI * (1.0 - 2.0 ** -20)
TINY = 1e-36
EPS_COS = 1e-8
SUM_LEAST, SUM_MOST = 1e-20, 1e30
ROUND = 1.5 * 2.0 ** 23

NEXT_AT = {1: "A_stats", 2: "A_norm", 3: "A_h", 4: "A_qk", 5: "A_q", 6: "A_k", 7: "A_v",
           9: "A_qn", 10: "A_hi", 11: "A_lo", 12: "A_tq", 13: "A_tk"}
PREV_AT = {0: "P_o0", 1: "P_o1", 2: "P_at", 3: "P_u", 4: "P_x1", 5: "P_qm", 6: "P_sin",
           8: "P_tanh", 9: "P_qe", 10: "P_y", 11: "P_v", 12: "P_x2", 13: "P_z", 14: "P_ffn",
           15: "P_out"}

SEMS = """
w_in w_zero w_ident w_step ones_ready
x_in modA_in modP_in xp_in rows_in kpad_in kfpad_in stored
A_sum A_agg A_var A_rstd A_xh A_tp h_ready A_qkmm A_qk1 A_qk2 A_n2 A_qk3 A_rn A_rn2 A_qn A_qmm q_ready A_kmm k_ready
A_vmm v_ready A_hi A_lo A_tq A_tk qf_ready kf_ready
fid_mm sin_done tile_read cw_mm exp_done av_done o_ready
P_tO P_rec P_at P_tat P_atF P_umm P_s1 P_g1 P_v1 P_r1 P_xh1 P_tx1 P_x1F P_qmm P_qm P_rr P_r2 P_r3 P_sin P_tanh P_qe
P_tqe P_qeF P_ymm P_s2 P_g2 P_v2 P_r2d P_v P_vG P_xB P_x2 P_x2c P_s3 P_g3 P_v3 P_r3d P_z P_tz P_h2
P_up P_g P_y2 P_yG P_out
G_norm G_row G_shrink G_scaled G_done G_dots G_max G_neg flag_good flag_sum flag_mm flag_ready
pr_c pr_silu pr_mm pr_ev pr_done pr_pe bf_in bf_up bf_b bf_dn zeroed
""".split()


def need(eng, sem, count):
    if not isinstance(count, int) or count > 0:
        eng.wait_ge(sem, count)


def build(nc, a, out):
    ctx = ExitStack()
    with ctx:
        def sb(name, shape, dt=F32):
            return ctx.enter_context(nc.sbuf_tensor(name, shape, dt))

        def pb(name, shape, dt=F32):
            return ctx.enter_context(nc.psum_tensor(name, shape, dt))

        s = {name: ctx.enter_context(nc.semaphore(name)) for name in SEMS}

        ident = sb("ident", [P, P])
        ident16 = sb("ident16", [P, P], F16)
        wq = sb("wq", [P, P])
        wk = sb("wk", [P, P])
        wv = sb("wv", [P, P])
        wo = sb("wo", [P, P])
        wqk = sb("wqk", [P, P])
        wfm = sb("wfm", [P, NQ])
        wq2 = sb("wq2", [NQ + 1, P])
        wup = sb("wup", [P, FF])
        wdn = sb("wdn", [P, CH, P])
        cols = sb("cols", [P, 14])
        bup = sb("bup", [P, CH])
        bqk_row = sb("bqk_row", [P, P])
        bfm_row = sb("bfm_row", [P, NQ])
        mod_cols = sb("mod_cols", [P, B, 5])
        half_pi = sb("half_pi", [P, 1])
        neg_half = sb("neg_half", [P, 64])
        BQ, BK, BV, BO, G1, BETA1, B1, UPB = 0, 1, 2, 3, 4, 5, 6, 10

        x_a = sb("x_a", [P, T, D])
        x_p = sb("x_p", [P, T, D])
        modA = sb("modA", [P, PB, 3])
        modP = sb("modP", [P, PB, 2])
        rows = [sb(f"rows{i}", [P, PB, 4, D]) for i in range(2)]
        xh = sb("xh", [P, T, D])
        h_F = [sb(f"h_F{i}", [P, TOK]) for i in range(2)]
        hb_F = [sb(f"hb_F{i}", [P, TOK]) for i in range(2)]
        q_F = [sb(f"q_F{i}", [P, TOK]) for i in range(2)]
        k_F = sb("k_F", [P, TOK])
        kpad = [sb(f"kpad{i}", [P, H, TOK]) for i in range(2)]
        v_T = [sb(f"v_T{i}", [P, T, H, 32]) for i in range(2)]
        qk = sb("qk", [P, 2, T, 64])
        sq = sb("sq", [P, 2, T, 64])
        n2 = sb("n2", [P, 64])
        n2c = sb("n2c", [P, 64])
        n2_least = sb("n2_least", [P, 64])
        l_least = sb("l_least", [P, 2 * H])
        l_total = sb("l_total", [P, 2 * H])
        good = sb("good", [P, 64 + 4 * H])
        n_good = sb("n_good", [P, 1])
        ones_col = sb("ones_col", [P, 1])
        flag = sb("flag", [1, 1], mybir.dt.int32)
        norms = sb("norms", [P, 64])
        shrink = sb("shrink", [P, 512])
        top = sb("top", [P, 4])
        rn = sb("rn", [P, 64])
        qn = sb("qn", [P, 2, T * H, NQ])
        parts = sb("parts", [P, 2, T * H, 4, NQ], F16)
        qf = [sb(f"qf{i}", [P, 2, TOK], F16) for i in range(2)]
        kf = sb("kf", [P, 2, TOK], F16)
        kfpad = [sb(f"kfpad{i}", [P, H, TOK], F16) for i in range(2)]
        stat = {c: sb(f"stat{c}", [P, T, 6]) for c in "A123"}
        agg = {c: sb(f"agg{c}", [P, T, 2]) for c in "A123"}
        var = {c: sb(f"var{c}", [P, T]) for c in "A123"}
        rstd = {c: sb(f"rstd{c}", [P, T]) for c in "A123"}
        sines = sb("sines", [P, 2, 1024])
        prob = sb("prob", [P, TILES, 1024])
        o_F = sb("o_F", [P, PB, TOK])
        rec = sb("rec", [P, 2 * H])
        at_T = sb("at_T", [P, T, D])
        at_F = sb("at_F", [P, TOK])
        xh1 = sb("xh1", [P, T, D])
        x1_F = sb("x1_F", [P, TOK])
        qm = sb("qm", [P, T * NQ])
        qm_n = sb("qm_n", [P, T * NQ])
        qm_r = sb("qm_r", [P, T * NQ])
        qm_sin = sb("qm_sin", [P, T * NQ])
        qm_tanh = sb("qm_tanh", [P, T * NQ])
        qe = sb("qe", [P, T, NQ + 1])
        qe_F = sb("qe_F", [NQ + 1, TOK])
        vv = sb("vv", [P, T, D])
        xB = sb("xB", [P, T, D])
        x2 = sb("x2", [P, T, D])
        x2c = sb("x2c", [P, T, D])
        z = sb("z", [P, T, D])
        h2_F = sb("h2_F", [P, TOK])
        g_F = sb("g_F", [P, CH, TOK])
        o_T = sb("o_T", [P, T, D])

        score = [pb(f"score{i}", [P, 1024]) for i in range(2)]
        av = pb("av", [P, 512])
        ca_ = pb("chainA", [P, 512])
        cp_ = pb("chainP", [P, 512])
        cx_ = pb("chainX", [P, 512])
        ca16 = ca_[:, :].bitcast(F16)

        rows_dram = nc.dram_tensor("gate_rows", [B, 4 * D], F32, kind="Internal").ap()

        ring = [prob[:, i, :] for i in range(8)] + \
               [kpad[i][:, 2 * j:2 * j + 2, :].rearrange("p a b -> p (a b)") for i in range(2) for j in range(4)] + \
               [g_F[:, 2 * j:2 * j + 2, :].rearrange("p a b -> p (a b)") for j in range(2)]
        up_w, dn_w = ring[:STAGES], ring[STAGES:]
        wmod = sb("wmod", [P, 6 * D])
        w1 = o_F[:, 0, :]
        w1T = o_F[:, 1, :]
        wcon = sines[:, 0, 0:512]
        wcon_t = sines[:, 0, 512:1024]
        w2 = sines[:, 1, 0:512]
        prod_up = h2_F[:, :], at_T[:, :, :].rearrange("p t d -> p (t d)")
        bexp = at_F[0:1, :]
        prod_b = [rows[1][0:1, i, :, :].rearrange("p r d -> p (r d)") for i in range(2)]
        prod_dn = h_F[1][:, :], hb_F[1][:, :]
        c_sb = xh1[0:B, 0, :]
        c_silu = xh1[0:B, 1, :]
        bcasts = xh1[:, 2, :]
        bcast1 = xh1[:, 3, :]
        sT = x2[:, 0, 0:B]
        wqT = x2[:, 1, :]
        wkT = x2[:, 2, :]
        blk = x2[:, 3, 0:64]
        bc2q_row = x2[:, 3, 64:128]
        wm = x2c[:, 0, 0:CH * NQ].rearrange("p (c q) -> p c q", c=CH)
        bm_row = x2c[:, 0, 64:64 + NQ]
        wqo = x1_F[0:NQ + 1, :]
        wqoT = x2c[:, 1, 0:CH * (NQ + 1)].rearrange("p (c q) -> p c q", c=CH)
        b2_rows = x2c[0:NQ + 1, 2, :]
        vec_rows = x2c[0:14, 3, :]
        gate = z[0:B, 0:2, :]
        gate_s = z[0:B, 2:4, :]
        gate_rows = xB[0:B, :, :]
        vec16 = vv[0:B, :, :]
        b1_cols = o_T[:, :, :]
        one = sb("one", [1, 1])

        x_d = a["L0_attn_x"].rearrange("b s d -> (b s) d").rearrange("(n t p) d -> n p t d", t=T, p=P)
        out_d = out.rearrange("b s d -> (b s) d").rearrange("(n t p) d -> n p t d", t=T, p=P)

        block = ctx.enter_context(nc.Block())
        LOADS = 37

        def butterfly(eng, op, y, w, prods, transposed, stage, step, base):
            st = 2 ** stage
            nb = FF // (2 * st)
            n_rows = y.shape[0]
            yv = y.rearrange("p (n c j) -> p n c j", n=nb, c=2)
            how = "p (n j c r) -> p r n c j" if transposed else "p (n j r c) -> p r n c j"
            wv_ = w[0:n_rows, :].rearrange(how, n=nb, j=st, r=2, c=2)
            pv = [x.rearrange("p (n c j) -> p n c j", n=nb, c=2) for x in prods]
            for r in range(2):
                op.tensor_tensor(pv[r], yv, wv_[:, r], ALU.mult).then_inc(step, 1)
            eng.wait_ge(step, base + 2)
            for r in range(2):
                op.tensor_tensor(yv[:, :, r, :], pv[r][:, :, 0, :], pv[r][:, :, 1, :], ALU.add).then_inc(step, 1)
            eng.wait_ge(step, base + 4)

        def general_pass(eng, pair, after=None):
            eng.wait_ge(s["flag_ready"], 1)
            unmet = eng.value_load(flag[0:1, 0:1], min_val=0, max_val=1)
            with eng.If(unmet > 0):
                with eng.Fori(0, PAIRS // 2) as i:
                    pair(2 * i + PAIRS, 0)
                    pair(2 * i + PAIRS + 1, 1)
                if after:
                    after()

        @block.sync
        def _(sp):
            def load(dst, src):
                sp.dma_start(dst, src).then_inc(s["w_in"], 16)

            def x_load(dst, sem, n, at):
                sp.dma_start(dst[:, :, :], x_d[at]).then_inc(s[sem], 16)

            x_load(x_a, "x_in", 0, 0)

            load(c_sb, a["L0_c"])
            load(wmod[:, :], a["L0_wmod"])
            for w, name in ((wq, "L0_attn_Wq"), (wk, "L0_attn_Wk"), (wv, "L0_attn_Wv")):
                load(w[:, :].rearrange("f (h d) -> f h d", h=H), a[name].rearrange("h f d -> f h d"))
            load(wo[:, :], a["L0_attn_Wo"])
            load(w1, a["L0_attn_W1"])
            load(wm, a["L0_attn_Wm"].rearrange("(c k) q -> k c q", c=CH))
            load(wqo[0:NQ, :], a["L0_attn_Wqo"])
            load(wqo[NQ:NQ + 1, :], a["L0_attn_bqo"].rearrange("(a n) -> a n", a=1))
            load(w2.rearrange("k (c f) -> k c f", c=CH), a["L0_attn_W2"].rearrange("(c k) f -> k c f", c=CH))
            load(wup[:, :], a["L0_ffn_W_exp"])
            load(wcon.rearrange("k (c f) -> k c f", c=CH), a["L0_ffn_W_con"].rearrange("(c k) f -> k c f", c=CH))
            load(bexp, a["L0_ffn_b_exp"].rearrange("(a n) -> a n", a=1))
            vecs = [("L0_attn_bq", "h d -> (h d)"), ("L0_attn_bk", "h d -> (h d)"), ("L0_attn_bv", "h d -> (h d)"),
                    ("L0_attn_bo", None), ("L0_attn_g1", None), ("L0_attn_beta1", None),
                    ("L0_attn_b1", None), ("L0_ffn_up_bias", None)]
            at = 0
            for name, how in vecs:
                v = a[name].rearrange(how) if how else a[name]
                v = v.rearrange("(r n) -> r n", n=P)
                load(vec_rows[at:at + v.shape[0], :], v)
                at += v.shape[0]
            assert at == 14
            for j, name in enumerate(("L0_attn_g2", "L0_attn_beta2", "L0_ffn_b_con", "L0_ffn_down_bias")):
                load(vec16[:, j, :], a[name].partition_broadcast(B))
            load(bc2q_row, a["L0_attn_bc2q"].rearrange("h q -> (h q)").partition_broadcast(P))
            load(bm_row, a["L0_attn_bm"].partition_broadcast(P))
            sp.wait_ge(s["w_zero"], 2)
            for h in range(H):
                load(blk[HD * h:HD * h + HD, NQ * h:NQ * h + NQ], a["L0_attn_Wc2q"][h])
            load(b2_rows[NQ:NQ + 1, :], a["L0_attn_b2"].rearrange("(a n) -> a n", a=1))
            for tiles, name in ((up_w, "L0_ffn_up_weights"), (dn_w, "L0_ffn_down_weights")):
                for j in range(STAGES):
                    sp.dma_start(tiles[j], a[name][j].rearrange("k r c -> (k r c)").partition_broadcast(P))\
                      .then_inc(s["bf_in"], 16)

            def next_in(n, base=0):
                need(sp, s["A_xh"], n)
                x_load(x_a, "x_in", n, n - base)
                mod_in(n, base)

            def mod_in(n, base=0):
                need(sp, s["h_ready"], n)
                sp.dma_start(modA[:, :, :], mod_cols[:, bass.ds(PB * (n - base), PB), 0:3]).then_inc(s["modA_in"], 16)

            def prev_in(n, q, base=0):
                need(sp, s["P_xB"], n)
                x_load(x_p, "xp_in", n, n - base)
                sp.dma_start(rows[q][:, :, :, :].rearrange("p b r d -> p b (r d)"),
                             rows_dram[bass.ds(PB * (n - base), PB), :].partition_broadcast(P)).then_inc(s["rows_in"], 16)

            def modP_in(n, base=0):
                sp.dma_start(modP[:, :, :], mod_cols[:, bass.ds(PB * (n - base), PB), 3:5]).then_inc(s["modP_in"], 16)

            def keys_out(n, q):
                sp.wait_ge(s["k_ready"], n + 1)
                for h in range(H):
                    sp.dma_start(kpad[q][HD * h:HD * h + HD, h, :], k_F[HD * h:HD * h + HD, :])\
                      .then_inc(s["kpad_in"], 16)

            def key_amps_out(n, q):
                sp.wait_ge(s["kf_ready"], n + 1)
                for j in range(4):
                    sp.dma_start(kfpad[q][32 * j:32 * j + 32, j:H:4, :], kf[32 * j:32 * j + 32, :, :])\
                      .then_inc(s["kfpad_in"], 16)

            def store(n, base=0):
                sp.wait_ge(s["P_out"], n + 1)
                sp.dma_start(out_d[n - base], o_T[:, :, :]).then_inc(s["stored"], 16)

            def body(n, q, prev, nxt):
                if nxt:
                    next_in(n + 1)
                if prev:
                    modP_in(n - 1)
                prev_in(n, q)
                if nxt:
                    keys_out(n + 1, 1 - q)
                    key_amps_out(n + 1, 1 - q)
                if prev:
                    store(n - 1)

            sp.wait_ge(s["pr_done"], 1)
            sp.dma_start(rows_dram, gate_rows.rearrange("b r d -> b (r d)")).then_inc(s["stored"], 16)
            mod_in(0)
            sp.wait_ge(s["zeroed"], 2)
            keys_out(0, 0)
            key_amps_out(0, 0)
            sp.wait_ge(s["stored"], 16)
            body(0, 0, False, True)
            with sp.Fori(0, (PAIRS - 2) // 2) as i:
                body(2 * i + 1, 1, True, True)
                body(2 * i + 2, 0, True, True)
            body(PAIRS - 1, 1, True, False)
            modP_in(PAIRS - 1)
            store(PAIRS - 1)
            sp.wait_ge(s["stored"], 16 * (PAIRS + 1))

            def general(n, q):
                next_in(n, PAIRS)
                keys_out(n, q)
                key_amps_out(n, q)
                prev_in(n, q, PAIRS)
                modP_in(n, PAIRS)
                store(n, PAIRS)

            general_pass(sp, general, lambda: sp.wait_ge(s["stored"], 16 * (2 * PAIRS + 1)))

        @block.tensor
        def _(pe):
            mm = nc.tensor.matmul

            def transposes(bank, tiles, eye=ident):
                for t, tile in enumerate(tiles):
                    last = nc.tensor.transpose(bank[:, P * t:P * t + P], tile, eye[:, :])
                return last

            pe.wait_ge(s["w_ident"], 4)
            pe.wait_ge(s["w_in"], 16 * LOADS)
            pe.wait_ge(s["x_in"], 16)
            pe.wait_ge(s["pr_silu"], 1)
            nc.tensor.transpose(cp_[:, 0:B], c_silu, ident[0:B, 0:B]).then_inc(s["pr_mm"], 1)
            transposes(cx_, [wq[:, :], wk[:, :]]).then_inc(s["pr_mm"], 1)
            nc.tensor.transpose(ca_[:, 0:14], vec_rows, ident[0:14, 0:14]).then_inc(s["pr_mm"], 1)
            transposes(score[0], [w1[:, P * c:P * c + P] for c in range(CH)]).then_inc(s["pr_mm"], 1)
            for c in range(CH):
                last = nc.tensor.transpose(av[:, (NQ + 1) * c:(NQ + 1) * (c + 1)], wqo[:, P * c:P * c + P],
                                           ident[0:NQ + 1, 0:NQ + 1])
            last.then_inc(s["pr_mm"], 1)
            transposes(score[0][:, 512:1024], [wcon[:, P * c:P * c + P] for c in range(CH)])\
                .then_inc(s["pr_mm"], 1)
            pe.wait_ge(s["pr_ev"], 1)
            for j, c in enumerate((1, 0, 4, 3)):
                mm(score[1][:, B * j:B * j + B], wmod[:, D * c:D * c + D], sT, start=True, stop=True)
            for j, c in enumerate((2, 5)):
                last = mm(score[1][0:B, 512 + D * j:512 + D * j + D], sT, wmod[:, D * c:D * c + D], start=True, stop=True)
            last.then_inc(s["pr_mm"], 1)
            pe.wait_ge(s["pr_ev"], 4)
            mm(cx_[:, 0:64], wqT, blk, start=True, stop=True)
            mm(cx_[:, 64:128], wkT, blk, start=True, stop=True)
            mm(cx_[:, 128:192], bcasts, blk, start=True, stop=True)
            mm(cx_[:, 192:256], bcast1, blk, start=True, stop=True).then_inc(s["pr_mm"], 1)
            mm(cp_[:, 0:1], wo[:, :], cols[:, BV:BV + 1], start=True, stop=True).then_inc(s["pr_mm"], 1)
            pe.wait_ge(s["pr_ev"], 5)
            for c in range(CH):
                mm(ca_[:, 0:NQ], w1T[:, P * c:P * c + P], wm[:, c, :], start=c == 0, stop=c == CH - 1)
            for c in range(CH):
                last = mm(ca_[:, NQ:2 * NQ], b1_cols[:, c, :], wm[:, c, :], start=c == 0, stop=c == CH - 1)
            last.then_inc(s["pr_mm"], 1)
            pe.wait_ge(s["pr_ev"], 6)
            for c in range(CH):
                last = mm(av[0:NQ + 1, 0:D], wqoT[:, c, :], w2[:, D * c:D * c + D], start=c == 0, stop=c == CH - 1)
            last.then_inc(s["pr_mm"], 1)

            def butterflies_done():
                pe.wait_ge(s["bf_dn"], 4 * STAGES)
                transposes(score[0], [wcon_t[:, P * c:P * c + P] for c in range(CH)]).then_inc(s["pr_pe"], 1)
                pe.wait_ge(s["bf_b"], 4 * STAGES)
                for c in range(CH):
                    last = mm(av[:, 256 + c:257 + c], bexp[:, P * c:P * c + P], one[:, :], start=True, stop=True)
                last.then_inc(s["pr_pe"], 1)

            def chain_a(step, n, q):
                if step == "A_h":
                    pe.wait_ge(s["A_xh"], n + 1)
                    need(pe, s["kf_ready"], n)
                    transposes(ca_, [xh[:, t, :] for t in range(T)]).then_inc(s["A_tp"], 1)
                elif step == "A_qk":
                    pe.wait_ge(s["h_ready"], n + 1)
                    for t in range(T):
                        last = mm(ca_[:, P * t:P * t + P], h_F[q][:, P * t:P * t + P], wqk[:, :], start=True, stop=True)
                    last.then_inc(s["A_qkmm"], 1)
                elif step == "A_q":
                    pe.wait_ge(s["A_qk1"], n + 1)
                    mm(ca_[:, :], wq[:, :], h_F[q][:, :], start=True, stop=True).then_inc(s["A_qmm"], 1)
                elif step == "A_k":
                    pe.wait_ge(s["q_ready"], n + 1)
                    mm(ca_[:, :], wk[:, :], h_F[q][:, :], start=True, stop=True).then_inc(s["A_kmm"], 1)
                elif step == "A_v":
                    pe.wait_ge(s["k_ready"], n + 1)
                    for t in range(T):
                        last = mm(ca_[:, P * t:P * t + P], h_F[q][:, P * t:P * t + P], wv[:, :], start=True, stop=True)
                    last.then_inc(s["A_vmm"], 1)
                elif step in ("A_tq", "A_tk"):
                    side = step == "A_tk"
                    if side:
                        pe.wait_ge(s["qf_ready"], n + 1)
                    else:
                        pe.wait_ge(s["v_ready"], n + 1)
                        pe.wait_ge(s["A_lo"], n + 1)
                    for g in range(2):
                        for t in range(T):
                            at = H * t + 4 * g
                            last = nc.tensor.transpose(ca16[:, TOK * g + P * t:TOK * g + P * t + P],
                                                       parts[:, side, at:at + 4, :, :].rearrange("p h c q -> p (h c q)"),
                                                       ident16[:, :])
                    last.then_inc(s[step], 1)

            def chain_p(step, n, q):
                if step in ("P_o0", "P_o1"):
                    b = step == "P_o1"
                    pe.wait_ge(s["o_ready"], PB * n + b + 1)
                    if b:
                        pe.wait_ge(s["P_at"], PB * n + 1)
                    for t in range(2):
                        for g in range(2):
                            last = nc.tensor.transpose(cp_[:, 256 * t + P * g:256 * t + P * g + P],
                                                       o_F[:, b, S * g + P * t:S * g + P * t + P], ident[:, :])
                    last.then_inc(s["P_tO"], 1)
                elif step == "P_at":
                    pe.wait_ge(s["P_at"], PB * n + 2)
                    transposes(cp_, [at_T[:, t, :] for t in range(T)]).then_inc(s["P_tat"], 1)
                elif step == "P_u":
                    pe.wait_ge(s["P_atF"], n + 1)
                    for t in range(T):
                        mm(cp_[:, P * t:P * t + P], at_F[:, P * t:P * t + P], wo[:, :], start=True, stop=False)
                        last = mm(cp_[:, P * t:P * t + P], hb_F[q][:, P * t:P * t + P], ident[:, :], start=False, stop=True)
                    last.then_inc(s["P_umm"], 1)
                elif step == "P_x1":
                    pe.wait_ge(s["P_xh1"], n + 1)
                    transposes(cp_, [xh1[:, t, :] for t in range(T)]).then_inc(s["P_tx1"], 1)
                elif step == "P_qm":
                    pe.wait_ge(s["P_x1F"], n + 1)
                    for t in range(T):
                        last = mm(cp_[:, NQ * t:NQ * t + NQ], x1_F[:, P * t:P * t + P], wfm[:, :], start=True, stop=True)
                    last.then_inc(s["P_qmm"], 1)
                elif step == "P_qe":
                    pe.wait_ge(s["P_qe"], n + 1)
                    for t in range(T):
                        last = nc.tensor.transpose(cp_[0:NQ + 1, P * t:P * t + P], qe[:, t, :], ident[:, :])
                    last.then_inc(s["P_tqe"], 1)
                elif step == "P_y":
                    pe.wait_ge(s["P_qeF"], n + 1)
                    for t in range(T):
                        mm(cp_[:, P * t:P * t + P], x1_F[:, P * t:P * t + P], ident[:, :], start=True, stop=False)
                        last = mm(cp_[:, P * t:P * t + P], qe_F[:, P * t:P * t + P], wq2[:, :], start=False, stop=True)
                    last.then_inc(s["P_ymm"], 1)
                elif step == "P_z":
                    pe.wait_ge(s["P_z"], n + 1)
                    transposes(cp_, [z[:, t, :] for t in range(T)]).then_inc(s["P_tz"], 1)
                elif step == "P_ffn":
                    pe.wait_ge(s["P_h2"], n + 1)
                    if isinstance(n, int) and n == 0:
                        pe.wait_ge(s["pr_done"], 2)
                        pe.wait_ge(s["bf_up"], 4 * STAGES)
                    for c in range(CH):
                        if c >= 2:
                            pe.wait_ge(s["P_g"], CH * n + c - 1)
                        mm((cp_, cx_)[c % 2][:, :], wup[:, P * c:P * c + P], h2_F[:, :], start=True, stop=True)\
                            .then_inc(s["P_up"], 1)
                elif step == "P_out":
                    pe.wait_ge(s["P_g"], CH * n + CH)
                    for t in range(T):
                        for c in range(CH):
                            last = mm(cp_[:, P * t:P * t + P], g_F[:, c, P * t:P * t + P], wdn[:, c, :],
                                      start=c == 0, stop=c == CH - 1)
                    last.then_inc(s["P_y2"], 1)

            def norm_rows(n, m):
                pe.wait_ge(s["G_norm"], n - PAIRS + 1)
                if m:
                    pe.wait_ge(s["G_done"], TILES * (n - PAIRS) + m)
                for u in range(2):
                    for k in range(2):
                        c = H * (2 * (m // 4) + k) + 2 * (m % 4) + u
                        at = S * u + P * k
                        last = mm(cx_[:, at:at + P], norms[:, c:c + 1].broadcast_to([P, P]), ident[:, :],
                                  start=True, stop=True)
                last.then_inc(s["G_row"], 1)

            def shifts(n, q, m):
                b = m // 4
                if m == 0:
                    pe.wait_ge(s["G_done"], TILES * (n - PAIRS + 1))
                    pe.wait_ge(s["P_yG"], n)
                for u in range(2):
                    h = 2 * (m % 4) + u
                    for k in range(2):
                        last = mm((cx_, cp_)[u][:, S * k:S * k + S], q_F[q][:, S * b + P * k:S * b + P * k + P],
                                  kpad[q][:, h, S * b:S * b + S], start=True, stop=True)
                last.then_inc(s["G_dots"], 1)
                pe.wait_ge(s["G_neg"], TILES * (n - PAIRS) + m + 1)

            def cosines(n, q, m):
                if m == 0:
                    pe.wait_ge(s["kfpad_in"], 64 * (n + 1))
                need(pe, s["tile_read"], 2 * TILES * n + m - 1)
                b = m // 4
                for u in range(2):
                    h = 2 * (m % 4) + u
                    for k in range(2):
                        last = mm(score[m % 2][:, 512 * u + S * k:512 * u + S * k + S],
                                  kfpad[q][:, h, S * b + P * k:S * b + P * k + P], qf[q][:, h // 4, S * b:S * b + S],
                                  start=True, stop=True)
                last.then_inc(s["fid_mm"], 1)

            def dots(n, q, m, general=False):
                if m == 0:
                    pe.wait_ge(s["kpad_in"], 128 * (n + 1))
                if general:
                    shifts(n, q, m)
                need(pe, s["tile_read"], 2 * TILES * n + TILES + m - 1)
                b = m // 4
                for u in range(2):
                    h = 2 * (m % 4) + u
                    for k in range(2):
                        at = 512 * u + S * k
                        keys = kpad[q][:, h, S * b + P * k:S * b + P * k + P]
                        if not general:
                            last = mm(score[m % 2][:, at:at + S], keys, q_F[q][:, S * b:S * b + S], start=True, stop=True)
                        else:
                            for i in range(2):
                                half = score[m % 2][:, at + P * i:at + P * i + P]
                                mm(half, keys, q_F[q][:, S * b + P * i:S * b + P * i + P], start=True, stop=False)
                                last = mm(half, top[:, 2 * u + i:2 * u + i + 1].broadcast_to([P, P]), ident[:, :],
                                          start=False, stop=True)
                last.then_inc(s["cw_mm"], 1)

            def heads(n, q, w):
                b, g = w // 2, w % 2
                pe.wait_ge(s["exp_done"], TILES * n + 2 * w + 2)
                if g == 0:
                    need(pe, s["o_ready"], PB * n + b)
                for k in range(2):
                    for j in range(4):
                        last = mm(av[32 * j:32 * j + 32, S * g:S * g + S], v_T[q][:, 2 * b + k, 4 * g + j, :],
                                  prob[:, 2 * w + j // 2, 512 * (j % 2) + S * k:512 * (j % 2) + S * k + S],
                                  start=k == 0, stop=k == 1, skip_group_check=True)
                last.then_inc(s["av_done"], 1)

            def body(n, q, prev, nxt, general=False):
                for k in range(2 * TILES):
                    if k < TILES:
                        if general:
                            norm_rows(n, k)
                        cosines(n, q, k)
                    else:
                        dots(n, q, k - TILES, general)
                        if k - TILES in (3, 5, 7):
                            heads(n, q, (k - TILES - 3) // 2)
                    if prev and k in PREV_AT:
                        chain_p(PREV_AT[k], n - 1, 1 - q)
                    if nxt and k in NEXT_AT:
                        chain_a(NEXT_AT[k], n + 1, 1 - q)
                heads(n, q, 3)
                if prev:
                    pe.wait_ge(s["P_yG"], n)

            butterflies_done()
            for k in range(2 * TILES):
                if k in NEXT_AT:
                    chain_a(NEXT_AT[k], 0, 0)
            body(0, 0, False, True)
            with pe.Fori(0, (PAIRS - 2) // 2) as i:
                body(2 * i + 1, 1, True, True)
                body(2 * i + 2, 0, True, True)
            body(PAIRS - 1, 1, True, False)
            for k in range(2 * TILES):
                if k in PREV_AT:
                    chain_p(PREV_AT[k], PAIRS - 1, 1)

            def general(n, q):
                for step in NEXT_AT.values():
                    chain_a(step, n, q)
                body(n, q, False, False, True)
                for step in PREV_AT.values():
                    chain_p(step, n, q)

            pe.wait_ge(s["flag_sum"], 1)
            mm(av[0:1, 0:1], n_good[:, :], ones_col[:, :], start=True, stop=True).then_inc(s["flag_mm"], 1)
            general_pass(pe, general)

        @block.scalar
        def _(act):
            fn = nc.scalar.activation
            act.wait_ge(s["w_in"], 16 * LOADS)
            fn(c_silu, c_sb, ACT.Silu).then_inc(s["pr_silu"], 1)

            def chain_a(step, n, q):
                if step == "A_h":
                    act.wait_ge(s["modA_in"], 16 * (n + 1))
                    act.wait_ge(s["A_tp"], n + 1)
                    for b in range(PB):
                        src = ca_[:, S * b:S * b + S]
                        fn(h_F[q][:, S * b:S * b + S], src, ACT.Identity, scale=modA[:, b, 0:1], bias=modA[:, b, 1:2])
                        last = fn(hb_F[q][:, S * b:S * b + S], src, ACT.Identity,
                                  scale=modA[:, b, 0:1], bias=modA[:, b, 2:3])
                    last.then_inc(s["h_ready"], 1)
                elif step == "A_q":
                    act.wait_ge(s["A_qmm"], n + 1)
                    fn(q_F[q][:, :], ca_[:, :], ACT.Identity, bias=cols[:, BQ:BQ + 1]).then_inc(s["q_ready"], 1)
                elif step == "A_k":
                    act.wait_ge(s["A_kmm"], n + 1)
                    need(act, s["kpad_in"], 128 * n)
                    fn(k_F[:, :], ca_[:, :], ACT.Identity, bias=cols[:, BK:BK + 1]).then_inc(s["k_ready"], 1)
                elif step == "A_v":
                    act.wait_ge(s["A_vmm"], n + 1)
                    fn(v_T[q][:, :, :, 0:HD], ca_[:, :].rearrange("p (t h d) -> p t h d", t=T, h=H), ACT.Copy)\
                        .then_inc(s["v_ready"], 1)
                elif step == "A_hi":
                    act.wait_ge(s["A_qn"], n + 1)
                    for side, slots in ((0, slice(0, 2)), (1, slice(0, 4, 2))):
                        last = fn(parts[:, side, :, slots, :],
                                  qn[:, side, :, :].unsqueeze(2).broadcast_to([P, T * H, 2, NQ]), ACT.Copy)
                    last.then_inc(s["A_hi"], 1)

            def chain_p(step, n, q):
                if step == "P_at":
                    act.wait_ge(s["P_tat"], n + 1)
                    fn(at_F[:, :], cp_[:, :], ACT.Copy).then_inc(s["P_atF"], 1)
                elif step == "P_x1":
                    act.wait_ge(s["P_tx1"], n + 1)
                    fn(x1_F[:, :], cp_[:, :], ACT.Identity, scale=cols[:, G1:G1 + 1], bias=cols[:, BETA1:BETA1 + 1])\
                        .then_inc(s["P_x1F"], 1)
                elif step == "P_sin":
                    act.wait_ge(s["P_r3"], n + 1)
                    fn(qm_sin[:, :], qm_r[:, :], ACT.Sin, scale=-2.0 * PI, bias=half_pi[:, :]).then_inc(s["P_sin"], 1)
                elif step == "P_tanh":
                    act.wait_ge(s["P_qm"], n + 1)
                    fn(qm_tanh[:, :], qm[:, :], ACT.Tanh).then_inc(s["P_tanh"], 1)
                elif step == "P_qe":
                    act.wait_ge(s["P_tqe"], n + 1)
                    fn(qe_F[:, :], cp_[0:NQ + 1, :], ACT.Copy).then_inc(s["P_qeF"], 1)
                elif step == "P_z":
                    act.wait_ge(s["modP_in"], 16 * (n + 1))
                    act.wait_ge(s["P_tz"], n + 1)
                    for b in range(PB):
                        last = fn(h2_F[:, S * b:S * b + S], cp_[:, S * b:S * b + S], ACT.Identity,
                                  scale=modP[:, b, 0:1], bias=modP[:, b, 1:2])
                    last.then_inc(s["P_h2"], 1)
                elif step == "P_ffn":
                    for c in range(CH):
                        act.wait_ge(s["P_up"], CH * n + c + 1)
                        fn(g_F[:, c, :], (cp_, cx_)[c % 2][:, :], ACT.Gelu, bias=bup[:, c:c + 1]).then_inc(s["P_g"], 1)

            def evacuate(n, b):
                act.wait_ge(s["av_done"], 4 * n + 2 * b + 2)
                if b == 0:
                    need(act, s["P_tO"], PB * n)
                fn(o_F[:, b, :], av[:, :], ACT.Copy).then_inc(s["o_ready"], 1)

            def body(n, q, prev, nxt, general=False):
                for k in range(2 * TILES):
                    m = k % TILES
                    if k < TILES:
                        if general:
                            act.wait_ge(s["G_done"], TILES * (n - PAIRS) + m + 1)
                        else:
                            act.wait_ge(s["fid_mm"], TILES * n + m + 1)
                        need(act, s["tile_read"], 2 * TILES * n + m - 1 if m >= 2 else 2 * TILES * (n - 1) + m + TILES - 1)
                        fn(sines[:, m % 2, :], score[m % 2][:, :], ACT.Sin, scale=SIN_SCALE).then_inc(s["sin_done"], 1)
                        if k == 0 and prev:
                            evacuate(n - 1, 1)
                    else:
                        act.wait_ge(s["tile_read"], 2 * TILES * n + TILES + m + 1)
                        fn(prob[:, m, :], prob[:, m, :], ACT.Exp, scale=0.05).then_inc(s["exp_done"], 1)
                        if m == 6:
                            evacuate(n, 0)
                    if prev and k in PREV_AT:
                        chain_p(PREV_AT[k], n - 1, 1 - q)
                    if nxt and k in NEXT_AT:
                        chain_a(NEXT_AT[k], n + 1, 1 - q)

            for k in range(2 * TILES):
                if k in NEXT_AT:
                    chain_a(NEXT_AT[k], 0, 0)
            body(0, 0, False, True)
            with act.Fori(0, (PAIRS - 2) // 2) as i:
                body(2 * i + 1, 1, True, True)
                body(2 * i + 2, 0, True, True)
            body(PAIRS - 1, 1, True, False)
            evacuate(PAIRS - 1, 1)
            for k in range(2 * TILES):
                if k in PREV_AT:
                    chain_p(PREV_AT[k], PAIRS - 1, 1)

            def general(n, q):
                for step in NEXT_AT.values():
                    chain_a(step, n, q)
                body(n, q, False, False, True)
                evacuate(n, 1)
                for step in PREV_AT.values():
                    chain_p(step, n, q)

            general_pass(act, general)

        @block.vector
        def _(dve):
            v = nc.vector

            v.memset(half_pi[:, :], PI / 2)
            v.memset(one[:, :], 1.0)
            v.memset(ones_col[:, :], 1.0)
            v.memset(n2_least[:, :], 1.0)
            v.memset(l_least[:, :], 1.0)
            v.memset(l_total[:, :], 0.0)
            v.memset(qe[:, :, NQ:NQ + 1], 1.0)
            for i in range(2):
                v.memset(v_T[i][:, :, :, HD:32], 1.0).then_inc(s["ones_ready"], 1)
            dve.wait_ge(s["w_in"], 16 * LOADS)

            def taken(n_mm):
                dve.wait_ge(s["pr_mm"], n_mm)

            taken(1)
            v.tensor_copy(sT, cp_[:, 0:B]).then_inc(s["pr_ev"], 1)
            taken(2)
            v.tensor_copy(x2[:, 1:3, :].rearrange("p a b -> p (a b)"), cx_[:, 0:256]).then_inc(s["pr_ev"], 1)
            taken(3)
            v.tensor_copy(cols[:, :], ca_[:, 0:14]).then_inc(s["pr_ev"], 1)
            dve.wait_ge(s["pr_ev"], 3)
            for dst, c in ((bcasts, BQ), (bcast1, BK), *((b1_cols[:, i, :], B1 + i) for i in range(CH))):
                last = v.tensor_scalar(dst, ident[:, :], 0.0, cols[:, c:c + 1], ALU.mult, ALU.add)
            last.then_inc(s["pr_ev"], 1)
            taken(4)
            v.tensor_copy(w1T, score[0][:, 0:512]).then_inc(s["pr_ev"], 1)
            taken(5)
            v.tensor_copy(wqoT.rearrange("p c q -> p (c q)"), av[:, 0:CH * (NQ + 1)]).then_inc(s["pr_ev"], 1)
            taken(6)
            v.tensor_copy(wcon_t, score[0][:, 512:1024]).then_inc(s["pr_ev"], 1)
            taken(7)
            v.tensor_scalar(mod_cols[:, :, 0], score[1][:, 0:B], 1.0, None, ALU.add)
            v.tensor_copy(mod_cols[:, :, 1], score[1][:, B:2 * B])
            v.tensor_copy(mod_cols[:, :, 4], score[1][:, 3 * B:4 * B])
            v.tensor_scalar(mod_cols[:, :, 3], score[1][:, 2 * B:3 * B], 1.0, None, ALU.add)
            v.tensor_copy(gate.rearrange("b r d -> b (r d)"), score[1][0:B, 512:768]).then_inc(s["pr_ev"], 1)
            dve.wait_ge(s["pr_ev"], 8)
            v.tensor_scalar(gate_s, gate, 0.0, 2.0, ALU.is_ge, ALU.mult).then_inc(s["pr_c"], 1)
            v.scalar_tensor_tensor(gate_rows[:, 0:2, :], gate, -1.0, gate, ALU.mult, ALU.max).then_inc(s["pr_c"], 1)
            v.tensor_tensor(vec16[:, 2, :], vec16[:, 2, :], vec16[:, 3, :], ALU.add).then_inc(s["pr_c"], 1)
            dve.wait_ge(s["pr_c"], 3)
            v.tensor_scalar(gate, gate_rows[:, 0:2, :], 0.25, None, ALU.max).then_inc(s["pr_c"], 1)
            dve.wait_ge(s["pr_c"], 4)
            v.scalar_tensor_tensor(gate_s, gate_s, -1.0, gate, ALU.add, ALU.mult).then_inc(s["pr_c"], 1)
            dve.wait_ge(s["pr_c"], 5)
            v.tensor_tensor(gate_rows[:, 0, :], gate_s[:, 0, :], vec16[:, 0, :], ALU.mult)
            v.tensor_tensor(gate_rows[:, 1, :], gate_s[:, 0, :], vec16[:, 1, :], ALU.mult)
            v.tensor_copy(gate_rows[:, 2, :], gate_s[:, 1, :])
            v.tensor_tensor(gate_rows[:, 3, :], gate_s[:, 1, :], vec16[:, 2, :], ALU.mult).then_inc(s["pr_c"], 1)
            taken(8)
            v.tensor_copy(wqk[:, :], cx_[:, 0:P])
            v.tensor_tensor(bqk_row[:, :].rearrange("p (s c) -> p s c", s=2), cx_[:, P:2 * P].rearrange("p (s c) -> p s c", s=2),
                            bc2q_row.unsqueeze(1).broadcast_to([P, 2, 64]), ALU.add).then_inc(s["pr_c"], 1)
            taken(9)
            v.tensor_tensor(rec[:, 0:1], cp_[:, 0:1], cols[:, BO:BO + 1], ALU.add).then_inc(s["pr_c"], 1)
            dve.wait_ge(s["pr_c"], 8)
            v.tensor_scalar(mod_cols[:, :, 2], mod_cols[:, :, 1], rec[:, 0:1], None, ALU.add).then_inc(s["pr_c"], 1)
            taken(10)
            v.tensor_copy(wfm[:, :], ca_[:, 0:NQ])
            v.tensor_tensor(bfm_row[:, :], ca_[:, NQ:2 * NQ], bm_row, ALU.add)
            taken(11)
            v.tensor_tensor(wq2[:, :], av[0:NQ + 1, 0:D], b2_rows, ALU.add).then_inc(s["pr_c"], 1)
            dve.wait_ge(s["pr_c"], 10)
            v.memset(rec[:, :], 0.0).then_inc(s["pr_done"], 1)

            def stats(c, n, tiles, sem_sum, sem_agg, sem_var):
                for t in range(T):
                    last = v.bn_stats(stat[c][:, t, :], tiles[t])
                last.then_inc(s[sem_sum], 1)
                dve.wait_ge(s[sem_sum], n + 1)
                even, odd = stat[c][:, :, 1], stat[c][:, :, 4]
                v.tensor_tensor(agg[c][:, :, 1], even, odd, ALU.subtract)
                v.scalar_tensor_tensor(var[c][:, :], stat[c][:, :, 2], LN_EPS * D, stat[c][:, :, 5], ALU.add, ALU.add)
                v.tensor_tensor(agg[c][:, :, 0], even, odd, ALU.add).then_inc(s[sem_agg], 1)
                dve.wait_ge(s[sem_agg], 3 * n + 1)
                v.scalar_tensor_tensor(agg[c][:, :, 1], agg[c][:, :, 1], 0.25, agg[c][:, :, 1], ALU.mult, ALU.mult)\
                    .then_inc(s[sem_agg], 1)
                v.tensor_scalar(agg[c][:, :, 0], agg[c][:, :, 0], 0.5, None, ALU.mult).then_inc(s[sem_agg], 1)
                dve.wait_ge(s[sem_agg], 3 * n + 3)
                v.scalar_tensor_tensor(var[c][:, :], var[c][:, :], 1.0 / D, agg[c][:, :, 1], ALU.mult, ALU.add)\
                    .then_inc(s[sem_var], 1)

            def normalise(c, tiles, outs):
                for t in range(T):
                    last = v.tensor_scalar(outs[:, t, :], tiles[t], agg[c][:, t, 0:1], rstd[c][:, t:t + 1],
                                           ALU.subtract, ALU.mult)
                return last

            def tiles_of(x):
                return [x[:, P * t:P * t + P] for t in range(T)]

            def chain_a(step, n, q):
                if step == "A_stats":
                    dve.wait_ge(s["x_in"], 16 * (n + 1))
                    stats("A", n, [x_a[:, t, :] for t in range(T)], "A_sum", "A_agg", "A_var")
                elif step == "A_norm":
                    dve.wait_ge(s["A_rstd"], n + 1)
                    need(dve, s["A_tp"], n)
                    normalise("A", [x_a[:, t, :] for t in range(T)], xh).then_inc(s["A_xh"], 1)
                elif step == "A_qk":
                    dve.wait_ge(s["A_qkmm"], n + 1)
                    need(dve, s["A_qn"], n)
                    v.tensor_tensor(qk[:, :, :, :], ca_[:, :].rearrange("p (t s c) -> p s t c", t=T, s=2),
                                    bqk_row[:, :].rearrange("p (s c) -> p s c", s=2).unsqueeze(2)
                                    .broadcast_to([P, 2, T, 64]), ALU.add).then_inc(s["A_qk1"], 1)
                    dve.wait_ge(s["A_qk1"], n + 1)
                    flat = qk[:, :, :, :].rearrange("p s t c -> p (s t c)")
                    sqf = sq[:, :, :, :].rearrange("p s t c -> p (s t c)")
                    v.tensor_tensor(sqf, flat, flat, ALU.mult).then_inc(s["A_qk2"], 1)
                    dve.wait_ge(s["A_qk2"], n + 1)
                    v.tensor_reduce(n2[:, :], sqf.rearrange("p (a q) -> p a q", q=NQ), AX.X, ALU.add)\
                        .then_inc(s["A_n2"], 1)
                    dve.wait_ge(s["A_n2"], n + 1)
                    v.tensor_tensor(n2_least[:, :], n2_least[:, :], n2[:, :], ALU.min)
                    v.tensor_scalar(n2c[:, :], n2[:, :], TINY, None, ALU.max).then_inc(s["A_qk3"], 1)
                elif step == "A_lo":
                    dve.wait_ge(s["A_hi"], n + 1)
                    for side, lo, hi in ((0, slice(2, 4), slice(0, 1)), (1, slice(1, 4, 2), slice(0, 1))):
                        last = v.tensor_tensor(parts[:, side, :, lo, :],
                                               qn[:, side, :, :].unsqueeze(2).broadcast_to([P, T * H, 2, NQ]),
                                               parts[:, side, :, hi, :].broadcast_to([P, T * H, 2, NQ]), ALU.subtract)
                    last.then_inc(s["A_lo"], 1)
                elif step == "A_tq":
                    dve.wait_ge(s["A_tq"], n + 1)
                    v.tensor_copy(qf[q][:, :, :].rearrange("p g t -> p (g t)"), ca16).then_inc(s["qf_ready"], 1)
                elif step == "A_tk":
                    dve.wait_ge(s["A_tk"], n + 1)
                    need(dve, s["kfpad_in"], 64 * n)
                    v.tensor_copy(kf[:, :, :].rearrange("p g t -> p (g t)"), ca16).then_inc(s["kf_ready"], 1)

            def chain_p(step, n, q):
                if step in ("P_o0", "P_o1"):
                    b = int(step == "P_o1")
                    dve.wait_ge(s["P_tO"], PB * n + b + 1)
                    o = cp_[:, :].rearrange("p (a d) -> p a d", d=32)
                    v.tensor_tensor(l_least[:, :], l_least[:, :], o[:, :, HD], ALU.min)
                    v.tensor_tensor(l_total[:, :], l_total[:, :], o[:, :, HD], ALU.add)
                    v.reciprocal(rec[:, :], o[:, :, HD]).then_inc(s["P_rec"], 1)
                    dve.wait_ge(s["P_rec"], PB * n + b + 1)
                    v.tensor_tensor(at_T[:, 2 * b:2 * b + 2, :].rearrange("p t (h d) -> p (t h) d", h=H), o[:, :, 0:HD],
                                    rec[:, :].unsqueeze(2).broadcast_to([P, 2 * H, HD]), ALU.mult)\
                        .then_inc(s["P_at"], 1)
                elif step == "P_u":
                    dve.wait_ge(s["P_umm"], n + 1)
                    stats("1", n, tiles_of(cp_), "P_s1", "P_g1", "P_v1")
                elif step == "P_x1":
                    dve.wait_ge(s["P_r1"], n + 1)
                    normalise("1", tiles_of(cp_), xh1).then_inc(s["P_xh1"], 1)
                elif step == "P_qm":
                    dve.wait_ge(s["P_qmm"], n + 1)
                    v.tensor_tensor(qm[:, :].rearrange("p (t q) -> p t q", t=T),
                                    cp_[:, 0:T * NQ].rearrange("p (t q) -> p t q", t=T),
                                    bfm_row[:, :].unsqueeze(1).broadcast_to([P, T, NQ]), ALU.add).then_inc(s["P_qm"], 1)
                    dve.wait_ge(s["P_qm"], n + 1)
                    v.tensor_scalar(qm_n[:, :], qm[:, :], 0.125, ROUND, ALU.mult, ALU.add).then_inc(s["P_rr"], 1)
                    dve.wait_ge(s["P_rr"], 3 * n + 1)
                    v.tensor_scalar(qm_n[:, :], qm_n[:, :], -ROUND, None, ALU.add).then_inc(s["P_rr"], 1)
                    dve.wait_ge(s["P_rr"], 3 * n + 2)
                    v.scalar_tensor_tensor(qm_r[:, :], qm[:, :], 0.125, qm_n[:, :], ALU.mult, ALU.subtract)\
                        .then_inc(s["P_rr"], 1)
                    dve.wait_ge(s["P_rr"], 3 * n + 3)
                    v.scalar_tensor_tensor(qm_n[:, :], qm_r[:, :], -1.0, qm_r[:, :], ALU.mult, ALU.max)\
                        .then_inc(s["P_r2"], 1)
                    dve.wait_ge(s["P_r2"], n + 1)
                    v.tensor_scalar(qm_r[:, :], qm_n[:, :], 0.5, None, ALU.min).then_inc(s["P_r3"], 1)
                elif step == "P_tanh":
                    dve.wait_ge(s["P_sin"], n + 1)
                    dve.wait_ge(s["P_tanh"], n + 1)
                    v.tensor_tensor(qe[:, :, 0:NQ], qm_sin[:, :].rearrange("p (t q) -> p t q", t=T),
                                    qm_tanh[:, :].rearrange("p (t q) -> p t q", t=T), ALU.mult).then_inc(s["P_qe"], 1)
                elif step == "P_y":
                    dve.wait_ge(s["P_ymm"], n + 1)
                    stats("2", n, tiles_of(cp_), "P_s2", "P_g2", "P_v2")
                elif step == "P_v":
                    dve.wait_ge(s["P_r2d"], n + 1)
                    normalise("2", tiles_of(cp_), vv).then_inc(s["P_v"], 1)
                elif step == "P_x2":
                    dve.wait_ge(s["P_v"], n + 1)
                    dve.wait_ge(s["P_xB"], n + 1)
                    v.tensor_tensor(vv[:, :, :].rearrange("p (b t) d -> p b t d", b=PB),
                                    vv[:, :, :].rearrange("p (b t) d -> p b t d", b=PB),
                                    rows[q][:, :, 0:1, :].broadcast_to([P, PB, 2, D]), ALU.mult).then_inc(s["P_vG"], 1)
                    dve.wait_ge(s["P_vG"], n + 1)
                    v.tensor_tensor(x2[:, :, :], vv[:, :, :], xB[:, :, :], ALU.add).then_inc(s["P_x2"], 1)
                    dve.wait_ge(s["P_x2"], n + 1)
                    stats("3", n, [x2[:, t, :] for t in range(T)], "P_s3", "P_g3", "P_v3")
                elif step == "P_z":
                    dve.wait_ge(s["P_r3d"], n + 1)
                    normalise("3", [x2[:, t, :] for t in range(T)], z).then_inc(s["P_z"], 1)
                elif step == "P_out":
                    dve.wait_ge(s["P_y2"], n + 1)
                    dve.wait_ge(s["P_x2c"], n + 1)
                    dve.wait_ge(s["stored"], 16 * (n + 1))
                    v.tensor_tensor(o_T[:, :, :].rearrange("p (b t) d -> p b t d", b=PB),
                                    cp_[:, :].rearrange("p (b t d) -> p b t d", b=PB, t=2),
                                    rows[q][:, :, 2:3, :].broadcast_to([P, PB, 2, D]), ALU.mult).then_inc(s["P_yG"], 1)
                    dve.wait_ge(s["P_yG"], n + 1)
                    v.tensor_tensor(o_T[:, :, :], o_T[:, :, :], x2c[:, :, :], ALU.add).then_inc(s["P_out"], 1)

            def guard(n, m):
                dve.wait_ge(s["fid_mm"], TILES * n + m + 1)
                dve.wait_ge(s["G_row"], TILES * (n - PAIRS) + m + 1)
                for u in range(2):
                    for k in range(2):
                        c = 32 + H * (2 * (m // 4) + k) + 2 * (m % 4) + u
                        v.tensor_scalar(shrink[:, S * k:S * k + S], cx_[:, S * u:S * u + S],
                                        norms[:, c:c + 1], 1.0 / EPS_COS, ALU.mult, ALU.mult).then_inc(s["G_shrink"], 1)
                    dve.wait_ge(s["G_shrink"], 4 * (TILES * (n - PAIRS) + m) + 2 * u + 2)
                    tile = score[m % 2][:, 512 * u:512 * u + 512]
                    last = v.scalar_tensor_tensor(tile, shrink[:, :], 1.0, tile, ALU.min, ALU.mult)
                    last.then_inc(s["G_scaled"], 1)
                    dve.wait_ge(s["G_scaled"], 2 * (TILES * (n - PAIRS) + m) + u + 1)
                v.tensor_copy(top[:, 0:1], norms[:, 0:1]).then_inc(s["G_done"], 1)

            def maxima(n, m):
                dve.wait_ge(s["G_dots"], TILES * (n - PAIRS) + m + 1)
                for u in range(2):
                    last = v.tensor_reduce(shrink[:, 2 * u:2 * u + 2], (cx_, cp_)[u][:, :].rearrange("p (k t) -> p k t", k=2),
                                           AX.X, ALU.max)
                last.then_inc(s["G_max"], 1)
                dve.wait_ge(s["G_max"], TILES * (n - PAIRS) + m + 1)
                v.tensor_scalar(top[:, :], shrink[:, 0:4], -1.0, None, ALU.mult).then_inc(s["G_neg"], 1)

            def body(n, q, prev, nxt, general=False):
                if general:
                    v.tensor_tensor(norms[:, :], n2c[:, :], rn[:, :], ALU.mult).then_inc(s["G_norm"], 1)
                for k in range(2 * TILES):
                    m = k % TILES
                    if general and k < TILES:
                        guard(n, m)
                    if general and k >= TILES:
                        maxima(n, m)
                    if k < TILES:
                        dve.wait_ge(s["sin_done"], TILES * n + m + 1)
                        need(dve, s["av_done"], 4 * n)
                        v.scalar_tensor_tensor(prob[:, m, :], sines[:, m % 2, :], 10.0, score[m % 2][:, :],
                                               ALU.add, ALU.mult).then_inc(s["tile_read"], 1)
                    else:
                        dve.wait_ge(s["cw_mm"], TILES * n + m + 1)
                        v.scalar_tensor_tensor(prob[:, m, :], score[m % 2][:, :], 2.5, prob[:, m, :],
                                               ALU.mult, ALU.add).then_inc(s["tile_read"], 1)
                    if prev and k in PREV_AT:
                        chain_p(PREV_AT[k], n - 1, 1 - q)
                    if nxt and k in NEXT_AT:
                        chain_a(NEXT_AT[k], n + 1, 1 - q)

            dve.wait_ge(s["bf_in"], 16 * 2 * STAGES)
            for j in range(STAGES):
                butterfly(dve, v, bexp, up_w[j], prod_b, False, j, s["bf_b"], 4 * j)
            for j in range(STAGES):
                butterfly(dve, v, wcon_t, dn_w[STAGES - 1 - j], prod_dn, True, STAGES - 1 - j, s["bf_dn"], 4 * j)
            dve.wait_ge(s["pr_pe"], 2)
            v.tensor_copy(wdn[:, :, :].rearrange("p c d -> p (c d)"), score[0][:, 0:512])
            v.tensor_tensor(bup[:, :], av[:, 256:256 + CH], cols[:, UPB:UPB + CH], ALU.add).then_inc(s["pr_done"], 1)

            for k in range(2 * TILES):
                if k in NEXT_AT:
                    chain_a(NEXT_AT[k], 0, 0)
            body(0, 0, False, True)
            with dve.Fori(0, (PAIRS - 2) // 2) as i:
                body(2 * i + 1, 1, True, True)
                body(2 * i + 2, 0, True, True)
            body(PAIRS - 1, 1, True, False)
            for k in range(2 * TILES):
                if k in PREV_AT:
                    chain_p(PREV_AT[k], PAIRS - 1, 1)

            def general(n, q):
                for step in NEXT_AT.values():
                    chain_a(step, n, q)
                body(n, q, False, False, True)
                for step in PREV_AT.values():
                    chain_p(step, n, q)

            v.tensor_scalar(good[:, 0:64], n2_least[:, :], EPS_COS, None, ALU.is_ge)
            v.tensor_scalar(good[:, 64:80], l_least[:, :], SUM_LEAST, None, ALU.is_ge)
            v.tensor_scalar(good[:, 80:96], l_total[:, :], SUM_MOST, None, ALU.is_le).then_inc(s["flag_good"], 1)
            dve.wait_ge(s["flag_good"], 1)
            v.tensor_reduce(n_good[:, :], good[:, :], AX.X, ALU.add).then_inc(s["flag_sum"], 1)
            dve.wait_ge(s["flag_mm"], 1)
            v.tensor_scalar(flag[:, :], av[0:1, 0:1], 96.0 * P - 0.5, None, ALU.is_lt).then_inc(s["flag_ready"], 1)
            general_pass(dve, general)

        @block.gpsimd
        def _(pool):
            g = nc.gpsimd
            g.memset(blk, 0.0).then_inc(s["w_zero"], 1)
            g.memset(b2_rows, 0.0).then_inc(s["w_zero"], 1)
            g.memset(ident[:, :], 0.0).then_inc(s["w_ident"], 1)
            g.memset(ident16[:, :], 0.0).then_inc(s["w_ident"], 1)
            pool.wait_ge(s["w_ident"], 2)
            for eye in (ident, ident16):
                g.affine_select(out=eye[:, :], in_=eye[:, :], compare_op=ALU.not_equal, fill=1.0,
                                base=0, pattern=[[-1, P]], channel_multiplier=1).then_inc(s["w_ident"], 1)
            g.memset(neg_half[:, :], -0.5).then_inc(s["w_step"], 1)
            for i in range(2):
                g.memset(kfpad[i][:, :, :], 0.0)
            pool.wait_ge(s["w_in"], 16 * LOADS)
            pool.wait_ge(s["bf_in"], 16 * 2 * STAGES)
            for j in range(STAGES):
                butterfly(pool, g, wup[:, :], up_w[j], prod_up, False, j, s["bf_up"], 4 * j)
            pool.wait_ge(s["bf_dn"], 4 * STAGES)
            pool.wait_ge(s["bf_b"], 4 * STAGES)
            for i in range(2):
                g.memset(kpad[i][:, :, :], 0.0).then_inc(s["zeroed"], 1)
            pool.wait_ge(s["w_step"], 1)

            def power(out_, in_, sem):
                g.tensor_tensor(out_, in_, neg_half[:, 0:in_.shape[1]], ALU.pow).then_inc(sem, 1)

            def chain_a(step, n, q):
                if step == "A_stats":
                    pool.wait_ge(s["A_var"], n + 1)
                    power(rstd["A"][:, :], var["A"][:, :], s["A_rstd"])
                elif step == "A_q":
                    pool.wait_ge(s["A_qk3"], n + 1)
                    power(rn[:, :], n2c[:, :], s["A_rn"])
                elif step == "A_qn":
                    pool.wait_ge(s["A_rn"], n + 1)
                    need(pool, s["A_lo"], n)
                    g.tensor_tensor(qn[:, :, :, :].rearrange("p s a q -> p (s a) q"),
                                    qk[:, :, :, :].rearrange("p s t (h q) -> p (s t h) q", q=NQ),
                                    rn[:, :].unsqueeze(2).broadcast_to([P, 64, NQ]), ALU.mult).then_inc(s["A_qn"], 1)

            def chain_p(step, n, q):
                if step == "P_o1":
                    pool.wait_ge(s["xp_in"], 16 * (n + 1))
                    pool.wait_ge(s["rows_in"], 16 * (n + 1))
                    g.tensor_tensor(xB[:, :, :].rearrange("p (b t) d -> p b t d", b=PB),
                                    x_p[:, :, :].rearrange("p (b t) d -> p b t d", b=PB),
                                    rows[q][:, :, 1:2, :].broadcast_to([P, PB, 2, D]), ALU.add).then_inc(s["P_xB"], 1)
                elif step == "P_u":
                    pool.wait_ge(s["P_v1"], n + 1)
                    power(rstd["1"][:, :], var["1"][:, :], s["P_r1"])
                elif step == "P_y":
                    pool.wait_ge(s["P_v2"], n + 1)
                    power(rstd["2"][:, :], var["2"][:, :], s["P_r2d"])
                elif step == "P_x2":
                    pool.wait_ge(s["P_v3"], n + 1)
                    power(rstd["3"][:, :], var["3"][:, :], s["P_r3d"])
                elif step == "P_z":
                    g.tensor_tensor(x2c[:, :, :].rearrange("p (b t) d -> p b t d", b=PB),
                                    x2[:, :, :].rearrange("p (b t) d -> p b t d", b=PB),
                                    rows[q][:, :, 3:4, :].broadcast_to([P, PB, 2, D]), ALU.add).then_inc(s["P_x2c"], 1)

            def body(n, q, prev, nxt, general=False):
                for k in range(2 * TILES):
                    if prev and k in PREV_AT:
                        chain_p(PREV_AT[k], n - 1, 1 - q)
                    if nxt and k in NEXT_AT:
                        chain_a(NEXT_AT[k], n + 1, 1 - q)

            for k in range(2 * TILES):
                if k in NEXT_AT:
                    chain_a(NEXT_AT[k], 0, 0)
            body(0, 0, False, True)
            with pool.Fori(0, (PAIRS - 2) // 2) as i:
                body(2 * i + 1, 1, True, True)
                body(2 * i + 2, 0, True, True)
            body(PAIRS - 1, 1, True, False)
            for k in range(2 * TILES):
                if k in PREV_AT:
                    chain_p(PREV_AT[k], PAIRS - 1, 1)

            def general(n, q):
                for step in NEXT_AT.values():
                    chain_a(step, n, q)
                body(n, q, False, False, True)
                for step in PREV_AT.values():
                    chain_p(step, n, q)

            general_pass(pool, general)


_INS = ["L0_attn_x", "L0_attn_Wq", "L0_attn_bq", "L0_attn_Wk", "L0_attn_bk", "L0_attn_Wv", "L0_attn_bv",
        "L0_attn_Wc2q", "L0_attn_bc2q", "L0_attn_Wo", "L0_attn_bo", "L0_attn_g1", "L0_attn_beta1", "L0_attn_g2",
        "L0_attn_beta2", "L0_attn_W1", "L0_attn_b1", "L0_attn_Wm", "L0_attn_bm", "L0_attn_Wqo", "L0_attn_bqo",
        "L0_attn_W2", "L0_attn_b2", "L0_ffn_W_exp", "L0_ffn_b_exp", "L0_ffn_up_weights", "L0_ffn_up_bias",
        "L0_ffn_down_weights", "L0_ffn_W_con", "L0_ffn_b_con", "L0_ffn_down_bias", "L0_c", "L0_wmod"]


def kernel(**inputs):
    import concourse.bacc as bacc
    import numpy as np
    from concourse.bass_utils import run_bass_kernel_spmd

    nc = bacc.Bacc("TRN2", target_bir_lowering=False, num_devices=1)
    arrays, args = {}, {}
    for name in _INS:
        arrays[f"in_{name}"] = np.ascontiguousarray(inputs[name])
        args[name] = nc.dram_tensor(f"in_{name}", arrays[f"in_{name}"].shape,
                                    mybir.dt.from_np(arrays[f"in_{name}"].dtype), kind="ExternalInput").ap()
    out = nc.dram_tensor("out", (B, S, D), F32, kind="ExternalOutput").ap()
    build(nc, args, out)
    r = run_bass_kernel_spmd(nc, [arrays], core_ids=[0])
    return r.results[0]["out"]
```

```python
from contextlib import ExitStack

import concourse.bass as bass
from concourse import mybir

F32 = mybir.dt.float32
F16 = mybir.dt.float16
ALU = mybir.AluOpType
ACT = mybir.ActivationFunctionType
AX = mybir.AxisListType

P = 128
B, S, D = 16, 256, 128
H, HD, NQ = 8, 16, 8
FF = 512
PB = 2
PAIRS = B // PB
TOK = PB * S
T = TOK // P
CH = FF // P
STAGES = 9
BLOCK_STAGES = 7
TILES = PB * H // 2
LN_EPS = 1e-5
PI = 3.141592653589793
SIN_SCALE = PI * (1.0 - 2.0 ** -20)
TINY = 1e-36
EPS_COS = 1e-8
SUM_LEAST, SUM_MOST = 1e-20, 1e30
ROUND = 1.5 * 2.0 ** 23

A_STEPS = ("A_stats", "A_norm", "A_h", "A_qk", "A_n2", "A_q", "A_k", "A_v", "A_qn", "A_hi", "A_lo", "A_tq", "A_tk")
P_STEPS = ("P_h3", "P_e1", "P_o0", "P_o1", "P_at", "P_u", "P_x1", "P_qm", "P_rr", "P_sin", "P_tanh", "P_qe", "P_y", "P_v",
           "P_x2", "P_z", "P_f0", "P_f1", "P_f2", "P_f3", "P_out")
PLAN = {
    "pe": ["P_h3 P_o0", "", "P_o1 P_at", "P_u", "A_h P_x1 A_qk", "P_qm", "A_q A_k", "A_v P_qe", "P_y", "", "",
           "H0", "A_tq H1", "P_z A_tk", "P_f0 P_f1 P_f2 P_f3", "P_out H2"],
    "act": ["P_e1", "", "P_at", "A_h", "P_x1", "", "A_q P_sin A_k P_tanh", "P_qe", "A_v", "A_hi", "", "", "",
            "P_z P_f0 P_f1 P_f2 P_f3", "E0", ""],
    "dve": ["P_o0", "P_o1 A_stats", "", "A_norm P_u P_x1", "A_qk A_n2", "P_qm P_rr", "P_tanh", "", "P_y",
            "P_v", "", "A_lo", "P_x2 A_tq", "P_z A_tk", "", "P_out"],
    "pool": ["P_o1", "", "", "A_stats", "", "P_u A_n2", "", "", "P_y A_qn", "P_x2", "P_z", "", "", "", "", ""],
}

SEMS = """
w_first w_rest w_zero w_ident w_mask ones_ready
x_in modA_in modP_in xp_in rows_in kpad_in kfpad_in stored
A_sum A_agg A_var A_rstd A_xh A_tp h_ready A_qkmm A_qk1 A_qk2 A_n2 A_qk3 A_rn A_rn2 A_qn A_qmm q_ready A_kmm k_ready
A_vmm v_ready A_hi A_lo A_tq A_tk qf_ready kf_ready
fid_mm sin_done tile_read cw_mm exp_done av_done o_ready
P_tO P_rec P_at P_tat P_atF P_umm P_s1 P_g1 P_v1 P_r1 P_xh1 P_tx1 P_x1F P_qmm P_qm P_rr P_r2 P_r3 P_sin P_tanh P_qe
P_tqe P_qeF P_ymm P_s2 P_g2 P_v2 P_r2d P_v P_vG P_xB P_x2 P_x2c P_s3 P_g3 P_v3 P_r3d P_z P_tz P_h2
P_up P_g P_y2 P_yG P_out
G_norm G_row G_shrink G_scaled G_done G_dots G_max G_neg flag_good flag_sum flag_mm flag_ready
pr_c pr_silu pr_mm pr_ev pr_bo pr_mod pr_rows pr_done pr_pe zeroed0 zeroed1
b_row up_in0 up_in1 up_in2 dn_in0 dn_in1 bf_up bf_b bf_dn
""".split()


def need(eng, sem, count):
    if not isinstance(count, int) or count > 0:
        eng.wait_ge(sem, count)


def build(nc, a, out):
    ctx = ExitStack()
    with ctx:
        def sb(name, shape, dt=F32):
            return ctx.enter_context(nc.sbuf_tensor(name, shape, dt))

        def pb(name, shape, dt=F32):
            return ctx.enter_context(nc.psum_tensor(name, shape, dt))

        s = {name: ctx.enter_context(nc.semaphore(name)) for name in SEMS}

        ident = sb("ident", [P, P])
        ident16 = sb("ident16", [P, P], F16)
        wq = sb("wq", [P, P])
        wk = sb("wk", [P, P])
        wv = sb("wv", [P, P])
        wo = sb("wo", [P, P])
        wqk = sb("wqk", [P, P])
        wfm = sb("wfm", [P, NQ])
        wq2 = sb("wq2", [NQ + 1, P])
        wup = sb("wup", [P, FF])
        wdn = sb("wdn", [P, CH, P])
        cols = sb("cols", [P, 14])
        bup = sb("bup", [P, CH])
        bqk_row = sb("bqk_row", [P, P])
        bfm_row = sb("bfm_row", [P, NQ])
        mod_cols = sb("mod_cols", [P, B, 5])
        half_pi = sb("half_pi", [P, 1])
        neg_half = sb("neg_half", [P, 64])
        BQ, BK, BV, BO, G1, BETA1, B1, UPB = 0, 1, 2, 3, 4, 5, 6, 10

        x_a = sb("x_a", [P, T, D])
        x_p = sb("x_p", [P, T, D])
        modA = sb("modA", [P, PB, 3])
        modP = sb("modP", [P, PB, 2])
        rows = [sb(f"rows{i}", [P, PB, 4, D]) for i in range(2)]
        xh = sb("xh", [P, T, D])
        h_F = [sb(f"h_F{i}", [P, TOK]) for i in range(2)]
        hb_F = [sb(f"hb_F{i}", [P, TOK]) for i in range(2)]
        q_F = [sb(f"q_F{i}", [P, TOK]) for i in range(2)]
        k_F = sb("k_F", [P, TOK])
        kpad = [sb(f"kpad{i}", [P, H, TOK]) for i in range(2)]
        v_T = [sb(f"v_T{i}", [P, T, H, 32]) for i in range(2)]
        qk = sb("qk", [P, 2, T, 64])
        sq = sb("sq", [P, 2, T, 64])
        n2 = sb("n2", [P, 64])
        n2c = sb("n2c", [P, 64])
        n2_least = sb("n2_least", [P, 64])
        l_least = sb("l_least", [P, 2 * H])
        l_total = sb("l_total", [P, 2 * H])
        good = sb("good", [P, 64 + 4 * H])
        n_good = sb("n_good", [P, 1])
        ones_col = sb("ones_col", [P, 1])
        flag = sb("flag", [1, 1], mybir.dt.int32)
        norms = sb("norms", [P, 64])
        shrink = sb("shrink", [P, 512])
        top = sb("top", [P, 4])
        rn = sb("rn", [P, 64])
        qn = sb("qn", [P, 2, T * H, NQ])
        parts = sb("parts", [P, 2, T * H, 4, NQ], F16)
        qf = [sb(f"qf{i}", [P, 2, TOK], F16) for i in range(2)]
        kf = sb("kf", [P, 2, TOK], F16)
        kfpad = [sb(f"kfpad{i}", [P, H, TOK], F16) for i in range(2)]
        stat = {c: sb(f"stat{c}", [P, T, 6]) for c in "A123"}
        agg = {c: sb(f"agg{c}", [P, T, 2]) for c in "A123"}
        var = {c: sb(f"var{c}", [P, T]) for c in "A123"}
        rstd = {c: sb(f"rstd{c}", [P, T]) for c in "A123"}
        sines = sb("sines", [P, 2, 1024])
        prob = sb("prob", [P, TILES, 1024])
        o_F = sb("o_F", [P, PB, TOK])
        rec = sb("rec", [P, 2 * H])
        at_T = sb("at_T", [P, T, D])
        at_F = sb("at_F", [P, TOK])
        xh1 = sb("xh1", [P, T, D])
        x1_F = sb("x1_F", [P, TOK])
        qm = sb("qm", [P, T * NQ])
        qm_n = sb("qm_n", [P, T * NQ])
        qm_r = sb("qm_r", [P, T * NQ])
        qm_sin = sb("qm_sin", [P, T * NQ])
        qm_tanh = sb("qm_tanh", [P, T * NQ])
        qe = sb("qe", [P, T, NQ + 1])
        qe_F = sb("qe_F", [NQ + 1, TOK])
        vv = sb("vv", [P, T, D])
        xB = sb("xB", [P, T, D])
        x2 = sb("x2", [P, T, D])
        x2c = sb("x2c", [P, T, D])
        z = sb("z", [P, T, D])
        h2_F = sb("h2_F", [P, TOK])
        g_F = sb("g_F", [P, CH, TOK])
        o_T = sb("o_T", [P, T, D])

        score = [pb(f"score{i}", [P, 1024]) for i in range(2)]
        av = pb("av", [P, 512])
        ca_ = pb("chainA", [P, 512])
        cp_ = pb("chainP", [P, 512])
        cx_ = pb("chainX", [P, 512])
        ca16 = ca_[:, :].bitcast(F16)

        rows_dram = nc.dram_tensor("gate_rows", [B, 4 * D], F32, kind="Internal").ap()

        ring = sb("ring", [P, 3, 1024])
        up_w = [ring[:, i, :] for i in range(3)]
        dn_w = [g_F[:, 2 * i:2 * i + 2, :].rearrange("p a b -> p (a b)") for i in range(2)]
        wmod = prob[:, 0, 0:6 * D]
        w1 = o_F[:, 0, :]
        w1T = o_F[:, 1, :]
        wcon = sines[:, 0, 0:512]
        wcon_t = x2[:, :, :].rearrange("p t d -> p (t d)")
        w2 = sines[:, 1, 0:512]
        prod_up = h2_F[:, :], at_T[:, :, :].rearrange("p t d -> p (t d)")
        b_blocks = at_F[0:CH, 0:P]
        bexp = x1_F[0:1, :]
        b_w = [rows[1][0:CH, :, :, :].rearrange("p b r (h w) -> p (b r h w)", h=1).rearrange("p (j w) -> p j w", j=4),
               sb("b_w", [CH, BLOCK_STAGES - 4, 2 * P])[:, :, :]]
        prod_blocks = [sb(f"prod_blocks{i}", [CH, P]) for i in range(2)]
        prod_dn = z[:, :, :].rearrange("p t d -> p (t d)"), xh1[:, :, :].rearrange("p t d -> p (t d)")
        prod_b = [o_T[0:1, :, :].rearrange("p t d -> p (t d)"), vv[0:1, :, :].rearrange("p t d -> p (t d)")]
        c_sb = xh1[0:B, 0, :]
        c_silu = xh1[0:B, 1, :]
        bcasts = xh1[:, 2, :]
        bcast1 = xh1[:, 3, :]
        sT = x2[:, 0, 0:B]
        wqT = x2[:, 1, :]
        wkT = x2[:, 2, :]
        blk = x2[:, 3, 0:64]
        bc2q_row = x2[:, 3, 64:128]
        wm = x2c[:, 0, 0:CH * NQ].rearrange("p (c q) -> p c q", c=CH)
        bm_row = x2c[:, 0, 64:64 + NQ]
        wqo = x1_F[0:NQ + 1, :]
        wqoT = x2c[:, 1, 0:CH * (NQ + 1)].rearrange("p (c q) -> p c q", c=CH)
        b2_rows = x2c[0:NQ + 1, 2, :]
        vec_rows = x2c[0:14, 3, :]
        gate = z[0:B, 0:2, :]
        gate_s = z[0:B, 2:4, :]
        gate_rows = xB[0:B, :, :]
        vec16 = vv[0:B, :, :]
        b1_cols = o_T[:, :, :]
        one = sb("one", [1, 1])
        zero = sb("zero", [P, 1])
        head_mask = sb("head_mask", [P, H])
        wc2q = sb("wc2q", [P, NQ])

        x_d = a["L0_attn_x"].rearrange("b s d -> (b s) d").rearrange("(n t p) d -> n p t d", t=T, p=P)
        out_d = out.rearrange("b s d -> (b s) d").rearrange("(n t p) d -> n p t d", t=T, p=P)

        block = ctx.enter_context(nc.Block())
        FIRST_LOADS, REST_LOADS = 16, 16
        EARLY_STAGES = 3
        STAGE_AT = {2 * k: k + EARLY_STAGES for k in range(STAGES - EARLY_STAGES)}
        FOLDED_AT = 14

        FIRST = 0

        def first(n):
            return isinstance(n, int) and n == FIRST

        def pairs_of(x, st):
            return x.rearrange("p (n c j) -> p n c j", c=2, j=st)

        def products(op, y, w, prods, transposed, stage, step):
            st = 2 ** stage
            how = "p (n j c r) -> p r n c j" if transposed else "p (n j r c) -> p r n c j"
            wv_ = w[0:y.shape[0], :].rearrange(how, j=st, r=2, c=2)
            for r in range(2):
                op.tensor_tensor(pairs_of(prods[r], st), pairs_of(y, st), wv_[:, r], ALU.mult).then_inc(step, 1)

        def sums(op, y, prods, stage, step):
            st = 2 ** stage
            for r in range(2):
                pv = pairs_of(prods[r], st)
                op.tensor_tensor(pairs_of(y, st)[:, :, r, :], pv[:, :, 0, :], pv[:, :, 1, :], ALU.add).then_inc(step, 1)

        def general_pass(eng, pair, after=None):
            eng.wait_ge(s["flag_ready"], 1)
            unmet = eng.value_load(flag[0:1, 0:1], min_val=0, max_val=1)
            with eng.If(unmet > 0):
                with eng.Fori(0, PAIRS // 2) as i:
                    pair(2 * i + PAIRS, 0)
                    pair(2 * i + PAIRS + 1, 1)
                if after:
                    after()

        @block.sync
        def _(sp):
            def load(dst, src, sem="w_first"):
                sp.dma_start(dst, src).then_inc(s[sem], 16)

            def rest(dst, src):
                load(dst, src, "w_rest")

            def x_load(dst, sem, n, at):
                sp.dma_start(dst[:, :, :], x_d[at]).then_inc(s[sem], 16)

            x_load(x_a, "x_in", 0, 0)

            load(c_sb, a["L0_c"])
            load(wmod, a["L0_wmod"])
            for w, name in ((wq, "L0_attn_Wq"), (wk, "L0_attn_Wk")):
                load(w[:, :].rearrange("f (h d) -> f h d", h=H), a[name].rearrange("h f d -> f h d"))
            vecs = [("L0_attn_bq", "h d -> (h d)"), ("L0_attn_bk", "h d -> (h d)"), ("L0_attn_bv", "h d -> (h d)"),
                    ("L0_attn_bo", None), ("L0_attn_g1", None), ("L0_attn_beta1", None),
                    ("L0_attn_b1", None), ("L0_ffn_up_bias", None)]
            at = 0
            for name, how in vecs:
                v = a[name].rearrange(how) if how else a[name]
                v = v.rearrange("(r n) -> r n", n=P)
                load(vec_rows[at:at + v.shape[0], :], v)
                at += v.shape[0]
            assert at == 14
            load(wo[:, :], a["L0_attn_Wo"])
            load(wc2q[:, :], a["L0_attn_Wc2q"].rearrange("h d q -> (h d) q"))
            load(bc2q_row, a["L0_attn_bc2q"].rearrange("h q -> (h q)").partition_broadcast(P))
            load(wv[:, :].rearrange("f (h d) -> f h d", h=H), a["L0_attn_Wv"].rearrange("h f d -> f h d"))

            for j, name in enumerate(("L0_attn_g2", "L0_attn_beta2", "L0_ffn_b_con", "L0_ffn_down_bias")):
                rest(vec16[:, j, :], a[name].partition_broadcast(B))
            rest(w1, a["L0_attn_W1"])
            rest(wm, a["L0_attn_Wm"].rearrange("(c k) q -> k c q", c=CH))
            rest(wqo[0:NQ, :], a["L0_attn_Wqo"])
            rest(wqo[NQ:NQ + 1, :], a["L0_attn_bqo"].rearrange("(a n) -> a n", a=1))
            rest(w2.rearrange("k (c f) -> k c f", c=CH), a["L0_attn_W2"].rearrange("(c k) f -> k c f", c=CH))
            rest(wcon.rearrange("k (c f) -> k c f", c=CH), a["L0_ffn_W_con"].rearrange("(c k) f -> k c f", c=CH))
            rest(wup[:, :], a["L0_ffn_W_exp"])
            rest(b_blocks, a["L0_ffn_b_exp"].rearrange("(c n) -> c n", c=CH))
            for tile, stages_ in ((b_w[0], slice(0, 4)), (b_w[1], slice(4, BLOCK_STAGES))):
                rest(tile, a["L0_ffn_up_weights"][stages_].rearrange("j (c k) r i -> c j (k r i)", c=CH))
            rest(bm_row, a["L0_attn_bm"].partition_broadcast(P))
            sp.wait_ge(s["w_zero"], 1)
            rest(b2_rows[NQ:NQ + 1, :], a["L0_attn_b2"].rearrange("(a n) -> a n", a=1))

            def up_in(j):
                if j >= 3:
                    sp.wait_ge(s["bf_up"], 4 * (j - 2))
                    need(sp, s["bf_b"], 4 * (j - 2) if j - 3 >= BLOCK_STAGES else 0)
                sp.dma_start(up_w[j % 3], a["L0_ffn_up_weights"][j].rearrange("k r c -> (k r c)").partition_broadcast(P))\
                  .then_inc(s[f"up_in{j % 3}"], 16)

            def dn_in(j):
                if j >= 2:
                    sp.wait_ge(s["bf_dn"], 4 * (j - 1))
                src = a["L0_ffn_down_weights"][STAGES - 1 - j]
                sp.dma_start(dn_w[j % 2], src.rearrange("k r c -> (k r c)").partition_broadcast(P))\
                  .then_inc(s[f"dn_in{j % 2}"], 16)

            def next_in(n, base=0):
                need(sp, s["A_xh"], n)
                x_load(x_a, "x_in", n, n - base)
                mod_in(n, base)

            def mod_in(n, base=0):
                need(sp, s["h_ready"], n)
                sp.dma_start(modA[:, :, :], mod_cols[:, bass.ds(PB * (n - base), PB), 0:3]).then_inc(s["modA_in"], 16)

            def prev_in(n, q, base=0):
                need(sp, s["P_xB"], n)
                x_load(x_p, "xp_in", n, n - base)
                sp.dma_start(rows[q][:, :, :, :].rearrange("p b r d -> p b (r d)"),
                             rows_dram[bass.ds(PB * (n - base), PB), :].partition_broadcast(P)).then_inc(s["rows_in"], 16)

            def modP_in(n, base=0):
                sp.dma_start(modP[:, :, :], mod_cols[:, bass.ds(PB * (n - base), PB), 3:5]).then_inc(s["modP_in"], 16)

            def keys_out(n, q):
                sp.wait_ge(s["k_ready"], n + 1)
                for h in range(H):
                    sp.dma_start(kpad[q][HD * h:HD * h + HD, h, :], k_F[HD * h:HD * h + HD, :])\
                      .then_inc(s["kpad_in"], 16)

            def key_amps_out(n, q):
                sp.wait_ge(s["kf_ready"], n + 1)
                for j in range(4):
                    sp.dma_start(kfpad[q][32 * j:32 * j + 32, j:H:4, :], kf[32 * j:32 * j + 32, :, :])\
                      .then_inc(s["kfpad_in"], 16)

            def store(n, base=0):
                sp.wait_ge(s["P_out"], n + 1)
                sp.dma_start(out_d[n - base], o_T[:, :, :]).then_inc(s["stored"], 16)

            def body(n, q, prev, nxt):
                if nxt:
                    next_in(n + 1)
                if prev:
                    modP_in(n - 1)
                prev_in(n, q)
                if nxt:
                    keys_out(n + 1, 1 - q)
                    key_amps_out(n + 1, 1 - q)
                if prev:
                    store(n - 1)

            up_in(0)
            dn_in(0)
            sp.wait_ge(s["pr_mod"], 1)
            mod_in(0)
            for j in (1, 2):
                up_in(j)
            dn_in(1)
            sp.wait_ge(s["zeroed0"], 2)
            keys_out(0, 0)
            sp.wait_ge(s["pr_rows"], 1)
            sp.dma_start(rows_dram, gate_rows.rearrange("b r d -> b (r d)")).then_inc(s["stored"], 16)
            key_amps_out(0, 0)
            for j in (3, 4):
                up_in(j)
                dn_in(j - 1)
            next_in(1)
            sp.wait_ge(s["stored"], 16)
            prev_in(0, 0)
            for j in (5, 6, 7):
                up_in(j)
                dn_in(j - 1)
            sp.wait_ge(s["zeroed1"], 2)
            keys_out(1, 1)
            up_in(8)
            dn_in(7)
            sp.wait_ge(s["bf_b"], 4 * BLOCK_STAGES)
            for c in range(CH):
                sp.dma_start(bexp[:, P * c:P * c + P], b_blocks[c:c + 1, :]).then_inc(s["b_row"], 16)
            dn_in(8)
            key_amps_out(1, 1)
            sp.wait_ge(s["pr_done"], 1)
            with sp.Fori(0, (PAIRS - 2) // 2) as i:
                body(2 * i + 1, 1, True, True)
                body(2 * i + 2, 0, True, True)
            body(PAIRS - 1, 1, True, False)
            modP_in(PAIRS - 1)
            store(PAIRS - 1)
            sp.wait_ge(s["stored"], 16 * (PAIRS + 1))

            def general(n, q):
                next_in(n, PAIRS)
                keys_out(n, q)
                key_amps_out(n, q)
                prev_in(n, q, PAIRS)
                modP_in(n, PAIRS)
                store(n, PAIRS)

            general_pass(sp, general, lambda: sp.wait_ge(s["stored"], 16 * (2 * PAIRS + 1)))

        @block.tensor
        def _(pe):
            mm = nc.tensor.matmul

            def transposes(bank, tiles, eye=ident):
                for t, tile in enumerate(tiles):
                    last = nc.tensor.transpose(bank[:, P * t:P * t + P], tile, eye[:, :])
                return last

            def first_products():
                pe.wait_ge(s["w_ident"], 4)
                pe.wait_ge(s["pr_silu"], 1)
                nc.tensor.transpose(cp_[:, 0:B], c_silu, ident[0:B, 0:B]).then_inc(s["pr_mm"], 1)
                pe.wait_ge(s["w_first"], 16 * FIRST_LOADS)
                transposes(cx_, [wq[:, :], wk[:, :]])
                nc.tensor.transpose(av[:, 0:14], vec_rows, ident[0:14, 0:14]).then_inc(s["pr_mm"], 1)
                pe.wait_ge(s["pr_ev"], 1)
                for j, c in enumerate((1, 0, 4, 3)):
                    mm(score[1][:, B * j:B * j + B], wmod[:, D * c:D * c + D], sT, start=True, stop=True)
                for j, c in enumerate((2, 5)):
                    last = mm(score[1][0:B, 512 + D * j:512 + D * j + D], sT, wmod[:, D * c:D * c + D],
                              start=True, stop=True)
                last.then_inc(s["pr_mm"], 1)
                pe.wait_ge(s["pr_ev"], 2)
                mm(ca_[:, 0:1], wo[:, :], cols[:, BV:BV + 1], start=True, stop=True).then_inc(s["pr_mm"], 1)
                pe.wait_ge(s["pr_ev"], 4)
                mm(score[0][:, 0:64], wqT, blk, start=True, stop=True)
                mm(score[0][:, 64:128], wkT, blk, start=True, stop=True)
                mm(score[0][:, 128:192], bcasts, blk, start=True, stop=True)
                mm(score[0][:, 192:256], bcast1, blk, start=True, stop=True).then_inc(s["pr_mm"], 1)

            def rest_transposes():
                pe.wait_ge(s["w_rest"], 16 * REST_LOADS)
                transposes(cx_, [w1[:, P * c:P * c + P] for c in range(CH)]).then_inc(s["pr_mm"], 1)
                for c in range(CH):
                    last = nc.tensor.transpose(cp_[:, (NQ + 1) * c:(NQ + 1) * (c + 1)], wqo[:, P * c:P * c + P],
                                               ident[0:NQ + 1, 0:NQ + 1])
                last.then_inc(s["pr_mm"], 1)
                transposes(score[0][:, 512:1024], [wcon[:, P * c:P * c + P] for c in range(CH)])\
                    .then_inc(s["pr_mm"], 1)

            def rest_products():
                pe.wait_ge(s["pr_ev"], 7)
                for c in range(CH):
                    mm(av[:, 0:NQ], w1T[:, P * c:P * c + P], wm[:, c, :], start=c == 0, stop=c == CH - 1)
                for c in range(CH):
                    last = mm(av[:, NQ:2 * NQ], b1_cols[:, c, :], wm[:, c, :], start=c == 0, stop=c == CH - 1)
                last.then_inc(s["pr_mm"], 1)
                pe.wait_ge(s["pr_ev"], 8)
                for c in range(CH):
                    last = mm(score[1][0:NQ + 1, 0:D], wqoT[:, c, :], w2[:, D * c:D * c + D], start=c == 0, stop=c == CH - 1)
                last.then_inc(s["pr_mm"], 1)

            def folded():
                pe.wait_ge(s["bf_dn"], 4 * STAGES)
                transposes(cx_, [wcon_t[:, P * c:P * c + P] for c in range(CH)]).then_inc(s["pr_pe"], 1)
                pe.wait_ge(s["bf_b"], 4 * STAGES)
                for c in range(CH):
                    last = mm(cp_[:, 128 + c:129 + c], bexp[:, P * c:P * c + P], one[:, :], start=True, stop=True)
                last.then_inc(s["pr_pe"], 1)

            def chain_a(step, n, q):
                if step == "A_h":
                    if first(n):
                        pe.wait_ge(s["pr_bo"], 1)
                    pe.wait_ge(s["A_xh"], n + 1)
                    need(pe, s["kf_ready"], n)
                    transposes(ca_, [xh[:, t, :] for t in range(T)]).then_inc(s["A_tp"], 1)
                elif step == "A_qk":
                    pe.wait_ge(s["h_ready"], n + 1)
                    if first(n):
                        pe.wait_ge(s["pr_ev"], 6)
                    for t in range(T):
                        last = mm(ca_[:, P * t:P * t + P], h_F[q][:, P * t:P * t + P], wqk[:, :], start=True, stop=True)
                    last.then_inc(s["A_qkmm"], 1)
                elif step == "A_q":
                    pe.wait_ge(s["A_qk1"], n + 1)
                    mm(ca_[:, :], wq[:, :], h_F[q][:, :], start=True, stop=True).then_inc(s["A_qmm"], 1)
                elif step == "A_k":
                    pe.wait_ge(s["q_ready"], n + 1)
                    mm(ca_[:, :], wk[:, :], h_F[q][:, :], start=True, stop=True).then_inc(s["A_kmm"], 1)
                elif step == "A_v":
                    pe.wait_ge(s["k_ready"], n + 1)
                    for t in range(T):
                        last = mm(ca_[:, P * t:P * t + P], h_F[q][:, P * t:P * t + P], wv[:, :], start=True, stop=True)
                    last.then_inc(s["A_vmm"], 1)
                elif step in ("A_tq", "A_tk"):
                    side = step == "A_tk"
                    if side:
                        pe.wait_ge(s["qf_ready"], n + 1)
                    else:
                        pe.wait_ge(s["v_ready"], n + 1)
                        pe.wait_ge(s["A_lo"], n + 1)
                    for g in range(2):
                        for t in range(T):
                            at = H * t + 4 * g
                            last = nc.tensor.transpose(ca16[:, TOK * g + P * t:TOK * g + P * t + P],
                                                       parts[:, side, at:at + 4, :, :].rearrange("p h c q -> p (h c q)"),
                                                       ident16[:, :])
                    last.then_inc(s[step], 1)

            def chain_p(step, n, q):
                if step == "P_h3":
                    heads(n, q, 3)
                elif step in ("P_o0", "P_o1"):
                    b = step == "P_o1"
                    pe.wait_ge(s["o_ready"], PB * n + b + 1)
                    if b:
                        pe.wait_ge(s["P_at"], PB * n + 1)
                    else:
                        pe.wait_ge(s["P_yG"], n + 1)
                    for t in range(2):
                        for g in range(2):
                            last = nc.tensor.transpose(cp_[:, 256 * t + P * g:256 * t + P * g + P],
                                                       o_F[:, b, S * g + P * t:S * g + P * t + P], ident[:, :])
                    last.then_inc(s["P_tO"], 1)
                elif step == "P_at":
                    pe.wait_ge(s["P_at"], PB * n + 2)
                    transposes(cp_, [at_T[:, t, :] for t in range(T)]).then_inc(s["P_tat"], 1)
                elif step == "P_u":
                    pe.wait_ge(s["P_atF"], n + 1)
                    for t in range(T):
                        mm(cp_[:, P * t:P * t + P], at_F[:, P * t:P * t + P], wo[:, :], start=True, stop=False)
                        last = mm(cp_[:, P * t:P * t + P], hb_F[q][:, P * t:P * t + P], ident[:, :], start=False, stop=True)
                    last.then_inc(s["P_umm"], 1)
                elif step == "P_x1":
                    pe.wait_ge(s["P_xh1"], n + 1)
                    transposes(cp_, [xh1[:, t, :] for t in range(T)]).then_inc(s["P_tx1"], 1)
                elif step == "P_qm":
                    pe.wait_ge(s["P_x1F"], n + 1)
                    for t in range(T):
                        last = mm(cp_[:, NQ * t:NQ * t + NQ], x1_F[:, P * t:P * t + P], wfm[:, :], start=True, stop=True)
                    last.then_inc(s["P_qmm"], 1)
                elif step == "P_qe":
                    pe.wait_ge(s["P_qe"], n + 1)
                    for t in range(T):
                        last = nc.tensor.transpose(cp_[0:NQ + 1, P * t:P * t + P], qe[:, t, :], ident[:, :])
                    last.then_inc(s["P_tqe"], 1)
                elif step == "P_y":
                    pe.wait_ge(s["P_qeF"], n + 1)
                    for t in range(T):
                        mm(cp_[:, P * t:P * t + P], x1_F[:, P * t:P * t + P], ident[:, :], start=True, stop=False)
                        last = mm(cp_[:, P * t:P * t + P], qe_F[:, P * t:P * t + P], wq2[:, :], start=False, stop=True)
                    last.then_inc(s["P_ymm"], 1)
                elif step == "P_z":
                    pe.wait_ge(s["P_z"], n + 1)
                    transposes(cp_, [z[:, t, :] for t in range(T)]).then_inc(s["P_tz"], 1)
                elif step in ("P_f0", "P_f1", "P_f2", "P_f3"):
                    c = int(step[3])
                    if c == 0:
                        pe.wait_ge(s["P_h2"], n + 1)
                    if c >= 2:
                        pe.wait_ge(s["P_g"], CH * n + c - 1)
                    mm((cp_, cx_)[c % 2][:, :], wup[:, P * c:P * c + P], h2_F[:, :], start=True, stop=True)\
                        .then_inc(s["P_up"], 1)
                elif step == "P_out":
                    pe.wait_ge(s["P_g"], CH * n + CH)
                    for t in range(T):
                        for c in range(CH):
                            last = mm(cp_[:, P * t:P * t + P], g_F[:, c, P * t:P * t + P], wdn[:, c, :],
                                      start=c == 0, stop=c == CH - 1)
                    last.then_inc(s["P_y2"], 1)

            def norm_rows(n, m):
                pe.wait_ge(s["G_norm"], n - PAIRS + 1)
                if m:
                    pe.wait_ge(s["G_done"], TILES * (n - PAIRS) + m)
                for u in range(2):
                    for k in range(2):
                        c = H * (2 * (m // 4) + k) + 2 * (m % 4) + u
                        at = S * u + P * k
                        last = mm(cx_[:, at:at + P], norms[:, c:c + 1].broadcast_to([P, P]), ident[:, :],
                                  start=True, stop=True)
                last.then_inc(s["G_row"], 1)

            def shifts(n, q, m):
                b = m // 4
                if m == 0:
                    pe.wait_ge(s["G_done"], TILES * (n - PAIRS + 1))
                    pe.wait_ge(s["P_yG"], n + 1)
                for u in range(2):
                    h = 2 * (m % 4) + u
                    for k in range(2):
                        last = mm((cx_, cp_)[u][:, S * k:S * k + S], q_F[q][:, S * b + P * k:S * b + P * k + P],
                                  kpad[q][:, h, S * b:S * b + S], start=True, stop=True)
                last.then_inc(s["G_dots"], 1)
                pe.wait_ge(s["G_neg"], TILES * (n - PAIRS) + m + 1)

            def cosines(n, q, m):
                if m == 0:
                    pe.wait_ge(s["kfpad_in"], 64 * (n + 1))
                need(pe, s["tile_read"], 2 * TILES * n + m - 1)
                b = m // 4
                for u in range(2):
                    h = 2 * (m % 4) + u
                    for k in range(2):
                        last = mm(score[m % 2][:, 512 * u + S * k:512 * u + S * k + S],
                                  kfpad[q][:, h, S * b + P * k:S * b + P * k + P], qf[q][:, h // 4, S * b:S * b + S],
                                  start=True, stop=True)
                last.then_inc(s["fid_mm"], 1)

            def dots(n, q, m, general=False):
                if m == 0:
                    pe.wait_ge(s["kpad_in"], 128 * (n + 1))
                if general:
                    shifts(n, q, m)
                need(pe, s["tile_read"], 2 * TILES * n + TILES + m - 1)
                b = m // 4
                for u in range(2):
                    h = 2 * (m % 4) + u
                    for k in range(2):
                        at = 512 * u + S * k
                        keys = kpad[q][:, h, S * b + P * k:S * b + P * k + P]
                        if not general:
                            last = mm(score[m % 2][:, at:at + S], keys, q_F[q][:, S * b:S * b + S], start=True, stop=True)
                        else:
                            for i in range(2):
                                half = score[m % 2][:, at + P * i:at + P * i + P]
                                mm(half, keys, q_F[q][:, S * b + P * i:S * b + P * i + P], start=True, stop=False)
                                last = mm(half, top[:, 2 * u + i:2 * u + i + 1].broadcast_to([P, P]), ident[:, :],
                                          start=False, stop=True)
                last.then_inc(s["cw_mm"], 1)

            def heads(n, q, w):
                b, g = w // 2, w % 2
                pe.wait_ge(s["exp_done"], TILES * n + 2 * w + 2)
                if g == 0:
                    need(pe, s["o_ready"], PB * n + b)
                for k in range(2):
                    for j in range(4):
                        last = mm(av[32 * j:32 * j + 32, S * g:S * g + S], v_T[q][:, 2 * b + k, 4 * g + j, :],
                                  prob[:, 2 * w + j // 2, 512 * (j % 2) + S * k:512 * (j % 2) + S * k + S],
                                  start=k == 0, stop=k == 1, skip_group_check=True)
                last.then_inc(s["av_done"], 1)

            def body(n, q, prev, nxt, general=False):
                for k in range(2 * TILES):
                    if k < TILES:
                        if general:
                            norm_rows(n, k)
                        cosines(n, q, k)
                    else:
                        dots(n, q, k - TILES, general)
                    for step in PLAN["pe"][k].split():
                        if step[0] == "P" and prev:
                            chain_p(step, n - 1, 1 - q)
                        elif step[0] == "A" and nxt:
                            chain_a(step, n + 1, 1 - q)
                        elif step[0] == "H":
                            heads(n, q, int(step[1]))
                    if first(n) and k == FOLDED_AT:
                        folded()
                if first(n):
                    pe.wait_ge(s["pr_done"], 1)
                    pe.wait_ge(s["bf_up"], 4 * STAGES)

            first_products()
            for step in A_STEPS:
                if step == "A_q":
                    rest_transposes()
                if step == "A_tq":
                    rest_products()
                chain_a(step, 0, 0)
            pe.wait_ge(s["pr_ev"], 10)
            body(FIRST, 0, False, True)
            with pe.Fori(0, (PAIRS - 2) // 2) as i:
                body(2 * i + 1, 1, True, True)
                body(2 * i + 2, 0, True, True)
            body(PAIRS - 1, 1, True, False)
            for step in P_STEPS:
                chain_p(step, PAIRS - 1, 1)

            def general(n, q):
                for step in A_STEPS:
                    chain_a(step, n, q)
                body(n, q, False, False, True)
                for step in P_STEPS:
                    chain_p(step, n, q)

            pe.wait_ge(s["flag_sum"], 1)
            mm(av[0:1, 0:1], n_good[:, :], ones_col[:, :], start=True, stop=True).then_inc(s["flag_mm"], 1)
            general_pass(pe, general)

        @block.scalar
        def _(act):
            fn = nc.scalar.activation
            act.wait_ge(s["ones_ready"], 1)
            fn(kpad[0][:, :, :].rearrange("p h t -> p (h t)"), zero[:, :].broadcast_to([P, H * TOK]), ACT.Copy)\
                .then_inc(s["zeroed0"], 1)
            act.wait_ge(s["w_first"], 16 * FIRST_LOADS)
            fn(c_silu, c_sb, ACT.Silu).then_inc(s["pr_silu"], 1)
            fn(kpad[1][:, :, :].rearrange("p h t -> p (h t)"), zero[:, :].broadcast_to([P, H * TOK]), ACT.Copy)\
                .then_inc(s["zeroed1"], 1)

            def chain_a(step, n, q):
                if step == "A_h":
                    act.wait_ge(s["modA_in"], 16 * (n + 1))
                    act.wait_ge(s["A_tp"], n + 1)
                    for b in range(PB):
                        src = ca_[:, S * b:S * b + S]
                        fn(h_F[q][:, S * b:S * b + S], src, ACT.Identity, scale=modA[:, b, 0:1], bias=modA[:, b, 1:2])
                        last = fn(hb_F[q][:, S * b:S * b + S], src, ACT.Identity,
                                  scale=modA[:, b, 0:1], bias=modA[:, b, 2:3])
                    last.then_inc(s["h_ready"], 1)
                elif step == "A_q":
                    act.wait_ge(s["A_qmm"], n + 1)
                    fn(q_F[q][:, :], ca_[:, :], ACT.Identity, bias=cols[:, BQ:BQ + 1]).then_inc(s["q_ready"], 1)
                elif step == "A_k":
                    act.wait_ge(s["A_kmm"], n + 1)
                    need(act, s["kpad_in"], 128 * n)
                    fn(k_F[:, :], ca_[:, :], ACT.Identity, bias=cols[:, BK:BK + 1]).then_inc(s["k_ready"], 1)
                elif step == "A_v":
                    act.wait_ge(s["A_vmm"], n + 1)
                    fn(v_T[q][:, :, :, 0:HD], ca_[:, :].rearrange("p (t h d) -> p t h d", t=T, h=H), ACT.Copy)\
                        .then_inc(s["v_ready"], 1)
                elif step == "A_hi":
                    act.wait_ge(s["A_qn"], n + 1)
                    for side, slots in ((0, slice(0, 2)), (1, slice(0, 4, 2))):
                        last = fn(parts[:, side, :, slots, :],
                                  qn[:, side, :, :].unsqueeze(2).broadcast_to([P, T * H, 2, NQ]), ACT.Copy)
                    last.then_inc(s["A_hi"], 1)

            def evacuate(n, b):
                act.wait_ge(s["av_done"], 4 * n + 2 * b + 2)
                if b == 0:
                    need(act, s["P_tO"], PB * n)
                fn(o_F[:, b, :], av[:, :], ACT.Copy).then_inc(s["o_ready"], 1)

            def chain_p(step, n, q):
                if step == "P_e1":
                    evacuate(n, 1)
                elif step == "P_at":
                    act.wait_ge(s["P_tat"], n + 1)
                    fn(at_F[:, :], cp_[:, :], ACT.Copy).then_inc(s["P_atF"], 1)
                elif step == "P_x1":
                    act.wait_ge(s["P_tx1"], n + 1)
                    fn(x1_F[:, :], cp_[:, :], ACT.Identity, scale=cols[:, G1:G1 + 1], bias=cols[:, BETA1:BETA1 + 1])\
                        .then_inc(s["P_x1F"], 1)
                elif step == "P_sin":
                    act.wait_ge(s["P_r3"], n + 1)
                    fn(qm_sin[:, :], qm_r[:, :], ACT.Sin, scale=-2.0 * PI, bias=half_pi[:, :]).then_inc(s["P_sin"], 1)
                elif step == "P_tanh":
                    act.wait_ge(s["P_qm"], n + 1)
                    fn(qm_tanh[:, :], qm[:, :], ACT.Tanh).then_inc(s["P_tanh"], 1)
                elif step == "P_qe":
                    act.wait_ge(s["P_tqe"], n + 1)
                    fn(qe_F[:, :], cp_[0:NQ + 1, :], ACT.Copy).then_inc(s["P_qeF"], 1)
                elif step == "P_z":
                    act.wait_ge(s["modP_in"], 16 * (n + 1))
                    act.wait_ge(s["P_tz"], n + 1)
                    for b in range(PB):
                        last = fn(h2_F[:, S * b:S * b + S], cp_[:, S * b:S * b + S], ACT.Identity,
                                  scale=modP[:, b, 0:1], bias=modP[:, b, 1:2])
                    last.then_inc(s["P_h2"], 1)
                elif step in ("P_f0", "P_f1", "P_f2", "P_f3"):
                    c = int(step[3])
                    act.wait_ge(s["P_up"], CH * n + c + 1)
                    fn(g_F[:, c, :], (cp_, cx_)[c % 2][:, :], ACT.Gelu, bias=bup[:, c:c + 1]).then_inc(s["P_g"], 1)

            def body(n, q, prev, nxt, general=False):
                for k in range(2 * TILES):
                    m = k % TILES
                    if k < TILES:
                        if general:
                            act.wait_ge(s["G_done"], TILES * (n - PAIRS) + m + 1)
                        else:
                            act.wait_ge(s["fid_mm"], TILES * n + m + 1)
                        need(act, s["tile_read"], 2 * TILES * n + m - 1 if m >= 2 else 2 * TILES * (n - 1) + m + TILES - 1)
                        fn(sines[:, m % 2, :], score[m % 2][:, :], ACT.Sin, scale=SIN_SCALE).then_inc(s["sin_done"], 1)
                    else:
                        act.wait_ge(s["tile_read"], 2 * TILES * n + TILES + m + 1)
                        fn(prob[:, m, :], prob[:, m, :], ACT.Exp, scale=0.05).then_inc(s["exp_done"], 1)
                    for step in PLAN["act"][k].split():
                        if step[0] == "P" and prev:
                            chain_p(step, n - 1, 1 - q)
                        elif step[0] == "A" and nxt:
                            chain_a(step, n + 1, 1 - q)
                        elif step == "E0":
                            evacuate(n, 0)

            for step in A_STEPS:
                chain_a(step, 0, 0)
            body(FIRST, 0, False, True)
            with act.Fori(0, (PAIRS - 2) // 2) as i:
                body(2 * i + 1, 1, True, True)
                body(2 * i + 2, 0, True, True)
            body(PAIRS - 1, 1, True, False)
            for step in P_STEPS:
                chain_p(step, PAIRS - 1, 1)

            def general(n, q):
                for step in A_STEPS:
                    chain_a(step, n, q)
                body(n, q, False, False, True)
                for step in P_STEPS:
                    chain_p(step, n, q)

            general_pass(act, general)

        @block.vector
        def _(dve):
            v = nc.vector

            v.memset(zero[:, :], 0.0).then_inc(s["ones_ready"], 1)
            v.memset(half_pi[:, :], PI / 2)
            v.memset(one[:, :], 1.0)
            v.memset(ones_col[:, :], 1.0)
            v.memset(n2_least[:, :], 1.0)
            v.memset(l_least[:, :], 1.0)
            v.memset(l_total[:, :], 0.0)
            v.memset(qe[:, :, NQ:NQ + 1], 1.0)
            for i in range(2):
                v.memset(v_T[i][:, :, :, HD:32], 1.0).then_inc(s["ones_ready"], 1)

            def taken(n_mm):
                dve.wait_ge(s["pr_mm"], n_mm)

            def scalars():
                taken(1)
                v.tensor_copy(sT, cp_[:, 0:B]).then_inc(s["pr_ev"], 1)
                taken(2)
                v.tensor_copy(cols[:, :], av[:, 0:14]).then_inc(s["pr_ev"], 1)
                v.tensor_copy(x2[:, 1:3, :].rearrange("p a b -> p (a b)"), cx_[:, 0:256]).then_inc(s["pr_ev"], 1)
                dve.wait_ge(s["pr_ev"], 2)
                dve.wait_ge(s["w_mask"], 1)
                for dst, c in ((bcasts, BQ), (bcast1, BK)):
                    v.tensor_scalar(dst, ident[:, :], 0.0, cols[:, c:c + 1], ALU.mult, ALU.add)
                v.tensor_tensor(blk.rearrange("p (h q) -> p h q", h=H), wc2q[:, :].unsqueeze(1).broadcast_to([P, H, NQ]),
                                head_mask[:, :].unsqueeze(2).broadcast_to([P, H, NQ]), ALU.mult)\
                    .then_inc(s["pr_ev"], 1)
                taken(3)
                v.tensor_scalar(mod_cols[:, :, 0], score[1][:, 0:B], 1.0, None, ALU.add)
                v.tensor_copy(mod_cols[:, :, 4], score[1][:, 3 * B:4 * B])
                v.tensor_scalar(mod_cols[:, :, 3], score[1][:, 2 * B:3 * B], 1.0, None, ALU.add)
                v.tensor_copy(gate.rearrange("b r d -> b (r d)"), score[1][0:B, 512:768])
                v.tensor_copy(mod_cols[:, :, 1], score[1][:, B:2 * B]).then_inc(s["pr_ev"], 1)
                taken(4)
                v.tensor_tensor(rec[:, 0:1], ca_[:, 0:1], cols[:, BO:BO + 1], ALU.add).then_inc(s["pr_bo"], 1)
                dve.wait_ge(s["pr_ev"], 5)
                dve.wait_ge(s["pr_bo"], 1)
                v.tensor_scalar(mod_cols[:, :, 2], mod_cols[:, :, 1], rec[:, 0:1], None, ALU.add).then_inc(s["pr_mod"], 1)
                taken(5)
                v.tensor_copy(wqk[:, :], score[0][:, 0:P])
                v.tensor_tensor(bqk_row[:, :].rearrange("p (s c) -> p s c", s=2),
                                score[0][:, P:2 * P].rearrange("p (s c) -> p s c", s=2),
                                bc2q_row.unsqueeze(1).broadcast_to([P, 2, 64]), ALU.add).then_inc(s["pr_ev"], 1)

            def gates():
                dve.wait_ge(s["w_rest"], 16 * REST_LOADS)
                v.tensor_scalar(gate_s, gate, 0.0, 2.0, ALU.is_ge, ALU.mult)
                v.scalar_tensor_tensor(gate_rows[:, 0:2, :], gate, -1.0, gate, ALU.mult, ALU.max)
                v.tensor_tensor(vec16[:, 2, :], vec16[:, 2, :], vec16[:, 3, :], ALU.add).then_inc(s["pr_c"], 1)
                dve.wait_ge(s["pr_c"], 1)
                v.tensor_scalar(gate, gate_rows[:, 0:2, :], 0.25, None, ALU.max).then_inc(s["pr_c"], 1)
                dve.wait_ge(s["pr_c"], 2)
                v.scalar_tensor_tensor(gate_s, gate_s, -1.0, gate, ALU.add, ALU.mult).then_inc(s["pr_c"], 1)
                dve.wait_ge(s["pr_c"], 3)
                v.tensor_tensor(gate_rows[:, 0, :], gate_s[:, 0, :], vec16[:, 0, :], ALU.mult)
                v.tensor_tensor(gate_rows[:, 1, :], gate_s[:, 0, :], vec16[:, 1, :], ALU.mult)
                v.tensor_copy(gate_rows[:, 2, :], gate_s[:, 1, :])
                v.tensor_tensor(gate_rows[:, 3, :], gate_s[:, 1, :], vec16[:, 2, :], ALU.mult).then_inc(s["pr_rows"], 1)

            def rest_weights():
                for i in range(CH):
                    v.tensor_scalar(b1_cols[:, i, :], ident[:, :], 0.0, cols[:, B1 + i:B1 + i + 1], ALU.mult, ALU.add)
                taken(6)
                v.tensor_copy(w1T, cx_[:, :]).then_inc(s["pr_ev"], 1)
                taken(7)
                v.tensor_copy(wqoT.rearrange("p c q -> p (c q)"), cp_[:, 0:CH * (NQ + 1)]).then_inc(s["pr_ev"], 1)
                taken(8)
                v.tensor_copy(wcon_t, score[0][:, 512:1024]).then_inc(s["pr_ev"], 1)

            def products_out():
                taken(9)
                v.tensor_copy(wfm[:, :], av[:, 0:NQ])
                v.tensor_tensor(bfm_row[:, :], av[:, NQ:2 * NQ], bm_row, ALU.add)
                taken(10)
                dve.wait_ge(s["w_rest"], 16 * REST_LOADS)
                v.tensor_tensor(wq2[:, :], score[1][0:NQ + 1, 0:D], b2_rows, ALU.add).then_inc(s["pr_ev"], 1)
                dve.wait_ge(s["pr_ev"], 10)

            def stage(j):
                if j < BLOCK_STAGES:
                    b, b_prods, w = b_blocks, [x[:, :] for x in prod_blocks], b_w[j // 4][:, j % 4, :]
                else:
                    b, b_prods, w = bexp, prod_b, up_w[j % 3]
                    dve.wait_ge(s[f"up_in{j % 3}"], 16 * (j // 3 + 1))
                    dve.wait_ge(s["b_row"], 16 * CH)
                products(v, b, w, b_prods, False, j, s["bf_b"])
                dve.wait_ge(s[f"dn_in{j % 2}"], 16 * (j // 2 + 1))
                products(v, wcon_t, dn_w[j % 2], prod_dn, True, STAGES - 1 - j, s["bf_dn"])
                dve.wait_ge(s["bf_b"], 4 * j + 2)
                sums(v, b, b_prods, j, s["bf_b"])
                dve.wait_ge(s["bf_dn"], 4 * j + 2)
                sums(v, wcon_t, prod_dn, STAGES - 1 - j, s["bf_dn"])
                dve.wait_ge(s["bf_b"], 4 * j + 4)
                dve.wait_ge(s["bf_dn"], 4 * j + 4)

            def folded():
                dve.wait_ge(s["pr_pe"], 2)
                v.tensor_copy(wdn[:, :, :].rearrange("p c d -> p (c d)"), cx_[:, :])
                v.tensor_tensor(bup[:, :], cp_[:, 128:128 + CH], cols[:, UPB:UPB + CH], ALU.add).then_inc(s["pr_done"], 1)
                v.memset(one[:, :], 1.0).then_inc(s["P_yG"], 1)

            def stats(c, n, tiles, sem_sum, sem_agg, sem_var):
                for t in range(T):
                    last = v.bn_stats(stat[c][:, t, :], tiles[t])
                last.then_inc(s[sem_sum], 1)
                dve.wait_ge(s[sem_sum], n + 1)
                even, odd = stat[c][:, :, 1], stat[c][:, :, 4]
                v.tensor_tensor(agg[c][:, :, 1], even, odd, ALU.subtract)
                v.scalar_tensor_tensor(var[c][:, :], stat[c][:, :, 2], LN_EPS * D, stat[c][:, :, 5], ALU.add, ALU.add)
                v.tensor_tensor(agg[c][:, :, 0], even, odd, ALU.add).then_inc(s[sem_agg], 1)
                dve.wait_ge(s[sem_agg], 3 * n + 1)
                v.scalar_tensor_tensor(agg[c][:, :, 1], agg[c][:, :, 1], 0.25, agg[c][:, :, 1], ALU.mult, ALU.mult)\
                    .then_inc(s[sem_agg], 1)
                v.tensor_scalar(agg[c][:, :, 0], agg[c][:, :, 0], 0.5, None, ALU.mult).then_inc(s[sem_agg], 1)
                dve.wait_ge(s[sem_agg], 3 * n + 3)
                v.scalar_tensor_tensor(var[c][:, :], var[c][:, :], 1.0 / D, agg[c][:, :, 1], ALU.mult, ALU.add)\
                    .then_inc(s[sem_var], 1)

            def normalise(c, tiles, outs):
                for t in range(T):
                    last = v.tensor_scalar(outs[:, t, :], tiles[t], agg[c][:, t, 0:1], rstd[c][:, t:t + 1],
                                           ALU.subtract, ALU.mult)
                return last

            def tiles_of(x):
                return [x[:, P * t:P * t + P] for t in range(T)]

            def chain_a(step, n, q):
                if step == "A_stats":
                    dve.wait_ge(s["x_in"], 16 * (n + 1))
                    stats("A", n, [x_a[:, t, :] for t in range(T)], "A_sum", "A_agg", "A_var")
                elif step == "A_norm":
                    dve.wait_ge(s["A_rstd"], n + 1)
                    need(dve, s["A_tp"], n)
                    normalise("A", [x_a[:, t, :] for t in range(T)], xh).then_inc(s["A_xh"], 1)
                elif step == "A_qk":
                    dve.wait_ge(s["A_qkmm"], n + 1)
                    need(dve, s["A_qn"], n)
                    v.tensor_tensor(qk[:, :, :, :], ca_[:, :].rearrange("p (t s c) -> p s t c", t=T, s=2),
                                    bqk_row[:, :].rearrange("p (s c) -> p s c", s=2).unsqueeze(2)
                                    .broadcast_to([P, 2, T, 64]), ALU.add).then_inc(s["A_qk1"], 1)
                elif step == "A_n2":
                    dve.wait_ge(s["A_qk1"], n + 1)
                    flat = qk[:, :, :, :].rearrange("p s t c -> p (s t c)")
                    sqf = sq[:, :, :, :].rearrange("p s t c -> p (s t c)")
                    v.tensor_tensor(sqf, flat, flat, ALU.mult).then_inc(s["A_qk2"], 1)
                    dve.wait_ge(s["A_qk2"], n + 1)
                    v.tensor_reduce(n2[:, :], sqf.rearrange("p (a q) -> p a q", q=NQ), AX.X, ALU.add)\
                        .then_inc(s["A_n2"], 1)
                    dve.wait_ge(s["A_n2"], n + 1)
                    v.tensor_tensor(n2_least[:, :], n2_least[:, :], n2[:, :], ALU.min)
                    v.tensor_scalar(n2c[:, :], n2[:, :], TINY, None, ALU.max).then_inc(s["A_qk3"], 1)
                elif step == "A_lo":
                    dve.wait_ge(s["A_hi"], n + 1)
                    for side, lo, hi in ((0, slice(2, 4), slice(0, 1)), (1, slice(1, 4, 2), slice(0, 1))):
                        last = v.tensor_tensor(parts[:, side, :, lo, :],
                                               qn[:, side, :, :].unsqueeze(2).broadcast_to([P, T * H, 2, NQ]),
                                               parts[:, side, :, hi, :].broadcast_to([P, T * H, 2, NQ]), ALU.subtract)
                    last.then_inc(s["A_lo"], 1)
                elif step == "A_tq":
                    dve.wait_ge(s["A_tq"], n + 1)
                    v.tensor_copy(qf[q][:, :, :].rearrange("p g t -> p (g t)"), ca16).then_inc(s["qf_ready"], 1)
                elif step == "A_tk":
                    dve.wait_ge(s["A_tk"], n + 1)
                    need(dve, s["kfpad_in"], 64 * n)
                    v.tensor_copy(kf[:, :, :].rearrange("p g t -> p (g t)"), ca16).then_inc(s["kf_ready"], 1)

            def chain_p(step, n, q):
                if step in ("P_o0", "P_o1"):
                    b = int(step == "P_o1")
                    dve.wait_ge(s["P_tO"], PB * n + b + 1)
                    o = cp_[:, :].rearrange("p (a d) -> p a d", d=32)
                    v.tensor_tensor(l_least[:, :], l_least[:, :], o[:, :, HD], ALU.min)
                    v.tensor_tensor(l_total[:, :], l_total[:, :], o[:, :, HD], ALU.add)
                    v.reciprocal(rec[:, :], o[:, :, HD]).then_inc(s["P_rec"], 1)
                    dve.wait_ge(s["P_rec"], PB * n + b + 1)
                    v.tensor_tensor(at_T[:, 2 * b:2 * b + 2, :].rearrange("p t (h d) -> p (t h) d", h=H), o[:, :, 0:HD],
                                    rec[:, :].unsqueeze(2).broadcast_to([P, 2 * H, HD]), ALU.mult)\
                        .then_inc(s["P_at"], 1)
                elif step == "P_u":
                    dve.wait_ge(s["P_umm"], n + 1)
                    stats("1", n, tiles_of(cp_), "P_s1", "P_g1", "P_v1")
                elif step == "P_x1":
                    dve.wait_ge(s["P_r1"], n + 1)
                    normalise("1", tiles_of(cp_), xh1).then_inc(s["P_xh1"], 1)
                elif step == "P_qm":
                    dve.wait_ge(s["P_qmm"], n + 1)
                    v.tensor_tensor(qm[:, :].rearrange("p (t q) -> p t q", t=T),
                                    cp_[:, 0:T * NQ].rearrange("p (t q) -> p t q", t=T),
                                    bfm_row[:, :].unsqueeze(1).broadcast_to([P, T, NQ]), ALU.add).then_inc(s["P_qm"], 1)
                elif step == "P_rr":
                    dve.wait_ge(s["P_qm"], n + 1)
                    v.tensor_scalar(qm_n[:, :], qm[:, :], 0.125, ROUND, ALU.mult, ALU.add).then_inc(s["P_rr"], 1)
                    dve.wait_ge(s["P_rr"], 3 * n + 1)
                    v.tensor_scalar(qm_n[:, :], qm_n[:, :], -ROUND, None, ALU.add).then_inc(s["P_rr"], 1)
                    dve.wait_ge(s["P_rr"], 3 * n + 2)
                    v.scalar_tensor_tensor(qm_r[:, :], qm[:, :], 0.125, qm_n[:, :], ALU.mult, ALU.subtract)\
                        .then_inc(s["P_rr"], 1)
                    dve.wait_ge(s["P_rr"], 3 * n + 3)
                    v.scalar_tensor_tensor(qm_n[:, :], qm_r[:, :], -1.0, qm_r[:, :], ALU.mult, ALU.max)\
                        .then_inc(s["P_r2"], 1)
                    dve.wait_ge(s["P_r2"], n + 1)
                    v.tensor_scalar(qm_r[:, :], qm_n[:, :], 0.5, None, ALU.min).then_inc(s["P_r3"], 1)
                elif step == "P_tanh":
                    dve.wait_ge(s["P_sin"], n + 1)
                    dve.wait_ge(s["P_tanh"], n + 1)
                    v.tensor_tensor(qe[:, :, 0:NQ], qm_sin[:, :].rearrange("p (t q) -> p t q", t=T),
                                    qm_tanh[:, :].rearrange("p (t q) -> p t q", t=T), ALU.mult).then_inc(s["P_qe"], 1)
                elif step == "P_y":
                    dve.wait_ge(s["P_ymm"], n + 1)
                    stats("2", n, tiles_of(cp_), "P_s2", "P_g2", "P_v2")
                elif step == "P_v":
                    dve.wait_ge(s["P_r2d"], n + 1)
                    normalise("2", tiles_of(cp_), vv).then_inc(s["P_v"], 1)
                elif step == "P_x2":
                    dve.wait_ge(s["P_v"], n + 1)
                    dve.wait_ge(s["P_xB"], n + 1)
                    v.tensor_tensor(vv[:, :, :].rearrange("p (b t) d -> p b t d", b=PB),
                                    vv[:, :, :].rearrange("p (b t) d -> p b t d", b=PB),
                                    rows[q][:, :, 0:1, :].broadcast_to([P, PB, 2, D]), ALU.mult).then_inc(s["P_vG"], 1)
                    dve.wait_ge(s["P_vG"], n + 1)
                    v.tensor_tensor(x2[:, :, :], vv[:, :, :], xB[:, :, :], ALU.add).then_inc(s["P_x2"], 1)
                    dve.wait_ge(s["P_x2"], n + 1)
                    stats("3", n, [x2[:, t, :] for t in range(T)], "P_s3", "P_g3", "P_v3")
                elif step == "P_z":
                    dve.wait_ge(s["P_r3d"], n + 1)
                    normalise("3", [x2[:, t, :] for t in range(T)], z).then_inc(s["P_z"], 1)
                elif step == "P_out":
                    dve.wait_ge(s["P_y2"], n + 1)
                    dve.wait_ge(s["P_x2c"], n + 1)
                    dve.wait_ge(s["stored"], 16 * (n + 1))
                    v.tensor_tensor(o_T[:, :, :].rearrange("p (b t) d -> p b t d", b=PB),
                                    cp_[:, :].rearrange("p (b t d) -> p b t d", b=PB, t=2),
                                    rows[q][:, :, 2:3, :].broadcast_to([P, PB, 2, D]), ALU.mult).then_inc(s["P_yG"], 1)
                    dve.wait_ge(s["P_yG"], n + 2)
                    v.tensor_tensor(o_T[:, :, :], o_T[:, :, :], x2c[:, :, :], ALU.add).then_inc(s["P_out"], 1)

            def guard(n, m):
                dve.wait_ge(s["fid_mm"], TILES * n + m + 1)
                dve.wait_ge(s["G_row"], TILES * (n - PAIRS) + m + 1)
                for u in range(2):
                    for k in range(2):
                        c = 32 + H * (2 * (m // 4) + k) + 2 * (m % 4) + u
                        v.tensor_scalar(shrink[:, S * k:S * k + S], cx_[:, S * u:S * u + S],
                                        norms[:, c:c + 1], 1.0 / EPS_COS, ALU.mult, ALU.mult).then_inc(s["G_shrink"], 1)
                    dve.wait_ge(s["G_shrink"], 4 * (TILES * (n - PAIRS) + m) + 2 * u + 2)
                    tile = score[m % 2][:, 512 * u:512 * u + 512]
                    last = v.scalar_tensor_tensor(tile, shrink[:, :], 1.0, tile, ALU.min, ALU.mult)
                    last.then_inc(s["G_scaled"], 1)
                    dve.wait_ge(s["G_scaled"], 2 * (TILES * (n - PAIRS) + m) + u + 1)
                v.tensor_copy(top[:, 0:1], norms[:, 0:1]).then_inc(s["G_done"], 1)

            def maxima(n, m):
                dve.wait_ge(s["G_dots"], TILES * (n - PAIRS) + m + 1)
                for u in range(2):
                    last = v.tensor_reduce(shrink[:, 2 * u:2 * u + 2], (cx_, cp_)[u][:, :].rearrange("p (k t) -> p k t", k=2),
                                           AX.X, ALU.max)
                last.then_inc(s["G_max"], 1)
                dve.wait_ge(s["G_max"], TILES * (n - PAIRS) + m + 1)
                v.tensor_scalar(top[:, :], shrink[:, 0:4], -1.0, None, ALU.mult).then_inc(s["G_neg"], 1)

            def body(n, q, prev, nxt, general=False):
                if general:
                    v.tensor_tensor(norms[:, :], n2c[:, :], rn[:, :], ALU.mult).then_inc(s["G_norm"], 1)
                for k in range(2 * TILES):
                    m = k % TILES
                    if general and k < TILES:
                        guard(n, m)
                    if general and k >= TILES:
                        maxima(n, m)
                    if k < TILES:
                        dve.wait_ge(s["sin_done"], TILES * n + m + 1)
                        need(dve, s["av_done"], 4 * n)
                        v.scalar_tensor_tensor(prob[:, m, :], sines[:, m % 2, :], 10.0, score[m % 2][:, :],
                                               ALU.add, ALU.mult).then_inc(s["tile_read"], 1)
                    else:
                        dve.wait_ge(s["cw_mm"], TILES * n + m + 1)
                        v.scalar_tensor_tensor(prob[:, m, :], score[m % 2][:, :], 2.5, prob[:, m, :],
                                               ALU.mult, ALU.add).then_inc(s["tile_read"], 1)
                    for step in PLAN["dve"][k].split():
                        if step[0] == "P" and prev:
                            chain_p(step, n - 1, 1 - q)
                        elif step[0] == "A" and nxt:
                            chain_a(step, n + 1, 1 - q)
                    if first(n) and k in STAGE_AT:
                        stage(STAGE_AT[k])
                    if first(n) and k == FOLDED_AT:
                        folded()

            for step in A_STEPS:
                if step == "A_norm":
                    scalars()
                chain_a(step, 0, 0)
                if step == "A_n2":
                    rest_weights()
                    gates()
                    dve.wait_ge(s["pr_rows"], 1)
                    stage(0)
                    products_out()
                    stage(1)
                if step == "A_tk":
                    stage(2)
            body(FIRST, 0, False, True)
            with dve.Fori(0, (PAIRS - 2) // 2) as i:
                body(2 * i + 1, 1, True, True)
                body(2 * i + 2, 0, True, True)
            body(PAIRS - 1, 1, True, False)
            for step in P_STEPS:
                chain_p(step, PAIRS - 1, 1)

            def general(n, q):
                for step in A_STEPS:
                    chain_a(step, n, q)
                body(n, q, False, False, True)
                for step in P_STEPS:
                    chain_p(step, n, q)

            v.tensor_scalar(good[:, 0:64], n2_least[:, :], EPS_COS, None, ALU.is_ge)
            v.tensor_scalar(good[:, 64:80], l_least[:, :], SUM_LEAST, None, ALU.is_ge)
            v.tensor_scalar(good[:, 80:96], l_total[:, :], SUM_MOST, None, ALU.is_le).then_inc(s["flag_good"], 1)
            dve.wait_ge(s["flag_good"], 1)
            v.tensor_reduce(n_good[:, :], good[:, :], AX.X, ALU.add).then_inc(s["flag_sum"], 1)
            dve.wait_ge(s["flag_mm"], 1)
            v.tensor_scalar(flag[:, :], av[0:1, 0:1], 96.0 * P - 0.5, None, ALU.is_lt).then_inc(s["flag_ready"], 1)
            general_pass(dve, general)

        @block.gpsimd
        def _(pool):
            g = nc.gpsimd
            g.memset(ident[:, :], 0.0).then_inc(s["w_ident"], 1)
            g.memset(ident16[:, :], 0.0).then_inc(s["w_ident"], 1)
            g.memset(head_mask[:, :], 1.0).then_inc(s["w_ident"], 1)
            g.memset(neg_half[:, :], -0.5)
            pool.wait_ge(s["w_ident"], 3)
            for eye in (ident, ident16):
                g.affine_select(out=eye[:, :], in_=eye[:, :], compare_op=ALU.not_equal, fill=1.0,
                                base=0, pattern=[[-1, P]], channel_multiplier=1).then_inc(s["w_ident"], 1)
            g.affine_select(out=head_mask[:, :], in_=head_mask[:, :], compare_op=ALU.is_ge, fill=0.0,
                            base=0, pattern=[[-HD, H]], channel_multiplier=1).then_inc(s["w_ident"], 1)
            pool.wait_ge(s["w_ident"], 6)
            g.affine_select(out=head_mask[:, :], in_=head_mask[:, :], compare_op=ALU.is_ge, fill=0.0,
                            base=HD - 1, pattern=[[HD, H]], channel_multiplier=-1).then_inc(s["w_mask"], 1)
            g.memset(b2_rows, 0.0).then_inc(s["w_zero"], 1)

            def stage(j):
                pool.wait_ge(s[f"up_in{j % 3}"], 16 * (j // 3 + 1))
                products(g, wup[:, :], up_w[j % 3], prod_up, False, j, s["bf_up"])
                pool.wait_ge(s["bf_up"], 4 * j + 2)
                sums(g, wup[:, :], prod_up, j, s["bf_up"])
                pool.wait_ge(s["bf_up"], 4 * j + 4)

            def power(out_, in_, sem):
                g.tensor_tensor(out_, in_, neg_half[:, 0:in_.shape[1]], ALU.pow).then_inc(sem, 1)

            def chain_a(step, n, q):
                if step == "A_stats":
                    pool.wait_ge(s["A_var"], n + 1)
                    power(rstd["A"][:, :], var["A"][:, :], s["A_rstd"])
                elif step == "A_n2":
                    pool.wait_ge(s["A_qk3"], n + 1)
                    power(rn[:, :], n2c[:, :], s["A_rn"])
                elif step == "A_qn":
                    pool.wait_ge(s["A_rn"], n + 1)
                    need(pool, s["A_lo"], n)
                    g.tensor_tensor(qn[:, :, :, :].rearrange("p s a q -> p (s a) q"),
                                    qk[:, :, :, :].rearrange("p s t (h q) -> p (s t h) q", q=NQ),
                                    rn[:, :].unsqueeze(2).broadcast_to([P, 64, NQ]), ALU.mult).then_inc(s["A_qn"], 1)

            def chain_p(step, n, q):
                if step == "P_o1":
                    pool.wait_ge(s["xp_in"], 16 * (n + 1))
                    pool.wait_ge(s["rows_in"], 16 * (n + 1))
                    g.tensor_tensor(xB[:, :, :].rearrange("p (b t) d -> p b t d", b=PB),
                                    x_p[:, :, :].rearrange("p (b t) d -> p b t d", b=PB),
                                    rows[q][:, :, 1:2, :].broadcast_to([P, PB, 2, D]), ALU.add).then_inc(s["P_xB"], 1)
                elif step == "P_u":
                    pool.wait_ge(s["P_v1"], n + 1)
                    power(rstd["1"][:, :], var["1"][:, :], s["P_r1"])
                elif step == "P_y":
                    pool.wait_ge(s["P_v2"], n + 1)
                    power(rstd["2"][:, :], var["2"][:, :], s["P_r2d"])
                elif step == "P_x2":
                    pool.wait_ge(s["P_v3"], n + 1)
                    power(rstd["3"][:, :], var["3"][:, :], s["P_r3d"])
                elif step == "P_z":
                    g.tensor_tensor(x2c[:, :, :].rearrange("p (b t) d -> p b t d", b=PB),
                                    x2[:, :, :].rearrange("p (b t) d -> p b t d", b=PB),
                                    rows[q][:, :, 3:4, :].broadcast_to([P, PB, 2, D]), ALU.add).then_inc(s["P_x2c"], 1)

            def body(n, q, prev, nxt, general=False):
                for k in range(2 * TILES):
                    for step in PLAN["pool"][k].split():
                        if step[0] == "P" and prev:
                            chain_p(step, n - 1, 1 - q)
                        elif step[0] == "A" and nxt:
                            chain_a(step, n + 1, 1 - q)
                    if first(n) and k in STAGE_AT:
                        stage(STAGE_AT[k])

            pool.wait_ge(s["w_zero"], 1)
            for step in A_STEPS:
                chain_a(step, 0, 0)
                if step == "A_stats":
                    g.memset(kfpad[0][:, :, :], 0.0).then_inc(s["zeroed0"], 1)
                if step == "A_qn":
                    g.memset(kfpad[1][:, :, :], 0.0).then_inc(s["zeroed1"], 1)
                    pool.wait_ge(s["w_rest"], 16 * REST_LOADS)
                if step == "A_tk":
                    for j in range(EARLY_STAGES):
                        stage(j)
            body(FIRST, 0, False, True)
            with pool.Fori(0, (PAIRS - 2) // 2) as i:
                body(2 * i + 1, 1, True, True)
                body(2 * i + 2, 0, True, True)
            body(PAIRS - 1, 1, True, False)
            for step in P_STEPS:
                chain_p(step, PAIRS - 1, 1)

            def general(n, q):
                for step in A_STEPS:
                    chain_a(step, n, q)
                body(n, q, False, False, True)
                for step in P_STEPS:
                    chain_p(step, n, q)

            general_pass(pool, general)


_INS = ["L0_attn_x", "L0_attn_Wq", "L0_attn_bq", "L0_attn_Wk", "L0_attn_bk", "L0_attn_Wv", "L0_attn_bv",
        "L0_attn_Wc2q", "L0_attn_bc2q", "L0_attn_Wo", "L0_attn_bo", "L0_attn_g1", "L0_attn_beta1", "L0_attn_g2",
        "L0_attn_beta2", "L0_attn_W1", "L0_attn_b1", "L0_attn_Wm", "L0_attn_bm", "L0_attn_Wqo", "L0_attn_bqo",
        "L0_attn_W2", "L0_attn_b2", "L0_ffn_W_exp", "L0_ffn_b_exp", "L0_ffn_up_weights", "L0_ffn_up_bias",
        "L0_ffn_down_weights", "L0_ffn_W_con", "L0_ffn_b_con", "L0_ffn_down_bias", "L0_c", "L0_wmod"]


def kernel(**inputs):
    import concourse.bacc as bacc
    import numpy as np
    from concourse.bass_utils import run_bass_kernel_spmd

    nc = bacc.Bacc("TRN2", target_bir_lowering=False, num_devices=1)
    arrays, args = {}, {}
    for name in _INS:
        arrays[f"in_{name}"] = np.ascontiguousarray(inputs[name])
        args[name] = nc.dram_tensor(f"in_{name}", arrays[f"in_{name}"].shape,
                                    mybir.dt.from_np(arrays[f"in_{name}"].dtype), kind="ExternalInput").ap()
    out = nc.dram_tensor("out", (B, S, D), F32, kind="ExternalOutput").ap()
    build(nc, args, out)
    r = run_bass_kernel_spmd(nc, [arrays], core_ids=[0])
    return r.results[0]["out"]
```

```python
from contextlib import ExitStack

import concourse.bass as bass
from concourse import mybir

F32 = mybir.dt.float32
F16 = mybir.dt.float16
ALU = mybir.AluOpType
ACT = mybir.ActivationFunctionType
AX = mybir.AxisListType

P = 128
B, S, D = 16, 256, 128
H, HD, NQ = 8, 16, 8
FF = 512
PB = 2
PAIRS = B // PB
TOK = PB * S
T = TOK // P
CH = FF // P
STAGES = 9
BLOCK_STAGES = 7
TILES = PB * H // 2
LN_EPS = 1e-5
PI = 3.141592653589793
SIN_SCALE = PI * (1.0 - 2.0 ** -20)
TINY = 1e-36
EPS_COS = 1e-8
SUM_LEAST, SUM_MOST = 1e-20, 1e30
ROUND = 1.5 * 2.0 ** 23

A_STEPS = ("A_stats", "A_norm", "A_h", "A_qk", "A_n2", "A_q", "A_k", "A_v", "A_hk", "A_lk", "A_tk",
           "A_hq", "A_lq", "A_tq")
P_STEPS = ("P_h3", "P_e1", "P_o0", "P_o1", "P_at", "P_u", "P_x1", "P_qm", "P_rr", "P_sin", "P_tanh", "P_qe",
           "P_y", "P_v", "P_x2", "P_z")
T_STEPS = ("T_z", "T_f0", "T_f1", "T_f2", "T_f3", "T_out")
PLAN = {
    "pe": ["T_f2 T_f3 P_h3", "P_o0", "P_o1", "P_at", "P_u", "A_h A_qk P_x1", "A_q P_qm", "A_k", "T_out P_qe",
           "P_y A_v", "", "", "H0", "A_tk H1", "", "t_z", "A_tq t_f0 t_f1 H2"],
    "act": ["T_f2 T_f3", "P_e1", "", "P_at", "A_h", "P_x1", "A_q P_sin", "A_k", "P_tanh P_qe", "A_v", "A_hk",
            "", "", "A_hq", "", "E0 t_z", "t_f0 t_f1"],
    "dve": ["A_stats P_o0", "P_o1", "", "A_norm P_u", "P_x1", "A_qk A_n2", "P_qm P_rr", "P_tanh", "T_out",
            "P_y", "P_v", "", "A_lk P_x2", "A_tk P_z", "", "A_lq", "A_tq"],
    "pool": ["", "", "", "A_stats P_o1", "", "", "", "", "P_u A_n2", "", "P_y P_x2 P_z", "", "", "", "", "",
             ""],
    "sp": "next keys store prev mod amps",
}
LAST = {
    "pe": "T_f2 T_f3 P_h3/1 P_o0/0 P_o1/1 P_at/0 P_at/1 P_u/0 P_u/1 T_out P_x1/0 P_x1/1 P_qm/0 "
          "P_qm/1 P_qe/0 P_qe/1 P_y/0 P_y/1 T_z/0 T_z/1 T_f0/0 T_f0/1 T_f1/0 T_f1/1 T_f2/0 T_f2/1 "
          "T_f3/0 T_f3/1 T_out/0 T_out/1",
    "act": "T_f2 T_f3 P_e1/1 P_at/0 P_at/1 P_x1/0 P_x1/1 P_sin/0 P_sin/1 P_tanh/1 P_tanh/0 P_qe/0 "
           "P_qe/1 T_z/0 T_z/1 T_f0/0 T_f0/1 T_f1/0 T_f1/1 T_f2/0 T_f2/1 T_f3/0 T_f3/1",
    "dve": "P_o0/0 P_o1/1 P_u/0 P_u/1 P_x1/0 P_x1/1 T_out P_qm/0 P_rr/0 P_qm/1 P_rr/1 P_tanh/0 "
           "P_tanh/1 P_y/0 P_v/0 P_y/1 P_x2/0 P_v/1 P_x2/1 P_z/0 P_z/1 T_out/0 T_out/1",
    "pool": "P_o0/0 P_u/0 P_o1/1 P_u/1 P_y/0 P_y/1 P_x2/0 P_x2/1 P_z/0 P_z/1",
}
STAGE_SLOTS = "0 2 4 5 8 9 11"

SEMS = """
w_mod w_first w_rest w_zero w_ident w_mask ones_ready
x_in modA_in modP_in xp_in rows_in kpad_in kfpad_in stored
A_sum A_agg A_var A_rstd A_xh A_tp h_ready A_qkmm A_qk1 A_qk2 A_n2 A_qk3 A_rn A_qn A_qmm q_ready A_kmm k_ready
A_vmm v_ready A_hi A_lo A_tq A_tk qf_ready kf_ready
fid_mm sin_done tile_read cw_mm exp_done av_done o_ready
P_tO P_rec P_at P_tat P_atF P_umm P_s1 P_g1 P_v1 P_r1 P_xh1 P_tx1 P_x1F P_qmm P_qm P_rr P_sin P_tanh P_qe
P_tqe P_qeF P_ymm P_s2 P_g2 P_v2 P_r2d P_v P_vG P_xB P_x2 P_x2c P_s3 P_g3 P_v3 P_r3d P_z
T_z T_h2 T_up T_g T_y T_yG T_out
G_norm G_row G_shrink G_scaled G_done G_dots G_max G_neg flag_good flag_sum flag_mm flag_ready
pr_c pr_silu pr_mm pr_ev pr_bo pr_mod pr_rows pr_done pr_pe zeroed0 zeroed1
LP_tat LP_atF LP_umm LP_sum LP_agg LP_var LP_rstd LP_xh1 LP_tx1 LP_x1F LP_qmm LP_qm LP_rr LP_sin LP_tanh LP_qe
LP_tqe LP_qeF LP_ymm LP_v LP_xB LP_x2 LP_x2c LP_z L_stored LT_z LT_h2 LT_up LT_g LT_y LT_out
b_row up_in0 up_in1 up_in2 dn_in0 dn_in1 bf_up bf_b bf_dn
""".split()


def need(eng, sem, count):
    if not isinstance(count, int) or count > 0:
        eng.wait_ge(sem, count)


def build(nc, a, out):
    ctx = ExitStack()
    with ctx:
        def sb(name, shape, dt=F32):
            return ctx.enter_context(nc.sbuf_tensor(name, shape, dt))

        def pb(name, shape, dt=F32):
            return ctx.enter_context(nc.psum_tensor(name, shape, dt))

        s = {name: ctx.enter_context(nc.semaphore(name)) for name in SEMS}

        ident = sb("ident", [P, P])
        ident16 = sb("ident16", [P, P], F16)
        wq = sb("wq", [P, P])
        wk = sb("wk", [P, P])
        wv = sb("wv", [P, P])
        wo = sb("wo", [P, P])
        wqk = sb("wqk", [P, P])
        wfm = sb("wfm", [P, NQ])
        wq2 = sb("wq2", [NQ + 1, P])
        wup = sb("wup", [P, FF])
        wdn = sb("wdn", [P, CH, P])
        cols = sb("cols", [P, 14])
        bup = sb("bup", [P, CH])
        bqk_row = sb("bqk_row", [P, P])
        bfm_row = sb("bfm_row", [P, NQ])
        mod_cols = sb("mod_cols", [P, B, 5])
        half_pi = sb("half_pi", [P, 1])
        neg_half = sb("neg_half", [P, 64])
        BQ, BK, BV, BO, G1, BETA1, B1, UPB = 0, 1, 2, 3, 4, 5, 6, 10

        x_a = sb("x_a", [P, T, D])
        x_p = sb("x_p", [P, T, D])
        modA = sb("modA", [P, PB, 3])
        modP = sb("modP", [P, PB, 2])
        rows = [sb(f"rows{i}", [P, PB, 4, D]) for i in range(2)]
        xh = sb("xh", [P, T, D])
        h_F = [sb(f"h_F{i}", [P, TOK]) for i in range(2)]
        hb_F = [sb(f"hb_F{i}", [P, TOK]) for i in range(2)]
        q_F = [sb(f"q_F{i}", [P, TOK]) for i in range(2)]
        k_F = sb("k_F", [P, TOK])
        kpad = [sb(f"kpad{i}", [P, H, TOK]) for i in range(2)]
        v_T = [sb(f"v_T{i}", [P, T, H, 32]) for i in range(2)]
        qk = sb("qk", [P, 2, T, 64])
        sq = sb("sq", [P, 2, T, 64])
        n2 = sb("n2", [P, 64])
        n2c = sb("n2c", [P, 64])
        n2_least = sb("n2_least", [P, 64])
        l_least = sb("l_least", [P, 2 * H])
        l_total = sb("l_total", [P, 2 * H])
        good = sb("good", [P, 64 + 4 * H])
        n_good = sb("n_good", [P, 1])
        ones_col = sb("ones_col", [P, 1])
        flag = sb("flag", [1, 1], mybir.dt.int32)
        norms = sb("norms", [P, 64])
        shrink = sb("shrink", [P, 512])
        top = sb("top", [P, 4])
        rn = sb("rn", [P, 64])
        qn = sb("qn", [P, 2, T * H, NQ])
        parts = sb("parts", [P, 2, T * H, 4, NQ], F16)
        qf = [sb(f"qf{i}", [P, 2, TOK], F16) for i in range(2)]
        kf = sb("kf", [P, 2, TOK], F16)
        kfpad = [sb(f"kfpad{i}", [P, H, TOK], F16) for i in range(2)]
        stat = {c: sb(f"stat{c}", [P, T, 6]) for c in "A123"}
        agg = {c: sb(f"agg{c}", [P, T, 2]) for c in "A123"}
        var = {c: sb(f"var{c}", [P, T]) for c in "A123"}
        rstd = {c: sb(f"rstd{c}", [P, T]) for c in "A123"}
        sines = sb("sines", [P, 2, 1024])
        prob = sb("prob", [P, TILES, 1024])
        o_F = sb("o_F", [P, PB, TOK])
        rec = sb("rec", [P, 2 * H])
        at_T = sb("at_T", [P, T, D])
        at_F = sb("at_F", [P, TOK])
        xh1 = sb("xh1", [P, T, D])
        x1_F = sb("x1_F", [P, TOK])
        qm = sb("qm", [P, T * NQ])
        qm_n = sb("qm_n", [P, T * NQ])
        qm_r = sb("qm_r", [P, T * NQ])
        qm_sin = sb("qm_sin", [P, T * NQ])
        qm_tanh = sb("qm_tanh", [P, T * NQ])
        qe = sb("qe", [P, T, NQ + 1])
        qe_F = sb("qe_F", [NQ + 1, TOK])
        vv = sb("vv", [P, T, D])
        xB = sb("xB", [P, T, D])
        x2 = sb("x2", [P, T, D])
        x2c = sb("x2c", [P, T, D])
        z = sb("z", [P, T, D])
        h2_F = sb("h2_F", [P, TOK])
        g_F = sb("g_F", [P, CH, TOK])
        o_T = sb("o_T", [P, T, D])

        score = [pb(f"score{i}", [P, 1024]) for i in range(2)]
        av = pb("av", [P, 512])
        ca_ = pb("chainA", [P, 512])
        cp_ = pb("chainP", [P, 512])
        cx_ = pb("chainX", [P, 512])
        ca16 = ca_[:, :].bitcast(F16)

        rows_dram = nc.dram_tensor("gate_rows", [B, 4 * D], F32, kind="Internal").ap()

        ring = sb("ring", [P, 3, 1024])
        up_w = [ring[:, i, :] for i in range(3)]
        dn_w = [g_F[:, 2 * i:2 * i + 2, :].rearrange("p a b -> p (a b)") for i in range(2)]
        wmod = prob[:, 0, 0:6 * D]
        w1 = o_F[:, 0, :]
        w1T = o_F[:, 1, :]
        wcon = sines[:, 0, 0:512]
        wcon_t = x2[:, :, :].rearrange("p t d -> p (t d)")
        w2 = sines[:, 1, 0:512]
        prod_up = h2_F[:, :], at_T[:, :, :].rearrange("p t d -> p (t d)")
        b_blocks = at_F[0:CH, 0:P]
        bexp = x1_F[0:1, :]
        b_w = [rows[1][0:CH, :, :, :].rearrange("p b r (h w) -> p (b r h w)", h=1).rearrange("p (j w) -> p j w", j=4),
               sb("b_w", [CH, BLOCK_STAGES - 4, 2 * P])[:, :, :]]
        prod_blocks = [sb(f"prod_blocks{i}", [CH, P]) for i in range(2)]
        prod_dn = z[:, :, :].rearrange("p t d -> p (t d)"), xh1[:, :, :].rearrange("p t d -> p (t d)")
        prod_b = [o_T[0:1, :, :].rearrange("p t d -> p (t d)"), vv[0:1, :, :].rearrange("p t d -> p (t d)")]
        c_sb = xh1[0:B, 0, :]
        c_silu = xh1[0:B, 1, :]
        bcasts = xh1[:, 2, :]
        bcast1 = xh1[:, 3, :]
        sT = x2[:, 0, 0:B]
        wqT = x2[:, 1, :]
        wkT = x2[:, 2, :]
        blk = x2[:, 3, 0:64]
        bc2q_row = x2[:, 3, 64:128]
        wm = x2c[:, 0, 0:CH * NQ].rearrange("p (c q) -> p c q", c=CH)
        bm_row = x2c[:, 0, 64:64 + NQ]
        wqo = x1_F[0:NQ + 1, :]
        wqoT = x2c[:, 1, 0:CH * (NQ + 1)].rearrange("p (c q) -> p c q", c=CH)
        b2_rows = x2c[0:NQ + 1, 2, :]
        vec_rows = x2c[0:14, 3, :]
        gate = z[0:B, 0:2, :]
        gate_s = z[0:B, 2:4, :]
        gate_rows = xB[0:B, :, :]
        vec16 = vv[0:B, :, :]
        b1_cols = o_T[:, :, :]
        one = sb("one", [1, 1])
        spare = sb("spare", [P, 1])
        zero = sb("zero", [P, 1])
        idle = sb("idle", [P, 1])
        head_mask = sb("head_mask", [P, H])
        wc2q = sb("wc2q", [P, NQ])

        x_d = a["L0_attn_x"].rearrange("b s d -> (b s) d").rearrange("(n t p) d -> n p t d", t=T, p=P)
        out_d = out.rearrange("b s d -> (b s) d").rearrange("(n t p) d -> n p t d", t=T, p=P)

        block = ctx.enter_context(nc.Block())
        FIRST_LOADS, REST_LOADS = 14, 16
        EARLY_STAGES = 3
        *slots, FOLDED_AT = [int(k) for k in STAGE_SLOTS.split()]
        STAGE_AT = {k: EARLY_STAGES + i for i, k in enumerate(slots)}

        FIRST = 0

        def tiles_in(h):
            return range(T) if h is None else range(2 * h, 2 * h + 2)

        def batches(h):
            return range(PB) if h is None else range(h, h + 1)

        def tile_slice(h):
            return slice(0, T) if h is None else slice(2 * h, 2 * h + 2)

        def batch_slice(h):
            return slice(0, PB) if h is None else slice(h, h + 1)

        def toks(h):
            return slice(0, TOK) if h is None else slice(S * h, S * h + S)

        def amps(h):
            return slice(0, T * NQ) if h is None else slice(2 * NQ * h, 2 * NQ * h + 2 * NQ)

        def bank_p(h):
            return ca_ if h == 0 else cp_

        def bank_t(h):
            return cx_ if h is None else (ca_, cp_)[h]

        def bank_up(h, c, alone):
            if h is None:
                return cx_ if alone else (cx_, ca_)[c % 2]
            return ((ca_, cx_, score[0][:, 0:512], score[0][:, 512:1024]),
                    (cp_, av, score[1][:, 0:512], score[1][:, 512:1024]))[h][c]

        SHARED = {"P_vG": ("P_x2", 0), "P_x2": ("P_x2", 1), "T_yG": ("T_out", 0), "T_out": ("T_out", 1)}
        for i, rstd_of in enumerate(("P_r1", "P_r2d", "P_r3d")):
            SHARED |= {f"P_s{i + 1}": ("P_sum", i), f"P_g{i + 1}": ("P_agg", 3 * i), f"P_v{i + 1}": ("P_var", i),
                       rstd_of: ("P_rstd", i)}

        def sem(name, h):
            return s["L" + SHARED.get(name, (name,))[0]] if h == 0 else s[name]

        def due(name, count, h, of_first=1):
            return (sem(name, h), of_first + SHARED.get(name, (0, 0))[1]) if h == 0 else (s[name], count)

        def last_step(chain_p, chain_t, step):
            if "/" not in step:
                chain_t(step, PAIRS - 2, 0)
            else:
                step, h = step.split("/")
                (chain_t if step[0] == "T" else chain_p)(step, PAIRS - 1, 1, int(h))

        def first(n):
            return isinstance(n, int) and n == FIRST

        def pairs_of(x, st):
            return x.rearrange("p (n c j) -> p n c j", c=2, j=st)

        def products(op, y, w, prods, transposed, stage, step):
            st = 2 ** stage
            how = "p (n j c r) -> p r n c j" if transposed else "p (n j r c) -> p r n c j"
            wv_ = w[0:y.shape[0], :].rearrange(how, j=st, r=2, c=2)
            for r in range(2):
                op.tensor_tensor(pairs_of(prods[r], st), pairs_of(y, st), wv_[:, r], ALU.mult).then_inc(step, 1)

        def sums(op, y, prods, stage, step):
            st = 2 ** stage
            for r in range(2):
                pv = pairs_of(prods[r], st)
                op.tensor_tensor(pairs_of(y, st)[:, :, r, :], pv[:, :, 0, :], pv[:, :, 1, :], ALU.add).then_inc(step, 1)

        def general_pass(eng, pair, after=None):
            eng.wait_ge(s["flag_ready"], 1)
            unmet = eng.value_load(flag[0:1, 0:1], min_val=0, max_val=1)
            with eng.If(unmet > 0):
                with eng.Fori(0, PAIRS // 2) as i:
                    pair(2 * i + PAIRS, 0)
                    pair(2 * i + PAIRS + 1, 1)
                if after:
                    after()

        @block.sync
        def _(sp):
            def load(dst, src, sem="w_first"):
                sp.dma_start(dst, src).then_inc(s[sem], 16)

            def rest(dst, src):
                load(dst, src, "w_rest")

            def x_load(dst, sem, n, at):
                sp.dma_start(dst[:, :, :], x_d[at]).then_inc(s[sem], 16)

            x_load(x_a, "x_in", 0, 0)

            load(c_sb, a["L0_c"], "w_mod")
            load(wmod, a["L0_wmod"], "w_mod")
            for w, name in ((wq, "L0_attn_Wq"), (wk, "L0_attn_Wk")):
                load(w[:, :].rearrange("f (h d) -> f h d", h=H), a[name].rearrange("h f d -> f h d"))
            vecs = [("L0_attn_bq", "h d -> (h d)"), ("L0_attn_bk", "h d -> (h d)"), ("L0_attn_bv", "h d -> (h d)"),
                    ("L0_attn_bo", None), ("L0_attn_g1", None), ("L0_attn_beta1", None),
                    ("L0_attn_b1", None), ("L0_ffn_up_bias", None)]
            at = 0
            for name, how in vecs:
                v = a[name].rearrange(how) if how else a[name]
                v = v.rearrange("(r n) -> r n", n=P)
                load(vec_rows[at:at + v.shape[0], :], v)
                at += v.shape[0]
            assert at == 14
            load(wo[:, :], a["L0_attn_Wo"])
            load(wc2q[:, :], a["L0_attn_Wc2q"].rearrange("h d q -> (h d) q"))
            load(bc2q_row, a["L0_attn_bc2q"].rearrange("h q -> (h q)").partition_broadcast(P))
            load(wv[:, :].rearrange("f (h d) -> f h d", h=H), a["L0_attn_Wv"].rearrange("h f d -> f h d"))

            for j, name in enumerate(("L0_attn_g2", "L0_attn_beta2", "L0_ffn_b_con", "L0_ffn_down_bias")):
                rest(vec16[:, j, :], a[name].partition_broadcast(B))
            rest(w1, a["L0_attn_W1"])
            rest(wm, a["L0_attn_Wm"].rearrange("(c k) q -> k c q", c=CH))
            rest(wqo[0:NQ, :], a["L0_attn_Wqo"])
            rest(wqo[NQ:NQ + 1, :], a["L0_attn_bqo"].rearrange("(a n) -> a n", a=1))
            rest(w2.rearrange("k (c f) -> k c f", c=CH), a["L0_attn_W2"].rearrange("(c k) f -> k c f", c=CH))
            rest(wcon.rearrange("k (c f) -> k c f", c=CH), a["L0_ffn_W_con"].rearrange("(c k) f -> k c f", c=CH))
            rest(wup[:, :], a["L0_ffn_W_exp"])
            rest(b_blocks, a["L0_ffn_b_exp"].rearrange("(c n) -> c n", c=CH))
            for tile, stages_ in ((b_w[0], slice(0, 4)), (b_w[1], slice(4, BLOCK_STAGES))):
                rest(tile, a["L0_ffn_up_weights"][stages_].rearrange("j (c k) r i -> c j (k r i)", c=CH))
            rest(bm_row, a["L0_attn_bm"].partition_broadcast(P))
            sp.wait_ge(s["w_zero"], 1)
            rest(b2_rows[NQ:NQ + 1, :], a["L0_attn_b2"].rearrange("(a n) -> a n", a=1))

            def up_in(j):
                if j >= 3:
                    sp.wait_ge(s["bf_up"], 4 * (j - 2))
                    need(sp, s["bf_b"], 4 * (j - 2) if j - 3 >= BLOCK_STAGES else 0)
                sp.dma_start(up_w[j % 3], a["L0_ffn_up_weights"][j].rearrange("k r c -> (k r c)").partition_broadcast(P))\
                  .then_inc(s[f"up_in{j % 3}"], 16)

            def dn_in(j):
                if j >= 2:
                    sp.wait_ge(s["bf_dn"], 4 * (j - 1))
                src = a["L0_ffn_down_weights"][STAGES - 1 - j]
                sp.dma_start(dn_w[j % 2], src.rearrange("k r c -> (k r c)").partition_broadcast(P))\
                  .then_inc(s[f"dn_in{j % 2}"], 16)

            def next_in(n, base=0):
                need(sp, s["A_xh"], n)
                x_load(x_a, "x_in", n, n - base)
                mod_in(n, base)

            def mod_in(n, base=0):
                need(sp, s["h_ready"], n)
                sp.dma_start(modA[:, :, :], mod_cols[:, bass.ds(PB * (n - base), PB), 0:3]).then_inc(s["modA_in"], 16)

            def prev_in(n, q, base=0):
                need(sp, s["P_xB"], n)
                x_load(x_p, "xp_in", n, n - base)
                need(sp, s["T_yG"], n)
                sp.dma_start(rows[q][:, :, :, :].rearrange("p b r d -> p (b r d)"),
                             rows_dram[bass.ds(PB * (n - base), PB), :].partition_broadcast(P))\
                        .then_inc(s["rows_in"], 16)

            def modP_in(n, base=0):
                need(sp, s["T_h2"], n)
                sp.dma_start(modP[:, :, :], mod_cols[:, bass.ds(PB * (n - base), PB), 3:5]).then_inc(s["modP_in"], 16)

            def keys_out(n, q):
                sp.wait_ge(s["k_ready"], n + 1)
                for h in range(H):
                    sp.dma_start(kpad[q][HD * h:HD * h + HD, h, :], k_F[HD * h:HD * h + HD, :])\
                      .then_inc(s["kpad_in"], 16)

            def key_amps_out(n, q):
                sp.wait_ge(s["kf_ready"], n + 1)
                for j in range(4):
                    sp.dma_start(kfpad[q][32 * j:32 * j + 32, j:H:4, :], kf[32 * j:32 * j + 32, :, :])\
                      .then_inc(s["kfpad_in"], 16)

            def store(n, base=0):
                sp.wait_ge(s["T_out"], n + 1)
                sp.dma_start(out_d[n - base], o_T[:, :, :]).then_inc(s["stored"], 16)

            def body(n, q, prev, last, nxt):
                for step in PLAN["sp"].split():
                    if step == "next" and nxt:
                        next_in(n + 1)
                    elif step == "mod" and prev:
                        modP_in(n - 1)
                    elif step == "store" and last:
                        store(n - 2)
                    elif step == "prev":
                        prev_in(n, q)
                    elif step == "keys" and nxt:
                        keys_out(n + 1, 1 - q)
                    elif step == "amps" and nxt:
                        key_amps_out(n + 1, 1 - q)

            up_in(0)
            dn_in(0)
            sp.wait_ge(s["pr_mod"], 1)
            for j in (1, 2):
                up_in(j)
            dn_in(1)
            sp.wait_ge(s["zeroed0"], 2)
            keys_out(0, 0)
            next_in(1)
            sp.wait_ge(s["pr_rows"], 1)
            sp.dma_start(rows_dram, gate_rows.rearrange("b r d -> b (r d)")).then_inc(s["stored"], 16)
            up_in(3)
            dn_in(2)
            key_amps_out(0, 0)
            sp.wait_ge(s["stored"], 16)
            prev_in(0, 0)
            up_in(4)
            dn_in(3)
            for j in (5, 6, 7):
                dn_in(j - 1)
                up_in(j)
            sp.wait_ge(s["zeroed1"], 2)
            keys_out(1, 1)
            dn_in(7)
            up_in(8)
            sp.wait_ge(s["bf_b"], 4 * BLOCK_STAGES)
            for c in range(CH):
                sp.dma_start(bexp[:, P * c:P * c + P], b_blocks[c:c + 1, :]).then_inc(s["b_row"], 16)
            dn_in(8)
            key_amps_out(1, 1)
            sp.wait_ge(s["pr_done"], 1)
            body(1, 1, True, False, True)
            with sp.Fori(0, (PAIRS - 4) // 2) as i:
                body(2 * i + 2, 0, True, True, True)
                body(2 * i + 3, 1, True, True, True)
            body(PAIRS - 2, 0, True, True, True)
            body(PAIRS - 1, 1, True, True, False)
            store(PAIRS - 2)
            modP_in(PAIRS - 1)
            for h in range(PB):
                sp.wait_ge(*due("T_out", PAIRS, h))
                sp.dma_start(out_d[PAIRS - 1][:, tile_slice(h), :], o_T[:, tile_slice(h), :])\
                  .then_inc(s["stored"] if h else s["L_stored"], 16)
            sp.wait_ge(s["L_stored"], 16)
            sp.wait_ge(s["stored"], 16 * (PAIRS + 1))

            def general(n, q):
                next_in(n, PAIRS)
                keys_out(n, q)
                key_amps_out(n, q)
                prev_in(n, q, PAIRS)
                modP_in(n, PAIRS)
                store(n, PAIRS)

            general_pass(sp, general, lambda: sp.wait_ge(s["stored"], 16 * (2 * PAIRS + 1)))

        @block.tensor
        def _(pe):
            mm = nc.tensor.matmul

            def transposes(bank, tiles, eye=ident, first=0):
                for t, tile in enumerate(tiles, first):
                    last = nc.tensor.transpose(bank[:, P * t:P * t + P], tile, eye[:, :])
                return last

            def first_products():
                pe.wait_ge(s["w_ident"], 4)
                pe.wait_ge(s["pr_silu"], 1)
                nc.tensor.transpose(cp_[:, 0:B], c_silu, ident[0:B, 0:B]).then_inc(s["pr_mm"], 1)
                chain_a("A_h", 0, 0)
                pe.wait_ge(s["pr_ev"], 1)
                for j, c in enumerate((1, 0, 4, 3)):
                    mm(score[1][:, B * j:B * j + B], wmod[:, D * c:D * c + D], sT, start=True, stop=True)
                for j, c in enumerate((2, 5)):
                    last = mm(score[1][0:B, 512 + D * j:512 + D * j + D], sT, wmod[:, D * c:D * c + D],
                              start=True, stop=True)
                last.then_inc(s["pr_mm"], 1)
                pe.wait_ge(s["w_first"], 16 * FIRST_LOADS)
                transposes(cx_, [wq[:, :], wk[:, :]])
                nc.tensor.transpose(av[:, 0:14], vec_rows, ident[0:14, 0:14]).then_inc(s["pr_mm"], 1)
                pe.wait_ge(s["pr_ev"], 3)
                mm(score[0][:, 512:513], wo[:, :], cols[:, BV:BV + 1], start=True, stop=True)\
                        .then_inc(s["pr_mm"], 1)
                pe.wait_ge(s["pr_ev"], 5)
                mm(score[0][:, 0:64], wqT, blk, start=True, stop=True)
                mm(score[0][:, 64:128], wkT, blk, start=True, stop=True)
                mm(score[0][:, 128:192], bcasts, blk, start=True, stop=True)
                mm(score[0][:, 192:256], bcast1, blk, start=True, stop=True).then_inc(s["pr_mm"], 1)

            def rest_transposes():
                pe.wait_ge(s["w_rest"], 16 * REST_LOADS)
                transposes(cx_, [w1[:, P * c:P * c + P] for c in range(CH)]).then_inc(s["pr_mm"], 1)
                for c in range(CH):
                    last = nc.tensor.transpose(cp_[:, (NQ + 1) * c:(NQ + 1) * (c + 1)], wqo[:, P * c:P * c + P],
                                               ident[0:NQ + 1, 0:NQ + 1])
                last.then_inc(s["pr_mm"], 1)
                pe.wait_ge(s["pr_bo"], 1)
                transposes(score[0][:, 512:1024], [wcon[:, P * c:P * c + P] for c in range(CH)])\
                    .then_inc(s["pr_mm"], 1)

            def rest_products():
                pe.wait_ge(s["pr_ev"], 7)
                for c in range(CH):
                    mm(av[:, 0:NQ], w1T[:, P * c:P * c + P], wm[:, c, :], start=c == 0, stop=c == CH - 1)
                for c in range(CH):
                    last = mm(av[:, NQ:2 * NQ], b1_cols[:, c, :], wm[:, c, :], start=c == 0, stop=c == CH - 1)
                last.then_inc(s["pr_mm"], 1)
                pe.wait_ge(s["pr_ev"], 8)
                for c in range(CH):
                    last = mm(score[1][0:NQ + 1, 0:D], wqoT[:, c, :], w2[:, D * c:D * c + D], start=c == 0, stop=c == CH - 1)
                last.then_inc(s["pr_mm"], 1)

            def folded():
                pe.wait_ge(s["bf_dn"], 4 * STAGES)
                transposes(cx_, [wcon_t[:, P * c:P * c + P] for c in range(CH)]).then_inc(s["pr_pe"], 1)
                pe.wait_ge(s["bf_b"], 4 * STAGES)
                for c in range(CH):
                    last = mm(cp_[:, 128 + c:129 + c], bexp[:, P * c:P * c + P], one[:, :], start=True, stop=True)
                last.then_inc(s["pr_pe"], 1)

            def chain_a(step, n, q):
                if step == "A_h":
                    pe.wait_ge(s["A_xh"], n + 1)
                    need(pe, s["qf_ready"], n)
                    need(pe, s["T_g"], CH * (n - 2))
                    transposes(ca_, [xh[:, t, :] for t in range(T)]).then_inc(s["A_tp"], 1)
                elif step == "A_qk":
                    pe.wait_ge(s["h_ready"], n + 1)
                    if first(n):
                        pe.wait_ge(s["pr_ev"], 6)
                    for t in range(T):
                        last = mm(ca_[:, P * t:P * t + P], h_F[q][:, P * t:P * t + P], wqk[:, :], start=True, stop=True)
                    last.then_inc(s["A_qkmm"], 1)
                elif step == "A_q":
                    pe.wait_ge(s["A_qk1"], n + 1)
                    mm(ca_[:, :], wq[:, :], h_F[q][:, :], start=True, stop=True).then_inc(s["A_qmm"], 1)
                elif step == "A_k":
                    pe.wait_ge(s["q_ready"], n + 1)
                    mm(ca_[:, :], wk[:, :], h_F[q][:, :], start=True, stop=True).then_inc(s["A_kmm"], 1)
                elif step == "A_v":
                    pe.wait_ge(s["k_ready"], n + 1)
                    for t in range(T):
                        last = mm(ca_[:, P * t:P * t + P], h_F[q][:, P * t:P * t + P], wv[:, :], start=True, stop=True)
                    last.then_inc(s["A_vmm"], 1)
                elif step in ("A_tk", "A_tq"):
                    side = step == "A_tk"
                    pe.wait_ge(s["v_ready" if side else "kf_ready"], n + 1)
                    pe.wait_ge(s["A_lo"], 2 * n + 2 - side)
                    for g in range(2):
                        for t in range(T):
                            at = H * t + 4 * g
                            last = nc.tensor.transpose(ca16[:, TOK * g + P * t:TOK * g + P * t + P],
                                                       parts[:, side, at:at + 4, :, :].rearrange("p h c q -> p (h c q)"),
                                                       ident16[:, :])
                    last.then_inc(s[step], 1)

            def chain_p(step, n, q, h=None):
                bank = bank_p(h)
                if step == "P_h3":
                    heads(n, q, 3)
                elif step in ("P_o0", "P_o1"):
                    b = step == "P_o1"
                    pe.wait_ge(s["o_ready"], PB * n + b + 1)
                    if h == 0:
                        pe.wait_ge(s["T_g"], CH * n)
                    elif b and h is None:
                        pe.wait_ge(s["P_at"], PB * n + 1)
                    else:
                        need(pe, s["P_v"], n)
                    for t in range(2):
                        for g in range(2):
                            last = nc.tensor.transpose(bank[:, 256 * t + P * g:256 * t + P * g + P],
                                                       o_F[:, b, S * g + P * t:S * g + P * t + P], ident[:, :])
                    last.then_inc(s["P_tO"], 1)
                elif step == "P_at":
                    pe.wait_ge(s["P_at"], PB * n + (1 if h == 0 else 2))
                    transposes(bank, [at_T[:, t, :] for t in tiles_in(h)], first=tiles_in(h)[0])\
                        .then_inc(sem("P_tat", h), 1)
                elif step == "P_u":
                    pe.wait_ge(*due("P_atF", n + 1, h))
                    for t in tiles_in(h):
                        nc.tensor.transpose(bank[:, P * t:P * t + P], hb_F[q][:, P * t:P * t + P], ident[:, :])
                        last = mm(bank[:, P * t:P * t + P], at_F[:, P * t:P * t + P], wo[:, :], start=False, stop=True,
                                  skip_group_check=True)
                    last.then_inc(sem("P_umm", h), 1)
                elif step == "P_x1":
                    pe.wait_ge(*due("P_xh1", n + 1, h))
                    transposes(bank, [xh1[:, t, :] for t in tiles_in(h)], first=tiles_in(h)[0])\
                        .then_inc(sem("P_tx1", h), 1)
                elif step == "P_qm":
                    pe.wait_ge(*due("P_x1F", n + 1, h))
                    for t in tiles_in(h):
                        last = mm(bank[:, NQ * t:NQ * t + NQ], x1_F[:, P * t:P * t + P], wfm[:, :], start=True, stop=True)
                    last.then_inc(sem("P_qmm", h), 1)
                elif step == "P_qe":
                    pe.wait_ge(*due("P_qe", n + 1, h))
                    for t in tiles_in(h):
                        last = nc.tensor.transpose(bank[0:NQ + 1, P * t:P * t + P], qe[:, t, :], ident[:, :])
                    last.then_inc(sem("P_tqe", h), 1)
                elif step == "P_y":
                    pe.wait_ge(*due("P_qeF", n + 1, h))
                    for t in tiles_in(h):
                        nc.tensor.transpose(bank[:, P * t:P * t + P], x1_F[:, P * t:P * t + P], ident[:, :])
                        last = mm(bank[:, P * t:P * t + P], qe_F[:, P * t:P * t + P], wq2[:, :], start=False, stop=True,
                                  skip_group_check=True)
                    last.then_inc(sem("P_ymm", h), 1)

            def chain_t(step, n, q, h=None, alone=False):
                bank = bank_t(h)
                if step == "T_z":
                    pe.wait_ge(*due("P_z", n + 1, h))
                    if h != 1:
                        pe.wait_ge(s["T_yG"], n + 1)
                    transposes(bank, [z[:, t, :] for t in tiles_in(h)], first=tiles_in(h)[0]).then_inc(sem("T_z", h), 1)
                elif step == "T_out":
                    pe.wait_ge(*due("T_g", CH * n + CH, h, CH))
                    for t in tiles_in(h):
                        for c in range(CH):
                            last = mm(bank[:, P * t:P * t + P], g_F[:, c, P * t:P * t + P], wdn[:, c, :],
                                      start=c == 0, stop=c == CH - 1)
                    last.then_inc(sem("T_y", h), 1)
                else:
                    c = int(step[3])
                    if c == 0:
                        pe.wait_ge(*due("T_h2", n + 1, h))
                        if h == 0:
                            pe.wait_ge(s["tile_read"], 2 * TILES * PAIRS)
                    elif alone:
                        pe.wait_ge(s["T_g"], CH * n + c)
                    elif h is None and c == 1:
                        pe.wait_ge(s["qf_ready"], min(n + 3, PAIRS) if isinstance(n, int) else n + 3)
                    elif h is None:
                        pe.wait_ge(s["T_g"], CH * n + c - 1)
                    mm(bank_up(h, c, alone)[:, toks(h)], wup[:, P * c:P * c + P], h2_F[:, toks(h)], start=True, stop=True)\
                        .then_inc(sem("T_up", h), 1)

            def norm_rows(n, m):
                pe.wait_ge(s["G_norm"], n - PAIRS + 1)
                if m == 0:
                    pe.wait_ge(s["T_yG"], n + 1)
                if m:
                    pe.wait_ge(s["G_done"], TILES * (n - PAIRS) + m)
                for u in range(2):
                    for k in range(2):
                        c = H * (2 * (m // 4) + k) + 2 * (m % 4) + u
                        at = S * u + P * k
                        last = mm(cx_[:, at:at + P], norms[:, c:c + 1].broadcast_to([P, P]), ident[:, :],
                                  start=True, stop=True)
                last.then_inc(s["G_row"], 1)

            def shifts(n, q, m):
                b = m // 4
                if m == 0:
                    pe.wait_ge(s["G_done"], TILES * (n - PAIRS + 1))
                for u in range(2):
                    h = 2 * (m % 4) + u
                    for k in range(2):
                        last = mm((cx_, cp_)[u][:, S * k:S * k + S], q_F[q][:, S * b + P * k:S * b + P * k + P],
                                  kpad[q][:, h, S * b:S * b + S], start=True, stop=True)
                last.then_inc(s["G_dots"], 1)
                pe.wait_ge(s["G_neg"], TILES * (n - PAIRS) + m + 1)

            def cosines(n, q, m):
                if m == 0:
                    pe.wait_ge(s["kfpad_in"], 64 * (n + 1))
                    pe.wait_ge(s["qf_ready"], n + 1)
                need(pe, s["tile_read"], 2 * TILES * n + m - 1)
                b = m // 4
                for u in range(2):
                    h = 2 * (m % 4) + u
                    for k in range(2):
                        last = mm(score[m % 2][:, 512 * u + S * k:512 * u + S * k + S],
                                  kfpad[q][:, h, S * b + P * k:S * b + P * k + P], qf[q][:, h // 4, S * b:S * b + S],
                                  start=True, stop=True)
                last.then_inc(s["fid_mm"], 1)

            def dots(n, q, m, general=False):
                if m == 0:
                    pe.wait_ge(s["kpad_in"], 128 * (n + 1))
                if general:
                    shifts(n, q, m)
                need(pe, s["tile_read"], 2 * TILES * n + TILES + m - 1)
                b = m // 4
                for u in range(2):
                    h = 2 * (m % 4) + u
                    for k in range(2):
                        at = 512 * u + S * k
                        keys = kpad[q][:, h, S * b + P * k:S * b + P * k + P]
                        if not general:
                            last = mm(score[m % 2][:, at:at + S], keys, q_F[q][:, S * b:S * b + S], start=True, stop=True)
                        else:
                            for i in range(2):
                                half = score[m % 2][:, at + P * i:at + P * i + P]
                                mm(half, keys, q_F[q][:, S * b + P * i:S * b + P * i + P], start=True, stop=False)
                                last = mm(half, top[:, 2 * u + i:2 * u + i + 1].broadcast_to([P, P]), ident[:, :],
                                          start=False, stop=True)
                last.then_inc(s["cw_mm"], 1)

            def heads(n, q, w):
                b, g = w // 2, w % 2
                pe.wait_ge(s["exp_done"], TILES * n + 2 * w + 2)
                if g == 0:
                    need(pe, s["o_ready"], PB * n + b)
                for k in range(2):
                    for j in range(4):
                        last = mm(av[32 * j:32 * j + 32, S * g:S * g + S], v_T[q][:, 2 * b + k, 4 * g + j, :],
                                  prob[:, 2 * w + j // 2, 512 * (j % 2) + S * k:512 * (j % 2) + S * k + S],
                                  start=k == 0, stop=k == 1, skip_group_check=True)
                last.then_inc(s["av_done"], 1)

            def body(n, q, prev, last, nxt, general=False):
                def steps(k):
                    for step in PLAN["pe"][k].split():
                        if step[0] == "P" and prev:
                            chain_p(step, n - 1, 1 - q)
                        elif step[0] == "T" and last:
                            chain_t(step, n - 2, q)
                        elif step[0] == "t" and prev:
                            chain_t("T" + step[1:], n - 1, 1 - q)
                        elif step[0] == "A" and nxt:
                            chain_a(step, n + 1, 1 - q)
                        elif step[0] == "H":
                            heads(n, q, int(step[1]))

                steps(0)
                for k in range(2 * TILES):
                    if k < TILES:
                        if general:
                            norm_rows(n, k)
                        cosines(n, q, k)
                    else:
                        dots(n, q, k - TILES, general)
                    steps(k + 1)
                    if first(n) and k == FOLDED_AT:
                        folded()
                if first(n):
                    pe.wait_ge(s["pr_done"], 1)
                    pe.wait_ge(s["bf_up"], 4 * STAGES)

            first_products()
            for step in A_STEPS:
                if step == "A_q":
                    rest_transposes()
                if step == "A_tk":
                    rest_products()
                if step != "A_h":
                    chain_a(step, 0, 0)
            pe.wait_ge(s["pr_ev"], 10)
            body(FIRST, 0, False, False, True)
            body(1, 1, True, False, True)
            with pe.Fori(0, (PAIRS - 4) // 2) as i:
                body(2 * i + 2, 0, True, True, True)
                body(2 * i + 3, 1, True, True, True)
            body(PAIRS - 2, 0, True, True, True)
            body(PAIRS - 1, 1, True, True, False)
            for step in LAST["pe"].split():
                last_step(chain_p, chain_t, step)

            def general(n, q):
                for step in A_STEPS:
                    chain_a(step, n, q)
                body(n, q, False, False, False, True)
                for step in P_STEPS:
                    chain_p(step, n, q)
                for step in T_STEPS:
                    chain_t(step, n, q, alone=True)

            pe.wait_ge(s["flag_sum"], 1)
            mm(av[0:1, 0:1], n_good[:, :], ones_col[:, :], start=True, stop=True).then_inc(s["flag_mm"], 1)
            general_pass(pe, general)

        @block.scalar
        def _(act):
            fn = nc.scalar.activation
            act.wait_ge(s["ones_ready"], 1)
            fn(kpad[0][:, :, :].rearrange("p h t -> p (h t)"), zero[:, :].broadcast_to([P, H * TOK]), ACT.Copy)\
                .then_inc(s["zeroed0"], 1)
            act.wait_ge(s["w_mod"], 16 * 2)
            fn(c_silu, c_sb, ACT.Silu).then_inc(s["pr_silu"], 1)
            fn(kpad[1][:, :, :].rearrange("p h t -> p (h t)"), zero[:, :].broadcast_to([P, H * TOK]), ACT.Copy)\
                .then_inc(s["zeroed1"], 1)

            def chain_a(step, n, q):
                if step == "A_h":
                    if first(n):
                        act.wait_ge(s["pr_mod"], 1)
                    else:
                        act.wait_ge(s["modA_in"], 16 * n)
                    mod = mod_cols if first(n) else modA
                    act.wait_ge(s["A_tp"], n + 1)
                    for b in range(PB):
                        src = ca_[:, S * b:S * b + S]
                        fn(h_F[q][:, S * b:S * b + S], src, ACT.Identity, scale=mod[:, b, 0:1], bias=mod[:, b, 1:2])
                        last = fn(hb_F[q][:, S * b:S * b + S], src, ACT.Identity,
                                  scale=mod[:, b, 0:1], bias=mod[:, b, 2:3])
                    last.then_inc(s["h_ready"], 1)
                elif step == "A_q":
                    act.wait_ge(s["A_qmm"], n + 1)
                    fn(q_F[q][:, :], ca_[:, :], ACT.Identity, bias=cols[:, BQ:BQ + 1]).then_inc(s["q_ready"], 1)
                elif step == "A_k":
                    act.wait_ge(s["A_kmm"], n + 1)
                    need(act, s["kpad_in"], 128 * n)
                    fn(k_F[:, :], ca_[:, :], ACT.Identity, bias=cols[:, BK:BK + 1]).then_inc(s["k_ready"], 1)
                elif step == "A_v":
                    act.wait_ge(s["A_vmm"], n + 1)
                    fn(v_T[q][:, :, :, 0:HD], ca_[:, :].rearrange("p (t h d) -> p t h d", t=T, h=H), ACT.Copy)\
                        .then_inc(s["v_ready"], 1)
                elif step in ("A_hk", "A_hq"):
                    side = int(step == "A_hk")
                    act.wait_ge(s["A_qn"], 2 * n + 2 - side)
                    fn(parts[:, side, :, slice(0, 4, 2) if side else slice(0, 2), :],
                       qn[:, side, :, :].unsqueeze(2).broadcast_to([P, T * H, 2, NQ]), ACT.Copy).then_inc(s["A_hi"], 1)

            def evacuate(n, b):
                act.wait_ge(s["av_done"], 4 * n + 2 * b + 2)
                if b == 0:
                    need(act, s["P_tO"], PB * n)
                fn(o_F[:, b, :], av[:, :], ACT.Copy).then_inc(s["o_ready"], 1)

            def chain_p(step, n, q, h=None):
                if step == "P_e1":
                    evacuate(n, 1)
                elif step == "P_at":
                    act.wait_ge(*due("P_tat", n + 1, h))
                    fn(at_F[:, toks(h)], bank_p(h)[:, toks(h)], ACT.Copy).then_inc(sem("P_atF", h), 1)
                elif step == "P_x1":
                    act.wait_ge(*due("P_tx1", n + 1, h))
                    fn(x1_F[:, toks(h)], bank_p(h)[:, toks(h)], ACT.Identity,
                       scale=cols[:, G1:G1 + 1], bias=cols[:, BETA1:BETA1 + 1])\
                        .then_inc(sem("P_x1F", h), 1)
                elif step == "P_sin":
                    act.wait_ge(*due("P_rr", 5 * n + 5, h, 5))
                    fn(qm_sin[:, amps(h)], qm_r[:, amps(h)], ACT.Sin, scale=-2.0 * PI, bias=half_pi[:, :])\
                        .then_inc(sem("P_sin", h), 1)
                elif step == "P_tanh":
                    act.wait_ge(*due("P_qm", n + 1, h))
                    fn(qm_tanh[:, amps(h)], qm[:, amps(h)], ACT.Tanh).then_inc(sem("P_tanh", h), 1)
                elif step == "P_qe":
                    act.wait_ge(*due("P_tqe", n + 1, h))
                    fn(qe_F[:, toks(h)], bank_p(h)[0:NQ + 1, toks(h)], ACT.Copy).then_inc(sem("P_qeF", h), 1)

            def chain_t(step, n, q, h=None, alone=False):
                if step == "T_z":
                    act.wait_ge(s["modP_in"], 16 * (n + 1))
                    act.wait_ge(*due("T_z", n + 1, h))
                    for b in batches(h):
                        last = fn(h2_F[:, S * b:S * b + S], bank_t(h)[:, S * b:S * b + S], ACT.Identity,
                                  scale=modP[:, b, 0:1], bias=modP[:, b, 1:2])
                    last.then_inc(sem("T_h2", h), 1)
                elif step != "T_out":
                    c = int(step[3])
                    act.wait_ge(*due("T_up", CH * n + c + 1, h, c + 1))
                    fn(g_F[:, c, toks(h)], bank_up(h, c, alone)[:, toks(h)], ACT.Gelu, bias=bup[:, c:c + 1])\
                        .then_inc(sem("T_g", h), 1)

            def body(n, q, prev, last, nxt, general=False):
                def steps(k):
                    for step in PLAN["act"][k].split():
                        if step[0] == "P" and prev:
                            chain_p(step, n - 1, 1 - q)
                        elif step[0] == "T" and last:
                            chain_t(step, n - 2, q)
                        elif step[0] == "t" and prev:
                            chain_t("T" + step[1:], n - 1, 1 - q)
                        elif step[0] == "A" and nxt:
                            chain_a(step, n + 1, 1 - q)
                        elif step == "E0":
                            evacuate(n, 0)

                steps(0)
                fn(idle[:, :], zero[:, :], ACT.Silu)
                for k in range(2 * TILES):
                    m = k % TILES
                    if k < TILES:
                        if general:
                            act.wait_ge(s["G_done"], TILES * (n - PAIRS) + m + 1)
                        else:
                            act.wait_ge(s["fid_mm"], TILES * n + m + 1)
                        need(act, s["tile_read"],
                             2 * TILES * n + m - 1 if m >= 2 else 2 * TILES * (n - 1) + m + TILES - 1)
                        fn(sines[:, m % 2, :], score[m % 2][:, :], ACT.Sin, scale=SIN_SCALE).then_inc(s["sin_done"], 1)
                    else:
                        act.wait_ge(s["tile_read"], 2 * TILES * n + TILES + m + 1)
                        fn(prob[:, m, :], prob[:, m, :], ACT.Exp, scale=0.05).then_inc(s["exp_done"], 1)
                    steps(k + 1)

            for step in A_STEPS:
                chain_a(step, 0, 0)
            body(FIRST, 0, False, False, True)
            body(1, 1, True, False, True)
            with act.Fori(0, (PAIRS - 4) // 2) as i:
                body(2 * i + 2, 0, True, True, True)
                body(2 * i + 3, 1, True, True, True)
            body(PAIRS - 2, 0, True, True, True)
            body(PAIRS - 1, 1, True, True, False)
            for step in LAST["act"].split():
                if step == "P_x1/0":
                    fn(idle[:, :], zero[:, :], ACT.Silu)
                if step == "T_z/0":
                    fn(idle[:, :], zero[:, :], ACT.Gelu)
                last_step(chain_p, chain_t, step)

            def general(n, q):
                for step in A_STEPS:
                    chain_a(step, n, q)
                body(n, q, False, False, False, True)
                for step in P_STEPS:
                    chain_p(step, n, q)
                for step in T_STEPS:
                    chain_t(step, n, q, alone=True)

            general_pass(act, general)

        @block.vector
        def _(dve):
            v = nc.vector

            v.memset(zero[:, :], 0.0).then_inc(s["ones_ready"], 1)
            v.memset(half_pi[:, :], PI / 2)
            v.memset(one[:, :], 1.0)
            v.memset(ones_col[:, :], 1.0)
            v.memset(n2_least[:, :], 1.0)
            v.memset(l_least[:, :], 1.0)
            v.memset(l_total[:, :], 0.0)
            v.memset(qe[:, :, NQ:NQ + 1], 1.0)
            for i in range(2):
                v.memset(v_T[i][:, :, :, HD:32], 1.0).then_inc(s["ones_ready"], 1)

            def taken(n_mm):
                dve.wait_ge(s["pr_mm"], n_mm)

            def scalars():
                taken(1)
                v.tensor_copy(sT, cp_[:, 0:B]).then_inc(s["pr_ev"], 1)
                taken(2)
                v.tensor_scalar(mod_cols[:, :, 0], score[1][:, 0:B], 1.0, None, ALU.add)
                v.tensor_copy(mod_cols[:, :, 4], score[1][:, 3 * B:4 * B])
                v.tensor_scalar(mod_cols[:, :, 3], score[1][:, 2 * B:3 * B], 1.0, None, ALU.add)
                v.tensor_copy(gate.rearrange("b r d -> b (r d)"), score[1][0:B, 512:768])
                v.tensor_copy(mod_cols[:, :, 1], score[1][:, B:2 * B]).then_inc(s["pr_ev"], 1)
                taken(3)
                v.tensor_copy(cols[:, :], av[:, 0:14]).then_inc(s["pr_ev"], 1)
                v.tensor_copy(x2[:, 1:3, :].rearrange("p a b -> p (a b)"), cx_[:, 0:256]).then_inc(s["pr_ev"], 1)
                dve.wait_ge(s["pr_ev"], 3)
                dve.wait_ge(s["w_mask"], 1)
                for dst, c in ((bcasts, BQ), (bcast1, BK)):
                    v.tensor_scalar(dst, ident[:, :], 0.0, cols[:, c:c + 1], ALU.mult, ALU.add)
                v.tensor_tensor(blk.rearrange("p (h q) -> p h q", h=H), wc2q[:, :].unsqueeze(1).broadcast_to([P, H, NQ]),
                                head_mask[:, :].unsqueeze(2).broadcast_to([P, H, NQ]), ALU.mult)\
                    .then_inc(s["pr_ev"], 1)
                taken(4)
                v.tensor_tensor(rec[:, 0:1], score[0][:, 512:513], cols[:, BO:BO + 1], ALU.add).then_inc(s["pr_bo"], 1)
                dve.wait_ge(s["pr_bo"], 1)
                v.tensor_scalar(mod_cols[:, :, 2], mod_cols[:, :, 1], rec[:, 0:1], None, ALU.add)\
                        .then_inc(s["pr_mod"], 1)
                taken(5)
                v.tensor_copy(wqk[:, :], score[0][:, 0:P])
                v.tensor_tensor(bqk_row[:, :].rearrange("p (s c) -> p s c", s=2),
                                score[0][:, P:2 * P].rearrange("p (s c) -> p s c", s=2),
                                bc2q_row.unsqueeze(1).broadcast_to([P, 2, 64]), ALU.add).then_inc(s["pr_ev"], 1)

            def gates():
                dve.wait_ge(s["w_rest"], 16 * REST_LOADS)
                v.tensor_scalar(gate_s, gate, 0.0, 2.0, ALU.is_ge, ALU.mult)
                v.scalar_tensor_tensor(gate_rows[:, 0:2, :], gate, -1.0, gate, ALU.mult, ALU.max)
                v.tensor_tensor(vec16[:, 2, :], vec16[:, 2, :], vec16[:, 3, :], ALU.add).then_inc(s["pr_c"], 1)
                dve.wait_ge(s["pr_c"], 1)
                v.tensor_scalar(gate, gate_rows[:, 0:2, :], 0.25, None, ALU.max).then_inc(s["pr_c"], 1)
                dve.wait_ge(s["pr_c"], 2)
                v.scalar_tensor_tensor(gate_s, gate_s, -1.0, gate, ALU.add, ALU.mult).then_inc(s["pr_c"], 1)
                dve.wait_ge(s["pr_c"], 3)
                v.tensor_tensor(gate_rows[:, 0, :], gate_s[:, 0, :], vec16[:, 0, :], ALU.mult)
                v.tensor_tensor(gate_rows[:, 1, :], gate_s[:, 0, :], vec16[:, 1, :], ALU.mult)
                v.tensor_copy(gate_rows[:, 2, :], gate_s[:, 1, :])
                v.tensor_tensor(gate_rows[:, 3, :], gate_s[:, 1, :], vec16[:, 2, :], ALU.mult).then_inc(s["pr_rows"], 1)

            def rest_weights():
                for i in range(CH):
                    v.tensor_scalar(b1_cols[:, i, :], ident[:, :], 0.0, cols[:, B1 + i:B1 + i + 1], ALU.mult, ALU.add)
                taken(6)
                v.tensor_copy(w1T, cx_[:, :]).then_inc(s["pr_ev"], 1)
                taken(7)
                v.tensor_copy(wqoT.rearrange("p c q -> p (c q)"), cp_[:, 0:CH * (NQ + 1)]).then_inc(s["pr_ev"], 1)
                taken(8)
                v.tensor_copy(wcon_t, score[0][:, 512:1024]).then_inc(s["pr_ev"], 1)

            def products_out():
                taken(9)
                v.tensor_copy(wfm[:, :], av[:, 0:NQ])
                v.tensor_tensor(bfm_row[:, :], av[:, NQ:2 * NQ], bm_row, ALU.add)
                taken(10)
                dve.wait_ge(s["w_rest"], 16 * REST_LOADS)
                v.tensor_tensor(wq2[:, :], score[1][0:NQ + 1, 0:D], b2_rows, ALU.add).then_inc(s["pr_ev"], 1)
                dve.wait_ge(s["pr_ev"], 10)

            def stage(j):
                dve.wait_ge(s[f"dn_in{j % 2}"], 16 * (j // 2 + 1))
                products(v, wcon_t, dn_w[j % 2], prod_dn, True, STAGES - 1 - j, s["bf_dn"])
                if j < BLOCK_STAGES:
                    b, b_prods, w = b_blocks, [x[:, :] for x in prod_blocks], b_w[j // 4][:, j % 4, :]
                else:
                    b, b_prods, w = bexp, prod_b, up_w[j % 3]
                    dve.wait_ge(s[f"up_in{j % 3}"], 16 * (j // 3 + 1))
                    dve.wait_ge(s["b_row"], 16 * CH)
                products(v, b, w, b_prods, False, j, s["bf_b"])
                dve.wait_ge(s["bf_dn"], 4 * j + 2)
                sums(v, wcon_t, prod_dn, STAGES - 1 - j, s["bf_dn"])
                dve.wait_ge(s["bf_b"], 4 * j + 2)
                sums(v, b, b_prods, j, s["bf_b"])
                dve.wait_ge(s["bf_dn"], 4 * j + 4)
                dve.wait_ge(s["bf_b"], 4 * j + 4)

            def folded():
                dve.wait_ge(s["pr_pe"], 2)
                v.tensor_copy(wdn[:, :, :].rearrange("p c d -> p (c d)"), cx_[:, :])
                v.tensor_tensor(bup[:, :], cp_[:, 128:128 + CH], cols[:, UPB:UPB + CH], ALU.add)\
                        .then_inc(s["pr_done"], 1)
                v.memset(spare[:, :], 1.0).then_inc(s["T_yG"], 1)

            def stats(c, n, tiles, sem_sum, sem_agg, sem_var, h=None):
                ts = tile_slice(h)
                for t in tiles_in(h):
                    last = v.bn_stats(stat[c][:, t, :], tiles[t])
                last.then_inc(sem(sem_sum, h), 1)
                dve.wait_ge(*due(sem_sum, n + 1, h))
                even, odd = stat[c][:, ts, 1], stat[c][:, ts, 4]
                mean, square = agg[c][:, ts, 0], agg[c][:, ts, 1]
                v.tensor_tensor(square, even, odd, ALU.subtract)
                v.scalar_tensor_tensor(var[c][:, ts], stat[c][:, ts, 2], LN_EPS * D, stat[c][:, ts, 5], ALU.add, ALU.add)
                v.tensor_tensor(mean, even, odd, ALU.add).then_inc(sem(sem_agg, h), 1)
                dve.wait_ge(*due(sem_agg, 3 * n + 1, h, 1))
                v.scalar_tensor_tensor(square, square, 0.25, square, ALU.mult, ALU.mult).then_inc(sem(sem_agg, h), 1)
                v.tensor_scalar(mean, mean, 0.5, None, ALU.mult).then_inc(sem(sem_agg, h), 1)
                dve.wait_ge(*due(sem_agg, 3 * n + 3, h, 3))
                v.scalar_tensor_tensor(var[c][:, ts], var[c][:, ts], 1.0 / D, square, ALU.mult, ALU.add)\
                    .then_inc(sem(sem_var, h), 1)

            def normalise(c, tiles, outs, h=None):
                for t in tiles_in(h):
                    last = v.tensor_scalar(outs[:, t, :], tiles[t], agg[c][:, t, 0:1], rstd[c][:, t:t + 1],
                                           ALU.subtract, ALU.mult)
                return last

            def tiles_of(x):
                return [x[:, P * t:P * t + P] for t in range(T)]

            def chain_a(step, n, q):
                if step == "A_stats":
                    dve.wait_ge(s["x_in"], 16 * (n + 1))
                    stats("A", n, [x_a[:, t, :] for t in range(T)], "A_sum", "A_agg", "A_var")
                elif step == "A_norm":
                    dve.wait_ge(s["A_rstd"], n + 1)
                    need(dve, s["A_tp"], n)
                    normalise("A", [x_a[:, t, :] for t in range(T)], xh).then_inc(s["A_xh"], 1)
                elif step == "A_qk":
                    dve.wait_ge(s["A_qkmm"], n + 1)
                    need(dve, s["A_qn"], 2 * n)
                    v.tensor_tensor(qk[:, :, :, :], ca_[:, :].rearrange("p (t s c) -> p s t c", t=T, s=2),
                                    bqk_row[:, :].rearrange("p (s c) -> p s c", s=2).unsqueeze(2)
                                    .broadcast_to([P, 2, T, 64]), ALU.add).then_inc(s["A_qk1"], 1)
                elif step == "A_n2":
                    dve.wait_ge(s["A_qk1"], n + 1)
                    flat = qk[:, :, :, :].rearrange("p s t c -> p (s t c)")
                    sqf = sq[:, :, :, :].rearrange("p s t c -> p (s t c)")
                    v.tensor_tensor(sqf, flat, flat, ALU.mult).then_inc(s["A_qk2"], 1)
                    dve.wait_ge(s["A_qk2"], n + 1)
                    v.tensor_reduce(n2[:, :], sqf.rearrange("p (a q) -> p a q", q=NQ), AX.X, ALU.add)\
                        .then_inc(s["A_n2"], 1)
                    dve.wait_ge(s["A_n2"], n + 1)
                    v.tensor_tensor(n2_least[:, :], n2_least[:, :], n2[:, :], ALU.min)
                    v.tensor_scalar(n2c[:, :], n2[:, :], TINY, None, ALU.max).then_inc(s["A_qk3"], 1)
                elif step in ("A_lk", "A_lq"):
                    side = int(step == "A_lk")
                    dve.wait_ge(s["A_hi"], 2 * n + 2 - side)
                    v.tensor_tensor(parts[:, side, :, slice(1, 4, 2) if side else slice(2, 4), :],
                                    qn[:, side, :, :].unsqueeze(2).broadcast_to([P, T * H, 2, NQ]),
                                    parts[:, side, :, 0:1, :].broadcast_to([P, T * H, 2, NQ]), ALU.subtract)\
                        .then_inc(s["A_lo"], 1)
                elif step == "A_tq":
                    dve.wait_ge(s["A_tq"], n + 1)
                    v.tensor_copy(qf[q][:, :, :].rearrange("p g t -> p (g t)"), ca16).then_inc(s["qf_ready"], 1)
                elif step == "A_tk":
                    dve.wait_ge(s["A_tk"], n + 1)
                    need(dve, s["kfpad_in"], 64 * n)
                    v.tensor_copy(kf[:, :, :].rearrange("p g t -> p (g t)"), ca16).then_inc(s["kf_ready"], 1)

            def chain_p(step, n, q, h=None):
                bank, ts, bs, am = bank_p(h), tile_slice(h), batch_slice(h), amps(h)
                if step in ("P_o0", "P_o1"):
                    b = int(step == "P_o1")
                    dve.wait_ge(s["P_tO"], PB * n + b + 1)
                    if h == 1:
                        dve.wait_ge(s["P_at"], PB * n + 1)
                    o = bank[:, :].rearrange("p (a d) -> p a d", d=32)
                    v.tensor_tensor(l_least[:, :], l_least[:, :], o[:, :, HD], ALU.min)
                    v.tensor_tensor(l_total[:, :], l_total[:, :], o[:, :, HD], ALU.add)
                    v.reciprocal(rec[:, :], o[:, :, HD]).then_inc(s["P_rec"], 1)
                    dve.wait_ge(s["P_rec"], PB * n + b + 1)
                    v.tensor_tensor(at_T[:, 2 * b:2 * b + 2, :].rearrange("p t (h d) -> p (t h) d", h=H), o[:, :, 0:HD],
                                    rec[:, :].unsqueeze(2).broadcast_to([P, 2 * H, HD]), ALU.mult)\
                        .then_inc(s["P_at"], 1)
                elif step == "P_u":
                    dve.wait_ge(*due("P_umm", n + 1, h))
                    stats("1", n, tiles_of(bank), "P_s1", "P_g1", "P_v1", h)
                elif step == "P_x1":
                    dve.wait_ge(*due("P_r1", n + 1, h))
                    normalise("1", tiles_of(bank), xh1, h).then_inc(sem("P_xh1", h), 1)
                elif step == "P_qm":
                    dve.wait_ge(*due("P_qmm", n + 1, h))
                    v.tensor_tensor(qm[:, am].rearrange("p (t q) -> p t q", q=NQ),
                                    bank[:, am].rearrange("p (t q) -> p t q", q=NQ),
                                    bfm_row[:, :].unsqueeze(1).broadcast_to([P, len(tiles_in(h)), NQ]), ALU.add)\
                        .then_inc(sem("P_qm", h), 1)
                elif step == "P_rr":
                    dve.wait_ge(*due("P_qm", n + 1, h))
                    v.tensor_scalar(qm_n[:, am], qm[:, am], 0.125, ROUND, ALU.mult, ALU.add).then_inc(sem("P_rr", h), 1)
                    dve.wait_ge(*due("P_rr", 5 * n + 1, h))
                    v.tensor_scalar(qm_n[:, am], qm_n[:, am], -ROUND, None, ALU.add).then_inc(sem("P_rr", h), 1)
                    dve.wait_ge(*due("P_rr", 5 * n + 2, h, 2))
                    v.scalar_tensor_tensor(qm_r[:, am], qm[:, am], 0.125, qm_n[:, am], ALU.mult, ALU.subtract)\
                        .then_inc(sem("P_rr", h), 1)
                    dve.wait_ge(*due("P_rr", 5 * n + 3, h, 3))
                    v.scalar_tensor_tensor(qm_n[:, am], qm_r[:, am], -1.0, qm_r[:, am], ALU.mult, ALU.max)\
                        .then_inc(sem("P_rr", h), 1)
                    dve.wait_ge(*due("P_rr", 5 * n + 4, h, 4))
                    v.tensor_scalar(qm_r[:, am], qm_n[:, am], 0.5, None, ALU.min).then_inc(sem("P_rr", h), 1)
                elif step == "P_tanh":
                    dve.wait_ge(*due("P_sin", n + 1, h))
                    dve.wait_ge(*due("P_tanh", n + 1, h))
                    v.tensor_tensor(qe[:, ts, 0:NQ], qm_sin[:, am].rearrange("p (t q) -> p t q", q=NQ),
                                    qm_tanh[:, am].rearrange("p (t q) -> p t q", q=NQ), ALU.mult)\
                        .then_inc(sem("P_qe", h), 1)
                elif step == "P_y":
                    dve.wait_ge(*due("P_ymm", n + 1, h))
                    stats("2", n, tiles_of(bank), "P_s2", "P_g2", "P_v2", h)
                elif step == "P_v":
                    dve.wait_ge(*due("P_r2d", n + 1, h))
                    normalise("2", tiles_of(bank), vv, h).then_inc(sem("P_v", h), 1)
                elif step == "P_x2":
                    dve.wait_ge(*due("P_v", n + 1, h))
                    dve.wait_ge(*due("P_xB", n + 1, h))
                    v.tensor_tensor(vv[:, ts, :].rearrange("p (b t) d -> p b t d", t=2),
                                    vv[:, ts, :].rearrange("p (b t) d -> p b t d", t=2),
                                    rows[q][:, bs, 0:1, :].broadcast_to([P, len(batches(h)), 2, D]), ALU.mult)\
                        .then_inc(sem("P_vG", h), 1)
                    dve.wait_ge(*due("P_vG", n + 1, h))
                    need(dve, s["P_x2c"], n)
                    v.tensor_tensor(x2[:, ts, :], vv[:, ts, :], xB[:, ts, :], ALU.add).then_inc(sem("P_x2", h), 1)
                    dve.wait_ge(*due("P_x2", n + 1, h))
                    stats("3", n, [x2[:, t, :] for t in range(T)], "P_s3", "P_g3", "P_v3", h)
                elif step == "P_z":
                    dve.wait_ge(*due("P_r3d", n + 1, h))
                    need(dve, s["T_z"], n)
                    normalise("3", [x2[:, t, :] for t in range(T)], z, h).then_inc(sem("P_z", h), 1)

            def chain_t(step, n, q, h=None, alone=False):
                ts, bs = tile_slice(h), batch_slice(h)
                if step == "T_out":
                    dve.wait_ge(*due("T_y", n + 1, h))
                    dve.wait_ge(*due("P_x2c", n + 1, h))
                    dve.wait_ge(s["stored"], 16 * (n + 1))
                    v.tensor_tensor(o_T[:, ts, :].rearrange("p (b t) d -> p b t d", t=2),
                                    bank_t(h)[:, toks(h)].rearrange("p (b t d) -> p b t d", t=2, d=D),
                                    rows[q][:, bs, 2:3, :].broadcast_to([P, len(batches(h)), 2, D]), ALU.mult)\
                        .then_inc(sem("T_yG", h), 1)
                    dve.wait_ge(*due("T_yG", n + 2, h))
                    v.tensor_tensor(o_T[:, ts, :], o_T[:, ts, :], x2c[:, ts, :], ALU.add).then_inc(sem("T_out", h), 1)

            def guard(n, m):
                dve.wait_ge(s["fid_mm"], TILES * n + m + 1)
                dve.wait_ge(s["G_row"], TILES * (n - PAIRS) + m + 1)
                for u in range(2):
                    for k in range(2):
                        c = 32 + H * (2 * (m // 4) + k) + 2 * (m % 4) + u
                        v.tensor_scalar(shrink[:, S * k:S * k + S], cx_[:, S * u:S * u + S],
                                        norms[:, c:c + 1], 1.0 / EPS_COS, ALU.mult, ALU.mult).then_inc(s["G_shrink"], 1)
                    dve.wait_ge(s["G_shrink"], 4 * (TILES * (n - PAIRS) + m) + 2 * u + 2)
                    tile = score[m % 2][:, 512 * u:512 * u + 512]
                    last = v.scalar_tensor_tensor(tile, shrink[:, :], 1.0, tile, ALU.min, ALU.mult)
                    last.then_inc(s["G_scaled"], 1)
                    dve.wait_ge(s["G_scaled"], 2 * (TILES * (n - PAIRS) + m) + u + 1)
                v.tensor_copy(top[:, 0:1], norms[:, 0:1]).then_inc(s["G_done"], 1)

            def maxima(n, m):
                dve.wait_ge(s["G_dots"], TILES * (n - PAIRS) + m + 1)
                for u in range(2):
                    last = v.tensor_reduce(shrink[:, 2 * u:2 * u + 2],
                                           (cx_, cp_)[u][:, :].rearrange("p (k t) -> p k t", k=2),
                                           AX.X, ALU.max)
                last.then_inc(s["G_max"], 1)
                dve.wait_ge(s["G_max"], TILES * (n - PAIRS) + m + 1)
                v.tensor_scalar(top[:, :], shrink[:, 0:4], -1.0, None, ALU.mult).then_inc(s["G_neg"], 1)

            def body(n, q, prev, last, nxt, general=False):
                def steps(k):
                    for step in PLAN["dve"][k].split():
                        if step[0] == "P" and prev:
                            chain_p(step, n - 1, 1 - q)
                        elif step[0] == "T" and last:
                            chain_t(step, n - 2, q)
                        elif step[0] == "t" and prev:
                            chain_t("T" + step[1:], n - 1, 1 - q)
                        elif step[0] == "A" and nxt:
                            chain_a(step, n + 1, 1 - q)

                steps(0)
                if general:
                    v.tensor_tensor(norms[:, :], n2c[:, :], rn[:, :], ALU.mult).then_inc(s["G_norm"], 1)
                for k in range(2 * TILES):
                    m = k % TILES
                    if general and k < TILES:
                        guard(n, m)
                    if general and k >= TILES:
                        maxima(n, m)
                    if k < TILES:
                        dve.wait_ge(s["sin_done"], TILES * n + m + 1)
                        need(dve, s["av_done"], 4 * n)
                        v.scalar_tensor_tensor(prob[:, m, :], sines[:, m % 2, :], 10.0, score[m % 2][:, :],
                                               ALU.add, ALU.mult).then_inc(s["tile_read"], 1)
                    else:
                        dve.wait_ge(s["cw_mm"], TILES * n + m + 1)
                        v.scalar_tensor_tensor(prob[:, m, :], score[m % 2][:, :], 2.5, prob[:, m, :],
                                               ALU.mult, ALU.add).then_inc(s["tile_read"], 1)
                    steps(k + 1)
                    if first(n) and k in STAGE_AT:
                        stage(STAGE_AT[k])
                    if first(n) and k == FOLDED_AT:
                        folded()

            for step in A_STEPS:
                chain_a(step, 0, 0)
                if step == "A_norm":
                    scalars()
                if step == "A_n2":
                    rest_weights()
                    gates()
                    dve.wait_ge(s["pr_rows"], 1)
                    stage(0)
                    products_out()
                    stage(1)
                if step == "A_tq":
                    stage(2)
            body(FIRST, 0, False, False, True)
            body(1, 1, True, False, True)
            with dve.Fori(0, (PAIRS - 4) // 2) as i:
                body(2 * i + 2, 0, True, True, True)
                body(2 * i + 3, 1, True, True, True)
            body(PAIRS - 2, 0, True, True, True)
            body(PAIRS - 1, 1, True, True, False)
            for step in LAST["dve"].split():
                last_step(chain_p, chain_t, step)

            def general(n, q):
                for step in A_STEPS:
                    chain_a(step, n, q)
                body(n, q, False, False, False, True)
                for step in P_STEPS:
                    chain_p(step, n, q)
                for step in T_STEPS:
                    chain_t(step, n, q, alone=True)

            v.tensor_scalar(good[:, 0:64], n2_least[:, :], EPS_COS, None, ALU.is_ge)
            v.tensor_scalar(good[:, 64:80], l_least[:, :], SUM_LEAST, None, ALU.is_ge)
            v.tensor_scalar(good[:, 80:96], l_total[:, :], SUM_MOST, None, ALU.is_le).then_inc(s["flag_good"], 1)
            dve.wait_ge(s["flag_good"], 1)
            v.tensor_reduce(n_good[:, :], good[:, :], AX.X, ALU.add).then_inc(s["flag_sum"], 1)
            dve.wait_ge(s["flag_mm"], 1)
            v.tensor_scalar(flag[:, :], av[0:1, 0:1], 96.0 * P - 0.5, None, ALU.is_lt).then_inc(s["flag_ready"], 1)
            general_pass(dve, general)

        @block.gpsimd
        def _(pool):
            g = nc.gpsimd
            g.memset(ident[:, :], 0.0).then_inc(s["w_ident"], 1)
            g.memset(ident16[:, :], 0.0).then_inc(s["w_ident"], 1)
            g.memset(head_mask[:, :], 1.0).then_inc(s["w_ident"], 1)
            g.memset(neg_half[:, :], -0.5)
            pool.wait_ge(s["w_ident"], 3)
            for eye in (ident, ident16):
                g.affine_select(out=eye[:, :], in_=eye[:, :], compare_op=ALU.not_equal, fill=1.0,
                                base=0, pattern=[[-1, P]], channel_multiplier=1).then_inc(s["w_ident"], 1)
            g.affine_select(out=head_mask[:, :], in_=head_mask[:, :], compare_op=ALU.is_ge, fill=0.0,
                            base=0, pattern=[[-HD, H]], channel_multiplier=1).then_inc(s["w_ident"], 1)
            pool.wait_ge(s["w_ident"], 6)
            g.affine_select(out=head_mask[:, :], in_=head_mask[:, :], compare_op=ALU.is_ge, fill=0.0,
                            base=HD - 1, pattern=[[HD, H]], channel_multiplier=-1).then_inc(s["w_mask"], 1)
            g.memset(b2_rows, 0.0).then_inc(s["w_zero"], 1)

            def stage(j):
                pool.wait_ge(s[f"up_in{j % 3}"], 16 * (j // 3 + 1))
                products(g, wup[:, :], up_w[j % 3], prod_up, False, j, s["bf_up"])
                pool.wait_ge(s["bf_up"], 4 * j + 2)
                sums(g, wup[:, :], prod_up, j, s["bf_up"])
                pool.wait_ge(s["bf_up"], 4 * j + 4)

            def power(out_, in_, sem):
                g.tensor_tensor(out_, in_, neg_half[:, 0:in_.shape[1]], ALU.pow).then_inc(sem, 1)

            def chain_a(step, n, q):
                if step == "A_stats":
                    pool.wait_ge(s["A_var"], n + 1)
                    power(rstd["A"][:, :], var["A"][:, :], s["A_rstd"])
                elif step == "A_n2":
                    pool.wait_ge(s["A_qk3"], n + 1)
                    for side in (1, 0):
                        half = slice(32 * side, 32 * side + 32)
                        power(rn[:, half], n2c[:, half], s["A_rn"])
                        pool.wait_ge(s["A_rn"], 2 * n + 2 - side)
                        need(pool, s["A_lo"], 2 * n - side)
                        g.tensor_tensor(qn[:, side, :, :],
                                        qk[:, side, :, :].rearrange("p t (h q) -> p (t h) q", q=NQ),
                                        rn[:, half].unsqueeze(2).broadcast_to([P, 32, NQ]), ALU.mult)\
                            .then_inc(s["A_qn"], 1)

            def chain_p(step, n, q, h=None):
                ts, bs = tile_slice(h), batch_slice(h)
                if step == ("P_o0" if h == 0 else "P_o1"):
                    pool.wait_ge(s["xp_in"], 16 * (n + 1))
                    pool.wait_ge(s["rows_in"], 16 * (n + 1))
                    g.tensor_tensor(xB[:, ts, :].rearrange("p (b t) d -> p b t d", t=2),
                                    x_p[:, ts, :].rearrange("p (b t) d -> p b t d", t=2),
                                    rows[q][:, bs, 1:2, :].broadcast_to([P, len(batches(h)), 2, D]), ALU.add)\
                        .then_inc(sem("P_xB", h), 1)
                elif step == "P_u":
                    pool.wait_ge(*due("P_v1", n + 1, h))
                    power(rstd["1"][:, ts], var["1"][:, ts], sem("P_r1", h))
                elif step == "P_y":
                    pool.wait_ge(*due("P_v2", n + 1, h))
                    power(rstd["2"][:, ts], var["2"][:, ts], sem("P_r2d", h))
                elif step == "P_x2":
                    pool.wait_ge(*due("P_v3", n + 1, h))
                    power(rstd["3"][:, ts], var["3"][:, ts], sem("P_r3d", h))
                elif step == "P_z":
                    need(pool, s["T_out"], n)
                    g.tensor_tensor(x2c[:, ts, :].rearrange("p (b t) d -> p b t d", t=2),
                                    x2[:, ts, :].rearrange("p (b t) d -> p b t d", t=2),
                                    rows[q][:, bs, 3:4, :].broadcast_to([P, len(batches(h)), 2, D]), ALU.add)\
                        .then_inc(sem("P_x2c", h), 1)

            def chain_t(step, n, q, h=None, alone=False):
                pass

            def body(n, q, prev, last, nxt, general=False):
                def steps(k):
                    for step in PLAN["pool"][k].split():
                        if step[0] == "P" and prev:
                            chain_p(step, n - 1, 1 - q)
                        elif step[0] == "T" and last:
                            chain_t(step, n - 2, q)
                        elif step[0] == "t" and prev:
                            chain_t("T" + step[1:], n - 1, 1 - q)
                        elif step[0] == "A" and nxt:
                            chain_a(step, n + 1, 1 - q)

                steps(0)
                for k in range(2 * TILES):
                    steps(k + 1)
                    if first(n) and k in STAGE_AT:
                        stage(STAGE_AT[k])

            pool.wait_ge(s["w_zero"], 1)
            for step in A_STEPS:
                chain_a(step, 0, 0)
                if step == "A_stats":
                    g.memset(kfpad[0][:, :, :], 0.0).then_inc(s["zeroed0"], 1)
                    pool.wait_ge(s["w_rest"], 16 * REST_LOADS)
                    stage(0)
                if step == "A_n2":
                    g.memset(kfpad[1][:, :, :], 0.0).then_inc(s["zeroed1"], 1)
                if step == "A_tq":
                    for j in range(1, EARLY_STAGES):
                        stage(j)
            body(FIRST, 0, False, False, True)
            body(1, 1, True, False, True)
            with pool.Fori(0, (PAIRS - 4) // 2) as i:
                body(2 * i + 2, 0, True, True, True)
                body(2 * i + 3, 1, True, True, True)
            body(PAIRS - 2, 0, True, True, True)
            body(PAIRS - 1, 1, True, True, False)
            for step in LAST["pool"].split():
                last_step(chain_p, chain_t, step)

            def general(n, q):
                for step in A_STEPS:
                    chain_a(step, n, q)
                body(n, q, False, False, False, True)
                for step in P_STEPS:
                    chain_p(step, n, q)
                for step in T_STEPS:
                    chain_t(step, n, q, alone=True)

            general_pass(pool, general)


_INS = ["L0_attn_x", "L0_attn_Wq", "L0_attn_bq", "L0_attn_Wk", "L0_attn_bk", "L0_attn_Wv", "L0_attn_bv",
        "L0_attn_Wc2q", "L0_attn_bc2q", "L0_attn_Wo", "L0_attn_bo", "L0_attn_g1", "L0_attn_beta1", "L0_attn_g2",
        "L0_attn_beta2", "L0_attn_W1", "L0_attn_b1", "L0_attn_Wm", "L0_attn_bm", "L0_attn_Wqo", "L0_attn_bqo",
        "L0_attn_W2", "L0_attn_b2", "L0_ffn_W_exp", "L0_ffn_b_exp", "L0_ffn_up_weights", "L0_ffn_up_bias",
        "L0_ffn_down_weights", "L0_ffn_W_con", "L0_ffn_b_con", "L0_ffn_down_bias", "L0_c", "L0_wmod"]


def kernel(**inputs):
    import concourse.bacc as bacc
    import numpy as np
    from concourse.bass_utils import run_bass_kernel_spmd

    nc = bacc.Bacc("TRN2", target_bir_lowering=False, num_devices=1)
    arrays, args = {}, {}
    for name in _INS:
        arrays[f"in_{name}"] = np.ascontiguousarray(inputs[name])
        args[name] = nc.dram_tensor(f"in_{name}", arrays[f"in_{name}"].shape,
                                    mybir.dt.from_np(arrays[f"in_{name}"].dtype), kind="ExternalInput").ap()
    out = nc.dram_tensor("out", (B, S, D), F32, kind="ExternalOutput").ap()
    build(nc, args, out)
    r = run_bass_kernel_spmd(nc, [arrays], core_ids=[0])
    return r.results[0]["out"]
```
